# Optimizing a Trainium2 kernel written in Bass

```python
import numpy as np
import jax
import jax.numpy as jnp

def _softmax(x, axis=-1):
    return jax.nn.softmax(x, axis=axis)

def _gelu(x):
    return jax.nn.gelu(x, approximate=True)

def _silu(x):
    return jax.nn.silu(x)

def _sigmoid(x):
    return jax.nn.sigmoid(x)

def _layernorm(x, axis=-1, eps=1e-05):
    m = jnp.mean(x, axis=axis, keepdims=True)
    v = jnp.var(x, axis=axis, keepdims=True)
    return (x - m) / jnp.sqrt(v + eps)

def _scatter_add(tgt, idx, src, axis=0):
    return tgt.at[idx].add(src)

def _segment_sum(src, seg, n):
    return jax.ops.segment_sum(src, seg, n)
kernel_name = 'mk_gnn_preln_d4_gnn_r8_338b38'

def setup_inputs(seed: int=0):
    np.random.seed(seed)
    _w = jnp.asarray

    def _rec_inputs():
        import jax
        import jax.numpy as jnp
        _gk = jax.random.key(seed)
        x = -0.0009044 + 1 * jax.random.normal(jax.random.fold_in(_gk, 1), (12500, 32), jnp.float32)
        _s = jax.random.randint(jax.random.fold_in(_gk, 2), (100000,), 0, 12500, jnp.int32)
        _d = jax.random.randint(jax.random.fold_in(_gk, 3), (100000,), 0, 12500, jnp.int32)
        _loop = jnp.arange(12500, dtype=jnp.int32)
        src = jnp.concatenate([_s, _d, _loop])
        dst = jnp.concatenate([_d, _s, _loop])
        _o = jnp.argsort(dst, stable=True)
        src = src[_o]
        dst = dst[_o]
        edge_attr_3 = 0.000844983 + 0.999762 * jax.random.normal(jax.random.fold_in(_gk, 13), (212500, 3), jnp.float32)
        edge_attr_32 = 0.000196303 + 1.00016 * jax.random.normal(jax.random.fold_in(_gk, 14), (212500, 32), jnp.float32)
        edge_weight = jax.random.uniform(jax.random.fold_in(_gk, 16), (212500,), jnp.float32, 0.0, 1)
        return (x, src, dst, edge_attr_3, edge_attr_32, edge_weight)
    x, src, dst, edge_attr_3, edge_attr_32, edge_weight = _rec_inputs()

    def _L0_gnn_setup():
        import jax, jax.numpy as jnp
        import numpy as np
        N_NODES = 6250
        N_EDGES = 100000
        X_DIM = 32
        E_DIM = 32
        HID = 64
        OUT = 32
        key = jax.random.key(seed)
        ks = jax.random.split(key, 6)
        x = jax.random.normal(ks[0], (N_NODES, X_DIM), dtype=jnp.float32)
        edge_index = jax.random.randint(ks[1], (2, N_EDGES), 0, N_NODES, dtype=jnp.int64)
        edge_attr = jax.random.normal(ks[2], (N_EDGES, E_DIM), dtype=jnp.float32)
        in_dim = 2 * X_DIM + E_DIM
        W1 = jax.random.normal(ks[3], (in_dim, HID), dtype=jnp.float32) * (1.0 / np.sqrt(in_dim))
        b1 = jnp.zeros((HID,), dtype=jnp.float32)
        W2 = jax.random.normal(ks[4], (HID, OUT), dtype=jnp.float32) * (1.0 / np.sqrt(HID))
        b2 = jnp.zeros((OUT,), dtype=jnp.float32)
        return {'x': x, 'edge_index': edge_index, 'edge_attr': edge_attr, 'W1': W1, 'b1': b1, 'W2': W2, 'b2': b2}
    _L0_gnn_all = _L0_gnn_setup()
    _L0_gnn_in = {k: v for k, v in _L0_gnn_all.items() if k in ('W1', 'b1', 'W2', 'b2')}
    del _L0_gnn_all

    def _L1_gnn_setup():
        import jax, jax.numpy as jnp
        import numpy as np
        N_NODES = 12500
        key = jax.random.key(seed)
        k1, k2, k3, k4 = jax.random.split(key, 4)
        features = jax.random.normal(k1, (N_NODES, 32), dtype=jnp.float32)
        src = jax.random.randint(k2, (200000,), 0, N_NODES, dtype=jnp.int64)
        dst = jax.random.randint(k3, (200000,), 0, N_NODES, dtype=jnp.int64)
        weight = jax.random.normal(k4, (32, 32), dtype=jnp.float32) * (1.0 / np.sqrt(32.0))
        bias = jnp.zeros((32,), dtype=jnp.float32)
        return {'features': features, 'src': src, 'dst': dst, 'weight': weight, 'bias': bias}
    _L1_gnn_all = _L1_gnn_setup()
    _L1_gnn_in = {k: v for k, v in _L1_gnn_all.items() if k in ('weight', 'bias')}
    del _L1_gnn_all

    def _L2_gnn_setup():
        import jax, jax.numpy as jnp
        import numpy as np
        N = 12500
        E = 100000
        NF = 32
        EF = 32
        L = 64
        ENTRY = NF + EF
        SECOND = NF + L
        SLOPE = 0.1
        EPS = 1e-05

        def _bn(h, g, b):
            m = h.mean(0)
            v = ((h - m) ** 2).mean(0)
            return (h - m) * jax.lax.rsqrt(v + EPS) * g + b

        def _lrelu(h):
            return jnp.where(h > 0, h, SLOPE * h)
        key = jax.random.key(seed)
        ks = jax.random.split(key, 16)

        def w(k, i, o):
            return jax.random.normal(k, (i, o), jnp.float32) / np.float32(np.sqrt(i))

        def bvec(k, o):
            return jax.random.normal(k, (o,), jnp.float32) * 0.01
        inp = {'x': jax.random.normal(ks[0], (N, NF), jnp.float32), 'edge_index': jax.random.randint(ks[1], (2, E), 0, N), 'edge_attr': jax.random.normal(ks[2], (E, EF), jnp.float32), 'u': jax.random.normal(ks[3], (1, 4), jnp.float32), 'batch': jnp.zeros((N,), jnp.int32), 'm1_g1': jnp.ones((ENTRY,), jnp.float32), 'm1_b1': jnp.zeros((ENTRY,), jnp.float32), 'm1_w1': w(ks[4], ENTRY, L), 'm1_c1': bvec(ks[5], L), 'm1_g2': jnp.ones((L,), jnp.float32), 'm1_b2': jnp.zeros((L,), jnp.float32), 'm1_w2': w(ks[6], L, L), 'm1_c2': bvec(ks[7], L), 'm1_g3': jnp.ones((L,), jnp.float32), 'm1_b3': jnp.zeros((L,), jnp.float32), 'm1_w3': w(ks[8], L, L), 'm1_c3': bvec(ks[9], L), 'm2_g1': jnp.ones((SECOND,), jnp.float32), 'm2_b1': jnp.zeros((SECOND,), jnp.float32), 'm2_w1': w(ks[10], SECOND, SECOND), 'm2_c1': bvec(ks[11], SECOND), 'm2_g2': jnp.ones((SECOND,), jnp.float32), 'm2_b2': jnp.zeros((SECOND,), jnp.float32), 'm2_w2': w(ks[12], SECOND, SECOND), 'm2_c2': bvec(ks[13], SECOND), 'm2_g3': jnp.ones((SECOND,), jnp.float32), 'm2_b3': jnp.zeros((SECOND,), jnp.float32), 'm2_w3': w(ks[14], SECOND, NF), 'm2_c3': bvec(ks[15], NF)}
        return inp
    _L2_gnn_all = _L2_gnn_setup()
    _L2_gnn_in = {k: v for k, v in _L2_gnn_all.items() if k in ('u', 'm1_g1', 'm1_b1', 'm1_w1', 'm1_c1', 'm1_g2', 'm1_b2', 'm1_w2', 'm1_c2', 'm1_g3', 'm1_b3', 'm1_w3', 'm1_c3', 'm2_g1', 'm2_b1', 'm2_w1', 'm2_c1', 'm2_g2', 'm2_b2', 'm2_w2', 'm2_c2', 'm2_g3', 'm2_b3', 'm2_w3', 'm2_c3')}
    del _L2_gnn_all

    def _L3_gnn_setup():
        import jax, jax.numpy as jnp
        import numpy as np
        from math import factorial, pi, sqrt
        MUL = 8
        RS = [(MUL, 0), (MUL, 1)]
        N_NODES = 2500
        N_EDGES = 80000
        FEAT_DIM = sum((m * (2 * l + 1) for m, l in RS))
        R_DIM = sum((mo * mi * (2 * min(lo, li) + 1) for mo, lo in RS for mi, li in RS))
        HIDDEN = 64

        def _cg(j1, j2, j3, m1, m2, m3):
            if m1 + m2 != m3:
                return 0.0
            f = factorial
            pre = sqrt((2 * j3 + 1) * f(j3 + j1 - j2) * f(j3 - j1 + j2) * f(j1 + j2 - j3) / f(j1 + j2 + j3 + 1))
            pre *= sqrt(f(j3 + m3) * f(j3 - m3) * f(j1 - m1) * f(j1 + m1) * f(j2 - m2) * f(j2 + m2))
            kmin = max(0, j2 - j3 - m1, j1 - j3 + m2)
            kmax = min(j1 + j2 - j3, j1 - m1, j2 + m2)
            s = 0.0
            for k in range(kmin, kmax + 1):
                s += (-1) ** k / (f(k) * f(j1 + j2 - j3 - k) * f(j1 - m1 - k) * f(j2 + m2 - k) * f(j3 - j2 + m1 + k) * f(j3 - j1 - m2 + k))
            return pre * s

        def _w3j_complex(l1, l2, l3):
            w = np.zeros((2 * l1 + 1, 2 * l2 + 1, 2 * l3 + 1))
            for m1 in range(-l1, l1 + 1):
                for m2 in range(-l2, l2 + 1):
                    m3 = -(m1 + m2)
                    if abs(m3) <= l3:
                        w[m1 + l1, m2 + l2, m3 + l3] = (-1) ** (l1 - l2 - m3) / sqrt(2 * l3 + 1) * _cg(l1, l2, l3, m1, m2, -m3)
            return w

        def _A(l):
            A = np.zeros((2 * l + 1, 2 * l + 1), dtype=complex)
            A[l, l] = 1.0
            for m in range(1, l + 1):
                A[l + m, l + m] = (-1) ** m / sqrt(2)
                A[l + m, l - m] = 1.0 / sqrt(2)
                A[l - m, l - m] = 1j / sqrt(2)
                A[l - m, l + m] = -1j * (-1) ** m / sqrt(2)
            return A

        def real_w3j(l1, l2, l3):
            wc = _w3j_complex(l1, l2, l3).astype(complex)
            wr = np.einsum('abc,ma,nb,oc->mno', wc, _A(l1).conj(), _A(l2).conj(), _A(l3).conj())
            i = int(np.argmax(np.abs(wr)))
            ph = wr.flat[i] / abs(wr.flat[i])
            wr = wr / ph
            assert np.abs(wr.imag).max() < 1e-10
            return np.real(wr).astype(np.float32)
        _W3J = {}
        for _mo, _lo in RS:
            for _mi, _li in RS:
                for _lf in range(abs(_lo - _li), _lo + _li + 1):
                    if (_lo, _lf, _li) not in _W3J:
                        _W3J[_lo, _lf, _li] = jnp.asarray(real_w3j(_lo, _lf, _li))
        _NORM = []
        for _mo, _lo in RS:
            _num = sum((mi * (2 * min(_lo, li) + 1) for mi, li in RS))
            _NORM.append(sqrt(4.0 * pi) * sqrt(2.0 * _lo + 1.0) / sqrt(_num))
        _F_OFFS = [0] + list(np.cumsum([mi * (2 * li + 1) for mi, li in RS]))

        def spherical_harmonics(rel_vec):
            r = rel_vec / jnp.linalg.norm(rel_vec, axis=-1, keepdims=True)
            x, y, z = (r[:, 0], r[:, 1], r[:, 2])
            y0 = jnp.full_like(x, 0.5 / sqrt(pi))[:, None]
            c1 = sqrt(3.0 / (4.0 * pi))
            y1 = c1 * jnp.stack([y, z, x], axis=-1)
            c2a = 0.5 * sqrt(15.0 / pi)
            c2b = 0.25 * sqrt(5.0 / pi)
            c2c = 0.25 * sqrt(15.0 / pi)
            y2 = jnp.stack([c2a * x * y, c2a * y * z, c2b * (3.0 * z * z - 1.0), c2a * x * z, c2c * (x * x - y * y)], axis=-1)
            return jnp.concatenate([y0, y1, y2], axis=-1)
        key = jax.random.key(seed)
        ks = jax.random.split(key, 6)
        features = jax.random.normal(ks[0], (N_NODES, FEAT_DIM), dtype=jnp.float32)
        abs_distances = jax.random.uniform(ks[1], (N_EDGES,), dtype=jnp.float32, minval=0.1, maxval=1.0)
        rel_vec = jax.random.normal(ks[2], (N_EDGES, 3), dtype=jnp.float32)
        edge_index = jax.random.randint(ks[3], (2, N_EDGES), 0, N_NODES, dtype=jnp.int32)
        w1 = jax.random.normal(ks[4], (1, HIDDEN), dtype=jnp.float32)
        b1 = jnp.zeros((HIDDEN,), jnp.float32)
        w2 = jax.random.normal(ks[5], (HIDDEN, R_DIM), dtype=jnp.float32) / sqrt(HIDDEN)
        b2 = jnp.zeros((R_DIM,), jnp.float32)
        return {'features': features, 'abs_distances': abs_distances, 'rel_vec': rel_vec, 'edge_index': edge_index, 'w1': w1, 'b1': b1, 'w2': w2, 'b2': b2}
    _L3_gnn_all = _L3_gnn_setup()
    _L3_gnn_in = {k: v for k, v in _L3_gnn_all.items() if k in ('w1', 'b1', 'w2', 'b2')}
    del _L3_gnn_all
    return {'x': x, 'src': src, 'dst': dst, 'edge_attr_3': edge_attr_3, 'edge_attr_32': edge_attr_32, 'edge_weight': edge_weight, 'L0_gnn_W1': _L0_gnn_in['W1'], 'L0_gnn_b1': _L0_gnn_in['b1'], 'L0_gnn_W2': _L0_gnn_in['W2'], 'L0_gnn_b2': _L0_gnn_in['b2'], 'L1_gnn_weight': _L1_gnn_in['weight'], 'L1_gnn_bias': _L1_gnn_in['bias'], 'L2_gnn_u': _L2_gnn_in['u'], 'L2_gnn_m1_g1': _L2_gnn_in['m1_g1'], 'L2_gnn_m1_b1': _L2_gnn_in['m1_b1'], 'L2_gnn_m1_w1': _L2_gnn_in['m1_w1'], 'L2_gnn_m1_c1': _L2_gnn_in['m1_c1'], 'L2_gnn_m1_g2': _L2_gnn_in['m1_g2'], 'L2_gnn_m1_b2': _L2_gnn_in['m1_b2'], 'L2_gnn_m1_w2': _L2_gnn_in['m1_w2'], 'L2_gnn_m1_c2': _L2_gnn_in['m1_c2'], 'L2_gnn_m1_g3': _L2_gnn_in['m1_g3'], 'L2_gnn_m1_b3': _L2_gnn_in['m1_b3'], 'L2_gnn_m1_w3': _L2_gnn_in['m1_w3'], 'L2_gnn_m1_c3': _L2_gnn_in['m1_c3'], 'L2_gnn_m2_g1': _L2_gnn_in['m2_g1'], 'L2_gnn_m2_b1': _L2_gnn_in['m2_b1'], 'L2_gnn_m2_w1': _L2_gnn_in['m2_w1'], 'L2_gnn_m2_c1': _L2_gnn_in['m2_c1'], 'L2_gnn_m2_g2': _L2_gnn_in['m2_g2'], 'L2_gnn_m2_b2': _L2_gnn_in['m2_b2'], 'L2_gnn_m2_w2': _L2_gnn_in['m2_w2'], 'L2_gnn_m2_c2': _L2_gnn_in['m2_c2'], 'L2_gnn_m2_g3': _L2_gnn_in['m2_g3'], 'L2_gnn_m2_b3': _L2_gnn_in['m2_b3'], 'L2_gnn_m2_w3': _L2_gnn_in['m2_w3'], 'L2_gnn_m2_c3': _L2_gnn_in['m2_c3'], 'L3_gnn_w1': _L3_gnn_in['w1'], 'L3_gnn_b1': _L3_gnn_in['b1'], 'L3_gnn_w2': _L3_gnn_in['w2'], 'L3_gnn_b2': _L3_gnn_in['b2']}

def reference(x, src, dst, edge_attr_3, edge_attr_32, edge_weight, L0_gnn_W1, L0_gnn_b1, L0_gnn_W2, L0_gnn_b2, L1_gnn_weight, L1_gnn_bias, L2_gnn_u, L2_gnn_m1_g1, L2_gnn_m1_b1, L2_gnn_m1_w1, L2_gnn_m1_c1, L2_gnn_m1_g2, L2_gnn_m1_b2, L2_gnn_m1_w2, L2_gnn_m1_c2, L2_gnn_m1_g3, L2_gnn_m1_b3, L2_gnn_m1_w3, L2_gnn_m1_c3, L2_gnn_m2_g1, L2_gnn_m2_b1, L2_gnn_m2_w1, L2_gnn_m2_c1, L2_gnn_m2_g2, L2_gnn_m2_b2, L2_gnn_m2_w2, L2_gnn_m2_c2, L2_gnn_m2_g3, L2_gnn_m2_b3, L2_gnn_m2_w3, L2_gnn_m2_c3, L3_gnn_w1, L3_gnn_b1, L3_gnn_w2, L3_gnn_b2):
    import jax
    import jax.numpy as jnp

    def _L0_gnn_ref(x, edge_index, edge_attr, W1, b1, W2, b2):
        import jax, jax.numpy as jnp
        import numpy as np
        N_NODES = 6250
        N_EDGES = 100000
        X_DIM = 32
        E_DIM = 32
        HID = 64
        OUT = 32
        num_nodes = x.shape[0]
        rol, col = (edge_index[0], edge_index[1])
        e_feat = jnp.concatenate([x[rol], x[col], edge_attr], axis=-1)
        h = jax.nn.relu(e_feat @ W1 + b1)
        v = h @ W2 + b2
        x_cand = jax.ops.segment_max(v, col, num_segments=num_nodes)
        return jnp.maximum(x_cand, x[:, -v.shape[-1]:])

    def _L1_gnn_ref(features, src, dst, weight, bias):
        import jax, jax.numpy as jnp
        import numpy as np
        N_NODES = 12500
        n = features.shape[0]
        ones = jnp.ones(src.shape[0], dtype=features.dtype)
        deg_out = jax.ops.segment_sum(ones, src, num_segments=n)
        deg_in = jax.ops.segment_sum(ones, dst, num_segments=n)
        norm_src = jax.lax.rsqrt(jnp.maximum(deg_out, 1.0))
        norm_dst = jax.lax.rsqrt(jnp.maximum(deg_in, 1.0))
        h = features * norm_src[:, None]
        msgs = h[src]
        agg = jax.ops.segment_sum(msgs, dst, num_segments=n)
        agg = agg * norm_dst[:, None]
        out = agg @ weight + bias
        return jax.nn.relu(out)

    def _L2_gnn_ref(x, edge_index, edge_attr, u, batch, m1_g1, m1_b1, m1_w1, m1_c1, m1_g2, m1_b2, m1_w2, m1_c2, m1_g3, m1_b3, m1_w3, m1_c3, m2_g1, m2_b1, m2_w1, m2_c1, m2_g2, m2_b2, m2_w2, m2_c2, m2_g3, m2_b3, m2_w3, m2_c3):
        import jax, jax.numpy as jnp
        import numpy as np
        N = 12500
        E = 100000
        NF = 32
        EF = 32
        L = 64
        ENTRY = NF + EF
        SECOND = NF + L
        SLOPE = 0.1
        EPS = 1e-05

        def _bn(h, g, b):
            m = h.mean(0)
            v = ((h - m) ** 2).mean(0)
            return (h - m) * jax.lax.rsqrt(v + EPS) * g + b

        def _lrelu(h):
            return jnp.where(h > 0, h, SLOPE * h)
        row, col = (edge_index[0], edge_index[1])
        h = jnp.concatenate([x[row], edge_attr], axis=1)
        h = _lrelu(_bn(h, m1_g1, m1_b1) @ m1_w1 + m1_c1)
        h = _lrelu(_bn(h, m1_g2, m1_b2) @ m1_w2 + m1_c2)
        h = _bn(h, m1_g3, m1_b3) @ m1_w3 + m1_c3
        agg = jax.ops.segment_sum(h, col, num_segments=x.shape[0])
        h2 = jnp.concatenate([x, agg], axis=1)
        h2 = _lrelu(_bn(h2, m2_g1, m2_b1) @ m2_w1 + m2_c1)
        h2 = _lrelu(_bn(h2, m2_g2, m2_b2) @ m2_w2 + m2_c2)
        out = _bn(h2, m2_g3, m2_b3) @ m2_w3 + m2_c3
        return out

    def _L3_gnn_ref(features, abs_distances, rel_vec, edge_index, w1, b1, w2, b2):
        import jax, jax.numpy as jnp
        import numpy as np
        from math import factorial, pi, sqrt
        MUL = 8
        RS = [(MUL, 0), (MUL, 1)]
        N_NODES = 2500
        N_EDGES = 80000
        FEAT_DIM = sum((m * (2 * l + 1) for m, l in RS))
        R_DIM = sum((mo * mi * (2 * min(lo, li) + 1) for mo, lo in RS for mi, li in RS))
        HIDDEN = 64

        def _cg(j1, j2, j3, m1, m2, m3):
            if m1 + m2 != m3:
                return 0.0
            f = factorial
            pre = sqrt((2 * j3 + 1) * f(j3 + j1 - j2) * f(j3 - j1 + j2) * f(j1 + j2 - j3) / f(j1 + j2 + j3 + 1))
            pre *= sqrt(f(j3 + m3) * f(j3 - m3) * f(j1 - m1) * f(j1 + m1) * f(j2 - m2) * f(j2 + m2))
            kmin = max(0, j2 - j3 - m1, j1 - j3 + m2)
            kmax = min(j1 + j2 - j3, j1 - m1, j2 + m2)
            s = 0.0
            for k in range(kmin, kmax + 1):
                s += (-1) ** k / (f(k) * f(j1 + j2 - j3 - k) * f(j1 - m1 - k) * f(j2 + m2 - k) * f(j3 - j2 + m1 + k) * f(j3 - j1 - m2 + k))
            return pre * s

        def _w3j_complex(l1, l2, l3):
            w = np.zeros((2 * l1 + 1, 2 * l2 + 1, 2 * l3 + 1))
            for m1 in range(-l1, l1 + 1):
                for m2 in range(-l2, l2 + 1):
                    m3 = -(m1 + m2)
                    if abs(m3) <= l3:
                        w[m1 + l1, m2 + l2, m3 + l3] = (-1) ** (l1 - l2 - m3) / sqrt(2 * l3 + 1) * _cg(l1, l2, l3, m1, m2, -m3)
            return w

        def _A(l):
            A = np.zeros((2 * l + 1, 2 * l + 1), dtype=complex)
            A[l, l] = 1.0
            for m in range(1, l + 1):
                A[l + m, l + m] = (-1) ** m / sqrt(2)
                A[l + m, l - m] = 1.0 / sqrt(2)
                A[l - m, l - m] = 1j / sqrt(2)
                A[l - m, l + m] = -1j * (-1) ** m / sqrt(2)
            return A

        def real_w3j(l1, l2, l3):
            wc = _w3j_complex(l1, l2, l3).astype(complex)
            wr = np.einsum('abc,ma,nb,oc->mno', wc, _A(l1).conj(), _A(l2).conj(), _A(l3).conj())
            i = int(np.argmax(np.abs(wr)))
            ph = wr.flat[i] / abs(wr.flat[i])
            wr = wr / ph
            assert np.abs(wr.imag).max() < 1e-10
            return np.real(wr).astype(np.float32)
        _W3J = {}
        for _mo, _lo in RS:
            for _mi, _li in RS:
                for _lf in range(abs(_lo - _li), _lo + _li + 1):
                    if (_lo, _lf, _li) not in _W3J:
                        _W3J[_lo, _lf, _li] = jnp.asarray(real_w3j(_lo, _lf, _li))
        _NORM = []
        for _mo, _lo in RS:
            _num = sum((mi * (2 * min(_lo, li) + 1) for mi, li in RS))
            _NORM.append(sqrt(4.0 * pi) * sqrt(2.0 * _lo + 1.0) / sqrt(_num))
        _F_OFFS = [0] + list(np.cumsum([mi * (2 * li + 1) for mi, li in RS]))

        def spherical_harmonics(rel_vec):
            r = rel_vec / jnp.linalg.norm(rel_vec, axis=-1, keepdims=True)
            x, y, z = (r[:, 0], r[:, 1], r[:, 2])
            y0 = jnp.full_like(x, 0.5 / sqrt(pi))[:, None]
            c1 = sqrt(3.0 / (4.0 * pi))
            y1 = c1 * jnp.stack([y, z, x], axis=-1)
            c2a = 0.5 * sqrt(15.0 / pi)
            c2b = 0.25 * sqrt(5.0 / pi)
            c2c = 0.25 * sqrt(15.0 / pi)
            y2 = jnp.stack([c2a * x * y, c2a * y * z, c2b * (3.0 * z * z - 1.0), c2a * x * z, c2c * (x * x - y * y)], axis=-1)
            return jnp.concatenate([y0, y1, y2], axis=-1)
        src, dst = (edge_index[0], edge_index[1])
        R = jax.nn.relu(abs_distances[:, None] @ w1 + b1) @ w2 + b2
        Y = spherical_harmonics(rel_vec)
        Fj = features[src]
        E = Fj.shape[0]
        msg_blocks = []
        r_off = 0
        for i, (mo, lo) in enumerate(RS):
            acc = jnp.zeros((E, mo, 2 * lo + 1), dtype=features.dtype)
            for j, (mi, li) in enumerate(RS):
                n_lf = 2 * min(lo, li) + 1
                sz = mo * mi * n_lf
                Rb = R[:, r_off:r_off + sz].reshape(E, mo, mi, n_lf)
                r_off += sz
                Fb = Fj[:, _F_OFFS[j]:_F_OFFS[j + 1]].reshape(E, mi, 2 * li + 1)
                for k, lf in enumerate(range(abs(lo - li), lo + li + 1)):
                    C = _W3J[lo, lf, li]
                    Yf = Y[:, lf * lf:(lf + 1) * (lf + 1)]
                    acc = acc + _NORM[i] * jnp.einsum('euv,ef,evi,ofi->euo', Rb[..., k], Yf, Fb, C)
            msg_blocks.append(acc.reshape(E, -1))
        msg = jnp.concatenate(msg_blocks, axis=-1)
        out = jnp.zeros((features.shape[0], msg.shape[1]), dtype=features.dtype)
        out = out.at[dst].add(msg)
        return out
    edge_index = jnp.stack([src, dst])
    batch0 = jnp.zeros((12500,), jnp.int32)
    h = jnp.maximum(_layernorm(x, axis=-1), 0.0)
    x = x + _L0_gnn_ref(h, edge_index, edge_attr_32, L0_gnn_W1, L0_gnn_b1, L0_gnn_W2, L0_gnn_b2)
    h = jnp.maximum(_layernorm(x, axis=-1), 0.0)
    x = x + _L1_gnn_ref(h, src, dst, L1_gnn_weight, L1_gnn_bias)
    h = jnp.maximum(_layernorm(x, axis=-1), 0.0)
    x = x + _L2_gnn_ref(h, edge_index, edge_attr_32, L2_gnn_u, batch0, L2_gnn_m1_g1, L2_gnn_m1_b1, L2_gnn_m1_w1, L2_gnn_m1_c1, L2_gnn_m1_g2, L2_gnn_m1_b2, L2_gnn_m1_w2, L2_gnn_m1_c2, L2_gnn_m1_g3, L2_gnn_m1_b3, L2_gnn_m1_w3, L2_gnn_m1_c3, L2_gnn_m2_g1, L2_gnn_m2_b1, L2_gnn_m2_w1, L2_gnn_m2_c1, L2_gnn_m2_g2, L2_gnn_m2_b2, L2_gnn_m2_w2, L2_gnn_m2_c2, L2_gnn_m2_g3, L2_gnn_m2_b3, L2_gnn_m2_w3, L2_gnn_m2_c3)
    h = jnp.maximum(_layernorm(x, axis=-1), 0.0)
    x = x + _L3_gnn_ref(h, edge_weight, edge_attr_3, edge_index, L3_gnn_w1, L3_gnn_b1, L3_gnn_w2, L3_gnn_b2)
    return x

_drawn_inputs = setup_inputs


def setup_inputs(seed=0):
    import zlib

    import numpy as np

    out = dict(_drawn_inputs(seed))
    spreads = {'L0_gnn_b1': (0.0, 0.1),
     'L0_gnn_b2': (0.0, 0.1),
     'L1_gnn_bias': (0.0, 0.1),
     'L2_gnn_m1_g1': (1.0, 0.2),
     'L2_gnn_m1_b1': (0.0, 0.312),
     'L2_gnn_m1_g2': (1.0, 0.2),
     'L2_gnn_m1_b2': (0.0, 0.34),
     'L2_gnn_m1_g3': (1.0, 0.2),
     'L2_gnn_m1_b3': (0.0, 0.1),
     'L2_gnn_m2_g1': (1.0, 0.2),
     'L2_gnn_m2_b1': (0.0, 0.282),
     'L2_gnn_m2_g2': (1.0, 0.2),
     'L2_gnn_m2_b2': (0.0, 0.318),
     'L2_gnn_m2_g3': (1.0, 0.2),
     'L2_gnn_m2_b3': (0.0, 0.1),
     'L3_gnn_b1': (0.0, 0.1),
     'L3_gnn_b2': (0.0, 0.1)}
    factors = {'L2_gnn_m1_c1': 8.0,
     'L2_gnn_m1_c2': 8.0,
     'L2_gnn_m1_c3': 8.0,
     'L2_gnn_m2_c1': 25.417,
     'L2_gnn_m2_c2': 24.319,
     'L2_gnn_m2_c3': 8.0}
    for name, (base, spread) in spreads.items():
        noise = np.random.default_rng([zlib.crc32(name.encode()), seed]).standard_normal(out[name].shape)
        drawn = base * np.exp(spread * noise) if base else spread * noise
        out[name] = jnp.asarray(drawn.astype(out[name].dtype))
    for name, factor in factors.items():
        out[name] = (out[name] * factor).astype(out[name].dtype)
    return out
```

```python
from contextlib import ExitStack

import numpy as np

import concourse.bass as bass
from concourse import mybir

F32 = mybir.dt.float32
BF16 = mybir.dt.bfloat16
I32 = mybir.dt.int32
ALU = mybir.AluOpType
ACT = mybir.ActivationFunctionType
AX_X = mybir.AxisListType.X

P = 128
N = 12500
E = 212500
D = 32
NB = -(-N // P)
NP = NB * P
TAIL = N - (NB - 1) * P
PAD_SRC = NP - 1
TJ = 4
U = TJ * P
BU = 4
BODY = BU * U
BODIES = -(-E // BODY)
EP = BODIES * BODY
NT = EP // P
UNITS = NT // TJ
LAST = E - (UNITS - 1) * U
ACC = 12672
CH = 500
NCH = N // CH
EPS = 1e-5
GRP = 14
QC, QK, QN = 425, 5, 25
assert 4 * QC * QK * QN == E and NB % GRP == 0 and 0 < LAST < P


def flow(eng, body, last=None, tail=None):
    for u in range(BU):
        body(0, u)
    end = BODIES - 1 if last else BODIES
    with eng.Fori(1, end) as i:
        for u in range(BU):
            body(i, u)
    if last:
        for u in range(BU):
            last(BODIES - 1, u)
    if tail:
        for u in range(BU):
            tail(BODIES, u)


def before(i, u, lag):
    u -= lag
    if u < 0:
        if isinstance(i, int) and i == 0:
            return None
        i, u = i - 1, u + BU
    return i, u


def wait_units(eng, sem, i, u, back=0, per=1):
    w = before(i, u, back)
    if w is not None:
        eng.wait_ge(sem, (w[0] * BU + w[1] + 1) * per)


def wait_slot(eng, sems, i, u, per=16):
    eng.wait_ge(sems[u % 2], (i * (BU // 2) + u // 2 + 1) * per)


def build(nc, A, out):
    with ExitStack() as ctx:
        n_sem = [0]
        in_use = []

        def sb(name, shape, dt=F32):
            return ctx.enter_context(nc.sbuf_tensor(name, shape, dt))

        def local(own, name, shape, dt=F32):
            n_sem[0] += 1
            return own.enter_context(nc.sbuf_tensor(f"{name}_{n_sem[0]}", shape, dt))

        def sem(name):
            n_sem[0] += 1
            handle = nc.alloc_semaphore(name=f"{name}_{n_sem[0]}")
            in_use.append(handle)
            return handle

        def recycle():
            nc.clear_and_free_semaphores(in_use)
            in_use.clear()
            nc.all_engine_barrier()

        def sems(name, n=2):
            return [sem(f"{name}{k}") for k in range(n)]

        def dram(name, shape, dt=F32):
            return nc.dram_tensor(name, shape, dt, kind="Internal").ap()

        h_table = dram("h_table", [NP, D])
        h1_table = dram("h1_table", [NP, D + 1])
        b_table = dram("b_table", [NP + P, 64])
        z1_dram = dram("z1_dram", [64, EP])

        ident = sb("ident", [P, P])
        iota = sb("iota", [P, P])
        iota_b = sb("iota_b", [P, P], BF16)
        x_nm = sb("x_nm", [P, NB, D])
        h_nm = sb("h_nm", [P, NB, D])
        dst_rel = sb("dst_rel", [P, NT])
        dst_last = sb("dst_last", [P, NT])
        first = sb("first", [1, NT], I32)
        deg_out = sb("deg_out", [P, NB])
        acc = sb("acc", [P, ACC])
        big = sb("big", [P, NP])
        ps = [ctx.enter_context(nc.psum_tensor(f"bank{k}", [P, 512], F32)) for k in range(8)]

        wz = sb("wz", [64, 64])
        wb = sb("wb", [D, 64])
        cols = sb("cols", [P, 32])
        w2x = sb("w2x", [65, D])
        w_l1 = sb("w_l1", [D + 1, D + 1])
        bias_l1 = sb("bias_l1", [P, D])
        m1w = [sb(f"m1w{k}", [65, 64]) for k in range(3)]
        c_rows = sb("c_rows", [1, 2, 64])
        m2w = [sb(f"m2w{k}", [96, 96]) for k in range(3)]
        w2r = sb("w2r", [65, 384])
        w2m = sb("w2m", [65, 384])

        class Chain:

            def __init__(self, eng, sem):
                self.eng, self.sem, self.n = eng, sem, 0

            def __call__(self, ins):
                self.n += 1
                ins.then_inc(self.sem, 1)
                self.eng.wait_ge(self.sem, self.n)

        with ExitStack() as own, nc.Block() as block:
            dst_i = local(own, "dst_i", [P, NT], I32)
            next_i = local(own, "next_i", [P, NT], I32)
            first_i = local(own, "first_i", [P, NT], I32)
            nxt = big[:, 0:NT]
            fst = big[:, NT:2 * NT]
            cleared = sem("cleared")
            loaded = sem("loaded")
            made = sem("made")
            masks = sem("masks")
            dve_step = sem("dve_step")
            n_loads = [0]

            @block.sync
            def _(sp):
                sp.wait_ge(cleared, 1)

                def load(dst, src):
                    n_loads[0] += 1
                    sp.dma_start(dst, src).then_inc(loaded, 16)
                load(dst_i[:], A["dst_t"])
                load(next_i[:], A["next_t"])
                load(first_i[:], A["first"].partition_broadcast(P))
                load(first[:], A["first"][None, :])
                load(x_nm[:, 0:NB - 2, :], A["x"][0:(NB - 2) * P, :].rearrange("(c p) f -> p c f", p=P))
                load(x_nm[:, NB - 2, :], A["x"][(NB - 2) * P:(NB - 1) * P, :])
                load(x_nm[0:TAIL, NB - 1, :], A["x"][(NB - 1) * P:N, :])
                load(wz[0:D, :], A["L0_gnn_W1"][0:D, :])
                load(wz[D:2 * D, :], A["L0_gnn_W1"][2 * D:3 * D, :])
                load(wb[:], A["L0_gnn_W1"][D:2 * D, :])
                load(w2x[0:64, :], A["L0_gnn_W2"])
                load(w2x[64:65, :], A["L0_gnn_b2"][None, :])
                load(w_l1[0:D, 0:D], A["L1_gnn_weight"])
                load(bias_l1[:], A["L1_gnn_bias"].partition_broadcast(P))
                for k in range(3):
                    load(m1w[k][0:64, :], A[f"L2_gnn_m1_w{k + 1}"])
                load(c_rows[:, 0, :], A["L2_gnn_m1_c2"][None, :])
                load(c_rows[:, 1, :], A["L2_gnn_m1_c3"][None, :])
                load(m2w[0][0:64, :], A["L2_gnn_m2_w1"][D:96, :])
                load(m2w[0][64:96, :], A["L2_gnn_m2_w1"][0:D, :])
                load(m2w[1][:], A["L2_gnn_m2_w2"])
                load(m2w[2][:, 0:D], A["L2_gnn_m2_w3"])
                load(w2r[0:64, :], A["L3_gnn_w2"])
                load(w2r[64:65, :], A["L3_gnn_b2"][None, :])

                def column(n, rows, name, lo=0, hi=None):
                    v = A[name]
                    hi = v.shape[-1] if hi is None else hi
                    v = v[0, :] if len(v.shape) == 2 else v
                    load(cols[rows:rows + hi - lo, n:n + 1], v[lo:hi].rearrange("(a b) -> a b", b=1))
                column(0, 0, "L0_gnn_b1")
                column(1, 0, "L3_gnn_w1")
                column(2, 0, "L3_gnn_b1")
                for k in range(3):
                    column(3 + 2 * k, 0, f"L2_gnn_m1_g{k + 1}")
                    column(4 + 2 * k, 0, f"L2_gnn_m1_b{k + 1}")
                column(9, 0, "L2_gnn_m1_c1")
                column(10, 0, "L2_gnn_m2_g1", D, 96)
                column(10, 64, "L2_gnn_m2_g1", 0, D)
                column(11, 0, "L2_gnn_m2_b1", D, 96)
                column(11, 64, "L2_gnn_m2_b1", 0, D)
                for k in (1, 2):
                    column(10 + 2 * k, 0, f"L2_gnn_m2_g{k + 1}")
                    column(11 + 2 * k, 0, f"L2_gnn_m2_b{k + 1}")
                for k in range(3):
                    column(16 + k, 0, f"L2_gnn_m2_c{k + 1}")
                sp.wait_ge(loaded, 16 * n_loads[0])

            @block.gpsimd
            def _(pool):
                pool.iota(iota[:], [[1, P]], base=0, channel_multiplier=0,
                          allow_small_or_imprecise_dtypes=True).then_inc(made, 1)
                pool.memset(ident[:], 0.0).then_inc(masks, 1)
                pool.wait_ge(masks, 1)
                pool.affine_select(out=ident[:], in_=ident[:], compare_op=ALU.not_equal, fill=1.0, base=0,
                                   pattern=[[-1, P]], channel_multiplier=1).then_inc(made, 1)

            @block.vector
            def _(v):
                step = Chain(v, dve_step)
                for t in (cols, x_nm, w_l1, m2w[2]):
                    step(v.memset(t[:], 0.0))
                v.memset(w_l1[D:D + 1, D:D + 1], 1.0).then_inc(cleared, 1)
                v.wait_ge(loaded, 16 * n_loads[0])
                v.wait_ge(made, 2)
                step(v.tensor_copy(iota_b[:], iota[:]))
                step(v.tensor_copy(dst_rel[:], dst_i[:]))
                step(v.tensor_copy(nxt, next_i[:]))
                step(v.tensor_copy(fst, first_i[:]))
                step(v.tensor_tensor(nxt, nxt, dst_rel[:], ALU.not_equal))
                step(v.tensor_tensor(dst_rel[:], dst_rel[:], fst, ALU.subtract))
                step(v.scalar_tensor_tensor(out=dst_last[:], in0=dst_rel[:], scalar=1.0, in1=nxt,
                                            op0=ALU.add, op1=ALU.mult))
                step(v.tensor_scalar(dst_last[:], dst_last[:], -1.0, None, ALU.add))
                w4 = [w2r[:, 64 * k:64 * (k + 1)].rearrange("p (u v) -> p u v", v=8) for k in range(3)]
                w5 = w2r[:, 192:384].rearrange("p (u v k) -> p u v k", v=8, k=3)
                o = w2m[:].rearrange("p (b u v) -> p b u v", b=3, v=16)
                q = float(np.sqrt(3.0 / 32.0))
                for dst, src, s in ((o[:, 0, :, 0:8], w4[0], 0.25), (o[:, 0, :, 8:16], w4[1], 0.25),
                                    (o[:, 1, :, 0:8], w4[2], q),
                                    (o[:, 1, :, 8:16], w5[:, :, :, 2], 0.375),
                                    (o[:, 2, :, 0:8], w5[:, :, :, 0], float(1.0 / np.sqrt(32.0))),
                                    (o[:, 2, :, 8:16], w5[:, :, :, 1], float(np.sqrt(3.0) / 8.0))):
                    step(v.tensor_scalar(dst, src, s, None, ALU.mult))
                step(v.scalar_tensor_tensor(out=o[:, 2, :, 0:8], in0=o[:, 1, :, 8:16], scalar=-1.0 / 3.0,
                                            in1=o[:, 2, :, 0:8], op0=ALU.mult, op1=ALU.add))

        def clear_sum(rows):
            with nc.Block() as block:
                @block.vector
                def _(v):
                    v.memset(acc[0:rows, :], 0.0)

        def layernorm():
            d = big[:, 0:NB * D].rearrange("p (c f) -> p c f", f=D)
            sq = big[:, NB * D:2 * NB * D].rearrange("p (c f) -> p c f", f=D)
            r1 = big[:, 2 * NB * D:2 * NB * D + NB]
            r2 = big[:, 2 * NB * D + NB:2 * NB * D + 2 * NB]

            def spread(r):
                return r.unsqueeze(2).broadcast_to([P, NB, D])
            step_done, var_ready, std_ready = sem("ln_step"), sem("var_ready"), sem("std_ready")
            with nc.Block() as block:
                @block.vector
                def _(v):
                    step = Chain(v, step_done)
                    step(v.tensor_reduce(r1, x_nm[:], AX_X, ALU.add))
                    step(v.tensor_scalar(r1, r1, 1.0 / D, None, ALU.mult))
                    step(v.tensor_tensor(d, x_nm[:], spread(r1), ALU.subtract))
                    step(v.tensor_tensor(sq, d, d, ALU.mult))
                    step(v.tensor_reduce(r2, sq, AX_X, ALU.add))
                    v.tensor_scalar(r2, r2, 1.0 / D, EPS, ALU.mult, ALU.add).then_inc(var_ready, 1)
                    v.wait_ge(std_ready, 1)
                    step(v.reciprocal(r2, r1))
                    step(v.tensor_tensor(d, d, spread(r2), ALU.mult))
                    step(v.tensor_scalar(h_nm[:], d, 0.0, None, ALU.max))

                @block.scalar
                def _(a):
                    a.wait_ge(var_ready, 1)
                    a.activation(r1, r2, ACT.Sqrt).then_inc(std_ready, 1)

        def store_table(table, src_nm):
            stored = sem("table_stored")
            with nc.Block() as block:
                @block.sync
                def _(sp):
                    sp.dma_start(table[0:NP, :].rearrange("(c p) f -> p c f", p=P), src_nm).then_inc(stored, 16)
                    sp.wait_ge(stored, 16)

        def sum_to_nodes(rows, rhs, width, post):
            turned, used, step_done = sem("turned"), sem("turned_used"), sem("post_step")
            with nc.Block() as block:
                @block.tensor
                def _(pe):
                    for g in range(NB // GRP):
                        if g >= 2:
                            pe.wait_ge(used, g - 1)
                        for j in range(GRP):
                            c = g * GRP + j
                            last = pe.matmul(ps[g % 2][:, j * width:(j + 1) * width],
                                             acc[0:rows, c * P:(c + 1) * P], rhs, start=True, stop=True)
                        last.then_inc(turned, 1)

                @block.vector
                def _(v):
                    step = Chain(v, step_done)
                    for g in range(NB // GRP):
                        v.wait_ge(turned, g + 1)
                        post(v, ps[g % 2][:, 0:GRP * width].rearrange("p (c f) -> p c f", f=width),
                             g * GRP, step)
                        v.sem_inc(used, 1)

        def one_hots(v, ring, i, u, scalars=None):
            scalars = dst_rel if scalars is None else scalars
            for j in range(TJ):
                ins = v.tensor_scalar(ring[:, u % 2, j, :], iota[:], scalars[:, bass.ds((i * BU + u) * TJ + j, 1)],
                                      None, ALU.is_equal)
            return ins

        def add_windows(v, bank, rows, i, u, added):
            for j in range(TJ):
                t = (i * BU + u) * TJ + j
                n0 = v.value_load(first[0:1, bass.ds(t, 1)], min_val=0, max_val=N)
                if not (isinstance(t, int) and t == 0):
                    v.wait_ge(added, t)
                w = acc[0:rows, bass.ds(n0, P)]
                v.tensor_tensor(w, w, bank[0:rows, j * P:(j + 1) * P], ALU.add).then_inc(added, 1)

        def gather_loop(pool, table, rows_of, idx, idx_in, gathered, rows_free, free_back=2):
            may_gather = sem("may_gather")

            def unit(i, u):
                if u % 2 == 0:
                    pool.wait_ge(idx_in[u // 2], 16 * (i + 1))
                wait_units(pool, rows_free, i, u, free_back)
                pool.sem_inc(may_gather, 1)
                for j in range(TJ):
                    pool.indirect_dma_start(
                        out=rows_of(u, j), out_offset=None, in_=table,
                        in_offset=bass.IndirectOffsetOnAxis(ap=idx[:, u // 2, (u % 2) * TJ + j:(u % 2) * TJ + j + 1],
                                                            axis=0)).then_inc(gathered[u], 16)
            flow(pool, unit)

        def load_indices(sp, idx, idx_in, gathered, i, u):
            if not (isinstance(i, int) and i == 0):
                for k in (u, u + 1):
                    sp.wait_ge(gathered[k], i * 16 * TJ)
            sp.dma_start(idx[:, u // 2, :],
                         A["src_t"][:, bass.ds((i * BU + u) * TJ, 2 * TJ)]).then_inc(idx_in[u // 2], 16)

        def wait_gathered(eng, gathered, i, u):
            eng.wait_ge(gathered[u], 16 * TJ * (i + 1))

        with ExitStack() as own, nc.Block() as block:
            src_i = local(own, "src_i", [P, NT], I32)
            lo_i = local(own, "lo_i", [P, NT], I32)
            oh = local(own, "oh", [P, 2, TJ, 2, P], BF16)
            lo, hi = big[:, 0:NT], big[:, NT:2 * NT]
            loaded, step_done, hots, counted = sem("src_loaded"), sem("hist_step"), sem("hots"), sem("counted")

            @block.sync
            def _(sp):
                sp.dma_start(src_i[:], A["src_t"]).then_inc(loaded, 16)
                sp.wait_ge(loaded, 16)

            @block.vector
            def _(v):
                step = Chain(v, step_done)
                v.wait_ge(loaded, 16)
                step(v.tensor_scalar(lo_i[:], src_i[:], P - 1, None, ALU.bitwise_and))
                step(v.tensor_scalar(src_i[:], src_i[:], 7, None, ALU.logical_shift_right))
                step(v.tensor_copy(lo, lo_i[:]))
                step(v.tensor_copy(hi, src_i[:]))

                def unit(i, u):
                    wait_units(v, counted, i, u, 2)
                    for j in range(TJ):
                        t = (i * BU + u) * TJ + j
                        for k, part in enumerate((lo, hi)):
                            last = v.tensor_scalar(oh[:, u % 2, j, k, :], iota_b[:], part[:, bass.ds(t, 1)], None,
                                                   ALU.is_equal)
                    last.then_inc(hots, 1)
                flow(v, unit)
                v.wait_ge(counted, UNITS)
                v.tensor_copy(deg_out[:], ps[0][:, 0:NB])

            @block.tensor
            def _(pe):
                def unit(i, u):
                    wait_units(pe, hots, i, u)
                    for j in range(TJ):
                        s = isinstance(i, int) and i == 0 and u == 0 and j == 0
                        e = isinstance(i, int) and i == BODIES - 1 and u == BU - 1 and j == TJ - 1
                        last = pe.matmul(ps[0][:, 0:NB], oh[:, u % 2, j, 0, :], oh[:, u % 2, j, 1, 0:NB],
                                         start=s, stop=e)
                    last.then_inc(counted, 1)
                flow(pe, unit, last=unit)

        layernorm()
        store_table(h_table, h_nm[:])
        with ExitStack() as own:
            hT = local(own, "hT", [D, 2, 4 * P], F32)
            rows = local(own, "rows", [P, NB, 64], F32)
            turned, copied, prod, rows_out, stored = (sem("b_turned"), sem("b_copied"), sem("b_prod"),
                                                      sem("b_rows"), sem("b_stored"))
            NG = -(-NB // 4)
            with nc.Block() as block:
                @block.tensor
                def _(pe):
                    for g in range(NG):
                        n = min(4, NB - 4 * g)
                        if g >= 2:
                            pe.wait_ge(copied, g - 1)
                        for j in range(n):
                            last = pe.transpose(ps[g % 2][0:D, j * P:(j + 1) * P], h_nm[:, 4 * g + j, :], ident[:])
                        last.then_inc(turned, 1)
                        pe.wait_ge(copied, g + 1)
                        if g >= 2:
                            pe.wait_ge(rows_out, g - 1)
                        for j in range(n):
                            last = pe.matmul(ps[2 + g % 2][:, j * 64:(j + 1) * 64], hT[:, g % 2, j * P:(j + 1) * P],
                                             wb[:], start=True, stop=True)
                        last.then_inc(prod, 1)

                @block.scalar
                def _(a):
                    for g in range(NG):
                        n = min(4, NB - 4 * g)
                        a.wait_ge(turned, g + 1)
                        if g >= 2:
                            a.wait_ge(prod, g - 1)
                        a.copy(hT[:, g % 2, 0:n * P], ps[g % 2][0:D, 0:n * P]).then_inc(copied, 1)

                @block.vector
                def _(v):
                    for g in range(NG):
                        n = min(4, NB - 4 * g)
                        v.wait_ge(prod, g + 1)
                        v.tensor_copy(rows[:, 4 * g:4 * g + n, :],
                                      ps[2 + g % 2][:, 0:n * 64].rearrange("p (c f) -> p c f", f=64)).then_inc(rows_out, 1)

                @block.sync
                def _(sp):
                    sp.wait_ge(rows_out, NG)
                    sp.dma_start(b_table[0:NP, :].rearrange("(c p) f -> p c f", p=P), rows[:]).then_inc(stored, 16)
                    sp.dma_start(b_table[NP:NP + P, :], rows[:, 0, :]).then_inc(stored, 16)
                    sp.wait_ge(stored, 32)
        clear_sum(D)

        with ExitStack() as own:
            def ring(name, shape, dt=F32):
                return local(own, name, shape, dt)
            idx = ring("idx", [P, 2, 2 * TJ], I32)
            rows = ring("rows", [P, 2, TJ, D])
            feat = ring("feat", [64, 2, U])
            bwin = ring("bwin", [P, 2, TJ, 64])
            oh = ring("oh", [P, 2, TJ, P])
            ohT = ring("ohT", [P, 2, U])
            ohl = ring("ohl", [P, 2, TJ, P])
            hid = ring("hid", [65, 2, U])
            dst_b = ring("dst_b", [D, 2, U + 1], I32)
            keep = ring("keep", [D, 2, U])
            run = ring("run", [D, 2, U])
            runT = ring("runT", [P, 2, TJ, D])
            idx_in, ea_in, win_in, dst_in = sems("idx_in"), sems("ea_in"), sems("win_in"), sems("dst_in")
            gathered = sems("gathered", BU)
            (turned, rows_copied, oh_copied, hots, z_done, hid_done, v_done, kept, ran, run_turned, run_copied,
             last_hots, summed, added, ones_set, pe_go) = [sem(s) for s in (
                 "turned", "rows_copied", "oh_copied", "hots", "z_done", "hid_done", "v_done", "kept", "ran",
                 "run_turned", "run_copied", "last_hots", "summed", "added", "ones_set", "pe_go")]
            with nc.Block() as block:
                @block.sync
                def _(sp):
                    def unit(i, u):
                        n = i * BU + u
                        if u % 2 == 0:
                            load_indices(sp, idx, idx_in, gathered, i, u)
                        wait_units(sp, z_done, i, u, 2)
                        sp.dma_start(feat[D:2 * D, u % 2, :], A["eaT"][:, bass.ds(n * U, U)]).then_inc(ea_in[u % 2], 16)
                        for j in range(TJ):
                            n0 = sp.value_load(first[0:1, bass.ds(n * TJ + j, 1)], min_val=0, max_val=N)
                            sp.dma_start(bwin[:, u % 2, j, :], b_table[bass.ds(n0, P), :]).then_inc(win_in[u % 2], 16)
                        wait_units(sp, kept, i, u, 2)
                        sp.dma_start(dst_b[:, u % 2, :],
                                     A["dst_row"][bass.ds(n * U, U + 1)].partition_broadcast(D)).then_inc(dst_in[u % 2], 16)
                    flow(sp, unit)

                @block.gpsimd
                def _(pool):
                    gather_loop(pool, h_table, lambda u, j: rows[:, u % 2, j, :], idx, idx_in, gathered, turned)

                @block.tensor
                def _(pe):
                    def turn(i, u):
                        wait_gathered(pe, gathered, i, u)
                        wait_units(pe, rows_copied, i, u, 1)
                        wait_units(pe, hots, i, u)
                        wait_units(pe, oh_copied, i, u, 1)
                        for j in range(TJ):
                            pe.transpose(ps[0][0:D, j * P:(j + 1) * P], rows[:, u % 2, j, :], ident[:])
                        for j in range(TJ):
                            last = pe.transpose(ps[1][:, j * P:(j + 1) * P], oh[:, u % 2, j, :], ident[:])
                        last.then_inc(turned, 1)

                    def hidden(i, u):
                        wait_units(pe, rows_copied, i, u)
                        wait_slot(pe, ea_in, i, u)
                        wait_units(pe, hid_done, i, u, 1)
                        pe.sem_inc(pe_go, 1)
                        pe.matmul(ps[2][0:64, :], wz[:], feat[:, u % 2, :], start=True, stop=False)
                        wait_units(pe, oh_copied, i, u)
                        wait_slot(pe, win_in, i, u, 16 * TJ)
                        for j in range(TJ):
                            last = pe.matmul(ps[2][0:64, j * P:(j + 1) * P], bwin[:, u % 2, j, :],
                                             ohT[:, u % 2, j * P:(j + 1) * P], start=False, stop=(j == TJ - 1))
                        last.then_inc(z_done, 1)

                    def outputs(i, u):
                        wait_units(pe, hid_done, i, u)
                        wait_units(pe, ran, i, u, 1)
                        pe.matmul(ps[3][0:D, :], w2x[:], hid[:, u % 2, :], start=True, stop=True).then_inc(v_done, 1)

                    def turn_run(i, u):
                        wait_units(pe, ran, i, u)
                        wait_units(pe, run_copied, i, u, 1)
                        pe.sem_inc(pe_go, 1)
                        for j in range(TJ):
                            last = pe.transpose(ps[4][:, j * D:(j + 1) * D], run[:, u % 2, j * P:(j + 1) * P],
                                                ident[0:D, 0:D])
                        last.then_inc(run_turned, 1)

                    def window_sums(i, u):
                        wait_units(pe, run_copied, i, u)
                        wait_units(pe, last_hots, i, u)
                        wait_units(pe, added, i, u, 1, TJ)
                        for j in range(TJ):
                            last = pe.matmul(ps[5][0:D, j * P:(j + 1) * P], runT[:, u % 2, j, :], ohl[:, u % 2, j, :],
                                             start=True, stop=True)
                        last.then_inc(summed, 1)

                    stages = ((hidden, 1), (outputs, 2), (turn_run, 3), (window_sums, 4))
                    pe.wait_ge(ones_set, 1)

                    def drain(i, u):
                        for f, lag in stages:
                            if lag > u:
                                f(*before(i, u, lag))

                    def unit(i, u):
                        turn(i, u)
                        for f, lag in stages:
                            if before(i, u, lag) is not None:
                                f(*before(i, u, lag))
                    flow(pe, unit, tail=drain)

                @block.scalar
                def _(a):
                    def copies(i, u):
                        wait_units(a, turned, i, u)
                        wait_units(a, z_done, i, u, 2)
                        a.copy(feat[0:D, u % 2, :], ps[0][0:D, :]).then_inc(rows_copied, 1)
                        a.copy(ohT[:, u % 2, :], ps[1][:]).then_inc(oh_copied, 1)

                    def relu(i, u):
                        wait_units(a, z_done, i, u)
                        wait_units(a, v_done, i, u, 2)
                        a.activation(hid[0:64, u % 2, :], ps[2][0:64, :], ACT.Relu,
                                     bias=cols[0:64, 0:1]).then_inc(hid_done, 1)

                    def copy_run(i, u):
                        wait_units(a, run_turned, i, u)
                        wait_units(a, summed, i, u, 2)
                        a.copy(runT[:, u % 2].rearrange("p j f -> p (j f)"), ps[4][:, 0:TJ * D]).then_inc(run_copied, 1)

                    stages = ((relu, 1), (copy_run, 3))

                    def drain(i, u):
                        for f, lag in stages:
                            if lag > u:
                                f(*before(i, u, lag))

                    def unit(i, u):
                        copies(i, u)
                        for f, lag in stages:
                            if before(i, u, lag) is not None:
                                f(*before(i, u, lag))
                    flow(a, unit, tail=drain)

                @block.vector
                def _(v):
                    v.memset(hid[64:65, :, :], 1.0).then_inc(ones_set, 1)

                    def prepare(i, u):
                        wait_units(v, turned, i, u, 2)
                        one_hots(v, oh, i, u).then_inc(hots, 1)

                    def same_node(i, u):
                        wait_slot(v, dst_in, i, u)
                        wait_units(v, ran, i, u, 2)
                        v.tensor_tensor(keep[:, u % 2, :], dst_b[:, u % 2, 1:U + 1], dst_b[:, u % 2, 0:U],
                                        ALU.is_equal).then_inc(kept, 1)

                    def scan(i, u):
                        wait_units(v, v_done, i, u)
                        wait_units(v, kept, i, u)
                        wait_units(v, run_turned, i, u, 2)
                        wait_units(v, ran, i, u, 1)
                        start = isinstance(i, int) and i == 0 and u == 0
                        v.tensor_tensor_scan(run[:, u % 2, :], keep[:, u % 2, :], ps[3][0:D, :],
                                             0.0 if start else run[:, (u + 1) % 2, U - 1:U],
                                             ALU.mult, ALU.max).then_inc(ran, 1)

                    def last_edges(i, u):
                        wait_units(v, summed, i, u, 2)
                        one_hots(v, ohl, i, u, dst_last).then_inc(last_hots, 1)

                    def add(i, u):
                        wait_units(v, summed, i, u)
                        add_windows(v, ps[5], D, i, u, added)

                    stages = ((same_node, 1), (scan, 2), (last_edges, 3), (add, 4))

                    def drain(i, u):
                        for f, lag in stages:
                            if lag > u:
                                f(*before(i, u, lag))

                    def unit(i, u):
                        prepare(i, u)
                        for f, lag in stages:
                            if before(i, u, lag) is not None:
                                f(*before(i, u, lag))
                    flow(v, unit, tail=drain)

        def l0_out(v, view, c0, step):
            xs, hs = x_nm[:, c0:c0 + GRP, :], h_nm[:, c0:c0 + GRP, :]
            step(v.tensor_tensor(hs, view, hs, ALU.max))
            step(v.tensor_tensor(xs, xs, hs, ALU.add))
        sum_to_nodes(D, ident[0:D, 0:D], D, l0_out)

        layernorm()
        with ExitStack() as own:
            rows = local(own, "scaled", [P, NB, D + 1])
            inv, root = local(own, "inv", [P, NB]), local(own, "root", [P, NB])
            step_done, clamped, rooted, ready, stored = (sem("scale_step"), sem("clamped"), sem("rooted"),
                                                         sem("scaled_ready"), sem("scaled_stored"))
            with nc.Block() as block:
                @block.vector
                def _(v):
                    step = Chain(v, step_done)
                    v.tensor_scalar(inv[:], deg_out[:], 1.0, None, ALU.max).then_inc(clamped, 1)
                    step(v.memset(rows[:], 1.0))
                    v.wait_ge(rooted, 1)
                    step(v.reciprocal(inv[:], root[:]))
                    v.tensor_tensor(rows[:, :, 0:D], h_nm[:], inv[:].unsqueeze(2).broadcast_to([P, NB, D]),
                                    ALU.mult).then_inc(ready, 1)
                    v.memset(acc[0:D + 1, :], 0.0)

                @block.scalar
                def _(a):
                    a.wait_ge(clamped, 1)
                    a.activation(root[:], inv[:], ACT.Sqrt).then_inc(rooted, 1)

                @block.sync
                def _(sp):
                    sp.wait_ge(ready, 1)
                    sp.dma_start(h1_table.rearrange("(c p) f -> p c f", p=P), rows[:]).then_inc(stored, 16)
                    sp.wait_ge(stored, 16)

        with ExitStack() as own:
            idx = local(own, "idx", [P, 2, 2 * TJ], I32)
            rows = local(own, "rows", [P, 2, TJ, D + 1])
            oh = local(own, "oh", [P, 2, TJ, P])
            idx_in, gathered = sems("idx_in"), sems("gathered", BU)
            hots, summed, added = sem("hots"), sem("summed"), sem("added")
            with nc.Block() as block:
                @block.sync
                def _(sp):
                    def unit(i, u):
                        if u % 2 == 0:
                            load_indices(sp, idx, idx_in, gathered, i, u)
                    flow(sp, unit)

                @block.gpsimd
                def _(pool):
                    gather_loop(pool, h1_table, lambda u, j: rows[:, u % 2, j, :], idx, idx_in, gathered, summed)

                @block.tensor
                def _(pe):
                    def unit(i, u):
                        wait_units(pe, added, i, u, 2, TJ)
                        wait_units(pe, hots, i, u)
                        wait_gathered(pe, gathered, i, u)
                        for j in range(TJ):
                            last = pe.matmul(ps[u % 2][0:D + 1, j * P:(j + 1) * P], rows[:, u % 2, j, :],
                                             oh[:, u % 2, j, :], start=True, stop=True)
                        last.then_inc(summed, 1)
                    flow(pe, unit)

                @block.vector
                def _(v):
                    def add(i, u):
                        wait_units(v, summed, i, u)
                        add_windows(v, ps[u % 2], D + 1, i, u, added)

                    def unit(i, u):
                        wait_units(v, summed, i, u, 2)
                        one_hots(v, oh, i, u).then_inc(hots, 1)
                        if before(i, u, 1) is not None:
                            add(*before(i, u, 1))

                    def drain(i, u):
                        if u == 0:
                            add(*before(i, u, 1))
                    flow(v, unit, tail=drain)

        with ExitStack() as own:
            nodes = big[:, 0:NB * (D + 1)].rearrange("p (c f) -> p c f", f=D + 1)
            inv, root = local(own, "inv", [P, NB]), local(own, "root", [P, NB])

            def l1_out(v, view, c0, step):
                step(v.tensor_copy(nodes[:, c0:c0 + GRP, :], view))
            sum_to_nodes(D + 1, w_l1[:], D + 1, l1_out)
            step_done, clamped, rooted = sem("norm_step"), sem("clamped"), sem("rooted")
            with nc.Block() as block:
                @block.vector
                def _(v):
                    step = Chain(v, step_done)
                    out_l1 = nodes[:, :, 0:D]
                    v.tensor_scalar(inv[:], nodes[:, :, D], 1.0, None, ALU.max).then_inc(clamped, 1)
                    step(v.tensor_copy(acc[64:65, :], acc[D:D + 1, :]))
                    v.wait_ge(rooted, 1)
                    step(v.reciprocal(inv[:], root[:]))
                    step(v.tensor_tensor(out_l1, out_l1, inv[:].unsqueeze(2).broadcast_to([P, NB, D]), ALU.mult))
                    step(v.tensor_tensor(out_l1, out_l1, bias_l1[:].unsqueeze(1).broadcast_to([P, NB, D]), ALU.add))
                    step(v.scalar_tensor_tensor(out=x_nm[:], in0=out_l1, scalar=0.0, in1=x_nm[:],
                                                op0=ALU.max, op1=ALU.add))

                @block.scalar
                def _(a):
                    a.wait_ge(clamped, 1)
                    a.activation(root[:], inv[:], ACT.Sqrt).then_inc(rooted, 1)

        recycle()

        layernorm()
        store_table(h_table, h_nm[:])
        def lrelu(v, dst, src):
            return v.scalar_tensor_tensor(out=dst, in0=src, scalar=0.1, in1=src, op0=ALU.mult, op1=ALU.max)

        MEAN, VAR, TMP, SCALE, SHIFT = 19, 20, 21, 22, 23

        def fold(rows, width, w, gain, bias, col, row=None):
            step_done, var_ready, rooted, shifted, const = (sem("fold_step"), sem("var_ready"), sem("rooted"),
                                                            sem("shifted"), sem("const"))

            def c(n):
                return cols[0:rows, n:n + 1]
            with nc.Block() as block:
                @block.vector
                def _(v):
                    step = Chain(v, step_done)
                    v.tensor_scalar(c(TMP), c(VAR), EPS, None, ALU.add).then_inc(var_ready, 1)
                    v.wait_ge(rooted, 1)
                    step(v.reciprocal(c(TMP), c(SCALE)))
                    step(v.tensor_tensor(c(SCALE), c(TMP), c(gain), ALU.mult))
                    step(v.tensor_tensor(c(TMP), c(MEAN), c(SCALE), ALU.mult))
                    v.tensor_tensor(c(SHIFT), c(bias), c(TMP), ALU.subtract).then_inc(shifted, 1)
                    v.wait_ge(const, 1)
                    step(v.tensor_scalar(w, w, c(SCALE), None, ALU.mult))
                    if row is None:
                        step(v.tensor_tensor(cols[0:width, col:col + 1], ps[7][0:width, 0:1],
                                             cols[0:width, col:col + 1], ALU.add))
                    else:
                        step(v.tensor_tensor(row, ps[7][0:1, 0:width], col, ALU.add))

                @block.scalar
                def _(a):
                    a.wait_ge(var_ready, 1)
                    a.activation(c(SCALE), c(TMP), ACT.Sqrt).then_inc(rooted, 1)

                @block.tensor
                def _(pe):
                    pe.wait_ge(shifted, 1)
                    if row is None:
                        pe.matmul(ps[7][0:width, 0:1], w, c(SHIFT), start=True, stop=True).then_inc(const, 1)
                    else:
                        pe.matmul(ps[7][0:1, 0:width], c(SHIFT), w, start=True, stop=True).then_inc(const, 1)

        with ExitStack() as own:
            ea = local(own, "ea", [P, 2, QK * QC])
            st = local(own, "st", [P, QN * QK, 6])
            quarter = local(own, "quarter", [P, D])
            two = local(own, "two", [P, 2])
            sq = big[:, 0:NB * D].rearrange("p (c f) -> p c f", f=D)
            ea_in = sems("ea_in")
            stats, squared, weighed, ready, joined, step_done = (sem("stats"), sem("squared"), sem("weighed"),
                                                                 sem("ea_ready"), sem("joined"), sem("bn_step"))
            with nc.Block() as block:
                @block.sync
                def _(sp):
                    def chunk(c, k, free):
                        if free is not None:
                            sp.wait_ge(stats, free)
                        for q in range(4):
                            sp.dma_start(ea[q * D:(q + 1) * D, k, :],
                                         A["eaT"][:, bass.ds(q * (E // 4) + c * (QK * QC), QK * QC)]).then_inc(ea_in[k], 16)
                    for c in (0, 1):
                        chunk(c, c, None)
                    with sp.Fori(1, QN // 2) as g:
                        for k in range(2):
                            chunk(g * 2 + k, k, g * 2 + k - 1)
                    chunk(QN - 1, 0, QN - 2)

                @block.vector
                def _(v):
                    step = Chain(v, step_done)
                    v.tensor_tensor(sq, h_nm[:], h_nm[:], ALU.mult).then_inc(squared, 1)

                    def chunk(g, k):
                        v.wait_ge(ea_in[k], (g + 1) * 64)
                        for b in range(QK):
                            last = v.bn_stats(st[:, bass.ds((g * 2 + k) * QK + b, 1), :].rearrange("p a s -> p (a s)"),
                                              ea[:, k, b * QC:(b + 1) * QC])
                        last.then_inc(stats, 1)
                    with v.Fori(0, QN // 2) as g:
                        for k in range(2):
                            chunk(g, k)
                    chunk(QN // 2, 0)
                    v.wait_ge(stats, QN)
                    step(v.bn_aggr(two[:], st[:].rearrange("p a s -> p (a s)")))
                    step(v.scalar_tensor_tensor(out=two[:, 1:2], in0=two[:, 0:1], scalar=two[:, 0:1],
                                                in1=two[:, 1:2], op0=ALU.mult, op1=ALU.add))
                    step(v.tensor_reduce(quarter[:], ident[:].rearrange("p (q f) -> p f q", q=4), AX_X, ALU.add))
                    v.tensor_scalar(quarter[:], quarter[:], 0.25, None, ALU.mult).then_inc(ready, 1)
                    v.wait_ge(joined, 1)
                    v.wait_ge(weighed, 1)
                    for k in range(2):
                        step(v.tensor_scalar(cols[0:D, MEAN + k:MEAN + k + 1], ps[k][0:D, 0:1], 1.0 / E, None, ALU.mult))
                    step(v.tensor_copy(cols[D:2 * D, MEAN:MEAN + 2], ps[2][0:D, 0:2]))
                    m, s, t = (cols[0:64, n:n + 1] for n in (MEAN, VAR, TMP))
                    step(v.tensor_tensor(t, m, m, ALU.mult))
                    step(v.tensor_tensor(s, s, t, ALU.subtract))

                @block.tensor
                def _(pe):
                    pe.wait_ge(squared, 1)
                    for c in range(NB):
                        k = P if c < NB - 1 else TAIL
                        for b, src in enumerate((h_nm, sq)):
                            last = pe.matmul(ps[b][0:D, 0:1], src[0:k, c, :], deg_out[0:k, c:c + 1],
                                             start=(c == 0), stop=(c == NB - 1))
                    last.then_inc(weighed, 1)
                    pe.wait_ge(ready, 1)
                    pe.matmul(ps[2][0:D, 0:2], quarter[:], two[:], start=True, stop=True).then_inc(joined, 1)
        fold(64, 64, m1w[0][0:64, :], 3, 4, 9)

        with ExitStack() as own:
            idx = local(own, "idx", [P, 2, 2 * TJ], I32)
            rows = local(own, "rows", [P, 2, TJ, D])
            feat = local(own, "feat", [64, 2, U])
            zc = local(own, "zc", [64, 2, U])
            z1 = local(own, "z1", [64, BU, U])
            st = local(own, "st", [64, UNITS, 6])
            idx_in, ea_in, gathered, stored = sems("idx_in"), sems("ea_in"), sems("gathered", BU), sems("stored", BU)
            turned, copied, z_done, z_copied, z1_done, stats, pe_go = [sem(s) for s in (
                "turned", "copied", "z_done", "z_copied", "z1_done", "stats", "pe_go")]
            with nc.Block() as block:
                @block.sync
                def _(sp):
                    def store(i, u):
                        wait_units(sp, z1_done, i, u)
                        sp.dma_start(z1_dram[:, bass.ds((i * BU + u) * U, U)], z1[:, u, :]).then_inc(stored[u], 16)

                    def unit(i, u):
                        if u % 2 == 0:
                            load_indices(sp, idx, idx_in, gathered, i, u)
                        wait_units(sp, z_done, i, u, 2)
                        sp.dma_start(feat[D:2 * D, u % 2, :],
                                     A["eaT"][:, bass.ds((i * BU + u) * U, U)]).then_inc(ea_in[u % 2], 16)
                        if before(i, u, 2) is not None:
                            store(*before(i, u, 2))

                    def drain(i, u):
                        if u < 2:
                            store(*before(i, u, 2))
                    flow(sp, unit, tail=drain)
                    for u in range(BU):
                        sp.wait_ge(stored[u], 16 * BODIES)

                @block.gpsimd
                def _(pool):
                    gather_loop(pool, h_table, lambda u, j: rows[:, u % 2, j, :], idx, idx_in, gathered, turned)

                @block.tensor
                def _(pe):
                    def product(i, u):
                        wait_units(pe, copied, i, u)
                        wait_units(pe, z_copied, i, u, 2)
                        wait_slot(pe, ea_in, i, u)
                        pe.sem_inc(pe_go, 1)
                        pe.matmul(ps[2 + u % 2][0:64, :], m1w[0][0:64, :], feat[:, u % 2, :],
                                  start=True, stop=True).then_inc(z_done, 1)

                    def unit(i, u):
                        wait_units(pe, copied, i, u, 2)
                        wait_gathered(pe, gathered, i, u)
                        for j in range(TJ):
                            last = pe.transpose(ps[u % 2][0:D, j * P:(j + 1) * P], rows[:, u % 2, j, :], ident[:])
                        last.then_inc(turned, 1)
                        if before(i, u, 1) is not None:
                            product(*before(i, u, 1))

                    def drain(i, u):
                        if u == 0:
                            product(*before(i, u, 1))
                    flow(pe, unit, tail=drain)

                @block.scalar
                def _(a):
                    def add_const(i, u):
                        wait_units(a, z_done, i, u)
                        wait_units(a, z1_done, i, u, 2)
                        a.activation(zc[:, u % 2, :], ps[2 + u % 2][0:64, :], ACT.Identity,
                                     bias=cols[0:64, 9:10]).then_inc(z_copied, 1)

                    def unit(i, u):
                        wait_units(a, z_done, i, u, 2)
                        wait_units(a, turned, i, u)
                        a.copy(feat[0:D, u % 2, :], ps[u % 2][0:D, :]).then_inc(copied, 1)
                        if before(i, u, 1) is not None:
                            add_const(*before(i, u, 1))

                    def drain(i, u):
                        if u == 0:
                            add_const(*before(i, u, 1))
                    flow(a, unit, tail=drain)

                @block.vector
                def _(v):
                    def unit(i, u, n=U):
                        if not (isinstance(i, int) and i == 0):
                            v.wait_ge(stored[u], i * 16)
                            v.wait_ge(stats, (i - 1) * BU + u + 1)
                        wait_units(v, z_copied, i, u)
                        lrelu(v, z1[:, u, :], zc[:, u % 2, :]).then_inc(z1_done, 1)
                        wait_units(v, z1_done, i, u)
                        v.bn_stats(st[:, bass.ds(i * BU + u, 1), :].rearrange("p a s -> p (a s)"),
                                   z1[:, u, 0:n]).then_inc(stats, 1)
                    flow(v, unit, last=lambda i, u: unit(i, u, U if u < BU - 1 else LAST))
                    v.wait_ge(stats, UNITS)
                    v.bn_aggr(cols[0:64, MEAN:MEAN + 2], st[:].rearrange("p a s -> p (a s)"))
        fold(64, 64, m1w[1][0:64, :], 5, 6, c_rows[:, 0, :], m1w[1][64:65, :])
        clear_sum(64)

        with ExitStack() as own:
            z1 = local(own, "z1", [65, 2, U])
            zc = local(own, "zc", [P, 2, TJ * 64])
            z2 = local(own, "z2", [P, 2, TJ, 64])
            oh = local(own, "oh", [P, 2, TJ, P])
            z1_in = sems("z1_in")
            (hots, z_done, z_copied, z2_done, summed, added, ones_set) = [sem(s) for s in (
                "hots", "z_done", "z_copied", "z2_done", "summed", "added", "ones_set")]
            with nc.Block() as block:
                @block.sync
                def _(sp):
                    def unit(i, u):
                        wait_units(sp, z_done, i, u, 2)
                        sp.dma_start(z1[0:64, u % 2, :], z1_dram[:, bass.ds((i * BU + u) * U, U)]).then_inc(z1_in[u % 2], 16)
                    flow(sp, unit)

                @block.tensor
                def _(pe):
                    pe.wait_ge(ones_set, 1)

                    def sums(i, u, last_unit=False):
                        wait_units(pe, z2_done, i, u)
                        wait_units(pe, hots, i, u)
                        wait_units(pe, added, i, u, 2, TJ)
                        for j in range(TJ):
                            z = z2[:, u % 2, j, :]
                            last = pe.matmul(ps[2 + u % 2][0:64, j * P:(j + 1) * P], z, oh[:, u % 2, j, :],
                                             start=True, stop=True)
                        for j in range(TJ):
                            k = P if not last_unit else LAST if j == 0 else 0
                            if k:
                                z = z2[0:k, u % 2, j, :]
                                last = pe.matmul(ps[4][0:64, 0:64], z, z,
                                                 start=(isinstance(i, int) and i == 0 and u == 0 and j == 0),
                                                 stop=last_unit)
                        last.then_inc(summed, 1)

                    def unit(i, u):
                        wait_units(pe, z_copied, i, u, 2)
                        wait_slot(pe, z1_in, i, u)
                        for j in range(TJ):
                            last = pe.matmul(ps[u % 2][:, j * 64:(j + 1) * 64], z1[:, u % 2, j * P:(j + 1) * P],
                                             m1w[1][:], start=True, stop=True)
                        last.then_inc(z_done, 1)
                        if before(i, u, 1) is not None:
                            sums(*before(i, u, 1))

                    def drain(i, u):
                        if u == 0:
                            sums(*before(i, u, 1), last_unit=True)
                    flow(pe, unit, tail=drain)

                @block.scalar
                def _(a):
                    def unit(i, u):
                        wait_units(a, z2_done, i, u, 2)
                        wait_units(a, z_done, i, u)
                        a.copy(zc[:, u % 2, :], ps[u % 2][:, 0:TJ * 64]).then_inc(z_copied, 1)
                    flow(a, unit)

                @block.vector
                def _(v):
                    v.memset(z1[64:65, :, :], 1.0).then_inc(ones_set, 1)

                    def add(i, u):
                        wait_units(v, summed, i, u)
                        add_windows(v, ps[2 + u % 2], 64, i, u, added)

                    def unit(i, u):
                        wait_units(v, summed, i, u, 2)
                        one_hots(v, oh, i, u).then_inc(hots, 1)
                        wait_units(v, z_copied, i, u)
                        lrelu(v, z2[:, u % 2].rearrange("p j f -> p (j f)"), zc[:, u % 2, :]).then_inc(z2_done, 1)
                        if before(i, u, 2) is not None:
                            add(*before(i, u, 2))

                    def drain(i, u):
                        if u < 2:
                            add(*before(i, u, 2))
                    flow(v, unit, tail=drain)

        with ExitStack() as own:
            gram = local(own, "gram", [64, 64])
            step_done = sem("bn_step")
            with nc.Block() as block:
                @block.vector
                def _(v):
                    step = Chain(v, step_done)
                    m, s, t = (cols[0:64, n:n + 1] for n in (MEAN, VAR, TMP))
                    step(v.tensor_reduce(m, acc[0:64, 0:N], AX_X, ALU.add))
                    step(v.tensor_scalar(m, m, 1.0 / E, None, ALU.mult))
                    step(v.tensor_tensor(gram[:], ps[4][0:64, 0:64], ident[0:64, 0:64], ALU.mult))
                    step(v.tensor_reduce(s, gram[:], AX_X, ALU.add))
                    step(v.tensor_tensor(t, m, m, ALU.mult))
                    step(v.scalar_tensor_tensor(out=s, in0=s, scalar=1.0 / E, in1=t, op0=ALU.mult, op1=ALU.subtract))
        fold(64, 64, m1w[2][0:64, :], 7, 8, c_rows[:, 1, :], m1w[2][64:65, :])

        recycle()

        turned, copied, prod, prod_copied = sem("n_turned"), sem("n_copied"), sem("n_prod"), sem("n_prod_copied")
        NG = -(-NB // 4)
        with nc.Block() as block:
            @block.tensor
            def _(pe):
                for g in range(NG):
                    if g >= 2:
                        pe.wait_ge(copied, g - 1)
                    for j in range(min(4, NB - 4 * g)):
                        last = pe.transpose(ps[g % 2][0:D, j * P:(j + 1) * P], h_nm[:, 4 * g + j, :], ident[:])
                    last.then_inc(turned, 1)
                for g in range(NCH):
                    if g >= 2:
                        pe.wait_ge(prod_copied, g - 1)
                    pe.matmul(ps[2 + g % 2][0:64, 0:CH], m1w[2][:], acc[0:65, g * CH:(g + 1) * CH],
                              start=True, stop=True).then_inc(prod, 1)

            @block.scalar
            def _(a):
                for g in range(NG):
                    n = min(4, NB - 4 * g) * P
                    a.wait_ge(turned, g + 1)
                    a.copy(big[64:96, g * 4 * P:g * 4 * P + n], ps[g % 2][0:D, 0:n]).then_inc(copied, 1)

            @block.vector
            def _(v):
                for g in range(NCH):
                    v.wait_ge(prod, g + 1)
                    v.tensor_copy(big[0:64, g * CH:(g + 1) * CH], ps[2 + g % 2][0:64, 0:CH]).then_inc(prod_copied, 1)

        with ExitStack() as own:
            st = local(own, "st", [96, NCH, 6])
            for k in range(3):
                width = 96 if k < 2 else D
                stats = sem("node_stats")
                with nc.Block() as block:
                    @block.vector
                    def _(v):
                        for g in range(NCH):
                            v.bn_stats(st[:, g, :], big[0:96, g * CH:(g + 1) * CH]).then_inc(stats, 1)
                        v.wait_ge(stats, NCH)
                        v.bn_aggr(cols[0:96, MEAN:MEAN + 2], st[:].rearrange("p a s -> p (a s)"))
                w = m2w[k][:, 0:width]
                fold(96, width, w, 10 + 2 * k, 11 + 2 * k, 16 + k)
                prod, used, shifted = sem("node_prod"), sem("node_used"), sem("node_shifted")
                zc = local(own, "zc", [96, 2, CH])
                with nc.Block() as block:
                    @block.tensor
                    def _(pe):
                        for g in range(NCH):
                            if g >= 4:
                                pe.wait_ge(used, g - 3)
                            pe.matmul(ps[g % 4][0:width, 0:CH], w, big[0:96, g * CH:(g + 1) * CH],
                                      start=True, stop=True).then_inc(prod, 1)

                    @block.scalar
                    def _(a):
                        for g in range(NCH):
                            a.wait_ge(prod, g + 1)
                            if k < 2 and g >= 2:
                                a.wait_ge(shifted, g - 1)
                            dst = zc[:, g % 2, :] if k < 2 else acc[0:D, g * CH:(g + 1) * CH]
                            a.activation(dst, ps[g % 4][0:width, 0:CH], ACT.Identity,
                                         bias=cols[0:width, 16 + k:17 + k]).then_inc(used, 1)

                    @block.vector
                    def _(v):
                        for g in range(NCH if k < 2 else 0):
                            v.wait_ge(used, g + 1)
                            lrelu(v, big[0:96, g * CH:(g + 1) * CH], zc[:, g % 2, :]).then_inc(shifted, 1)

        def add_to_x(v, view, c0, step):
            xs = x_nm[:, c0:c0 + GRP, :]
            step(v.tensor_tensor(xs, xs, view, ALU.add))
        sum_to_nodes(D, ident[0:D, 0:D], D, add_to_x)

        recycle()

        layernorm()
        store_table(h_table, h_nm[:])
        r5 = big[:, 0:NT * 5].rearrange("p (t k) -> p t k", k=5)
        with ExitStack() as own:
            rel = local(own, "rel", [P, NT, 3])
            n2, root = acc[:, 0:NT], acc[:, NT:2 * NT]
            sq = acc[:, 2 * NT:5 * NT].rearrange("p (t k) -> p t k", k=3)
            loaded, step_done, summed, rooted = sem("rel_loaded"), sem("rel_step"), sem("rel_summed"), sem("rel_rooted")
            with nc.Block() as block:
                @block.sync
                def _(sp):
                    sp.dma_start(rel[:], A["rel_t"]).then_inc(loaded, 16)
                    sp.wait_ge(loaded, 16)

                @block.vector
                def _(v):
                    step = Chain(v, step_done)
                    v.wait_ge(loaded, 16)
                    step(v.tensor_tensor(sq, rel[:], rel[:], ALU.mult))
                    v.tensor_reduce(n2, sq, AX_X, ALU.add).then_inc(summed, 1)
                    v.wait_ge(rooted, 1)
                    step(v.reciprocal(n2, root))
                    for k in range(5):
                        step(v.tensor_tensor(r5[:, :, k], rel[:, :, (k + 1) % 3], n2, ALU.mult))
                    step(v.memset(acc[0:D, :], 0.0))

                @block.scalar
                def _(a):
                    a.wait_ge(summed, 1)
                    a.activation(root, n2, ACT.Sqrt).then_inc(rooted, 1)

        with ExitStack() as own:
            idx = local(own, "idx", [P, 2, 2 * TJ], I32)
            rows = local(own, "rows", [P, 2, TJ, D])
            dist = local(own, "dist", [64, 2, U])
            hid = local(own, "hid", [65, 2, U])
            oh = local(own, "oh", [P, 2, TJ, P])
            r = local(own, "r", [P, 2, TJ, 5])
            f_d = local(own, "f_d", [P, 2, TJ, 16])
            f_x = local(own, "f_x", [P, 2, TJ, 5, 16])
            t1 = local(own, "t1", [P, TJ, 3, 8])
            t2 = local(own, "t2", [P, TJ, 3, 8])
            t3 = local(own, "t3", [P, TJ, 3, 8])
            prod = local(own, "prod", [P, 2, 40, 16])
            msg = local(own, "msg", [P, 2, TJ, 40])
            rb = local(own, "rb", [P, 8 * TJ, 3])
            idx_in, dist_in, gathered = sems("idx_in"), sems("dist_in"), sems("gathered", BU)
            (spread, hid_done, r_done, r_used, x_step, x_done, hots, prods, reduced, msg_step, msg_done, summed,
             added, ones_set, may_gather) = [sem(s) for s in (
                 "spread", "hid_done", "r_done", "r_used", "x_step", "x_done", "hots", "prods", "reduced", "msg_step",
                 "msg_done", "summed", "added", "ones_set", "may_gather")]
            with nc.Block() as block:
                @block.sync
                def _(sp):
                    def unit(i, u):
                        if u % 2 == 0:
                            load_indices(sp, idx, idx_in, gathered, i, u)
                        wait_units(sp, hid_done, i, u, 2)
                        sp.dma_start(dist[:, u % 2, :],
                                     A["dist"][bass.ds((i * BU + u) * U, U)].partition_broadcast(64)).then_inc(dist_in[u % 2], 16)
                    flow(sp, unit)

                @block.gpsimd
                def _(pool):
                    XS = 5

                    def gather(i, u):
                        if u % 2 == 0:
                            pool.wait_ge(idx_in[u // 2], 16 * (i + 1))
                        wait_units(pool, spread, i, u, 2)
                        pool.sem_inc(may_gather, 1)
                        for j in range(TJ):
                            pool.indirect_dma_start(
                                out=rows[:, u % 2, j, :], out_offset=None, in_=h_table,
                                in_offset=bass.IndirectOffsetOnAxis(
                                    ap=idx[:, u // 2, (u % 2) * TJ + j:(u % 2) * TJ + j + 1], axis=0)).then_inc(gathered[u], 16)

                    def cross(i, u):
                        base = (i * BU + u) * XS
                        wait_units(pool, spread, i, u)
                        wait_units(pool, prods, i, u, 2, TJ)

                        def rr(lo):
                            return r[:, u % 2, :, lo:lo + 3].unsqueeze(3).broadcast_to([P, TJ, 3, 8])

                        def f(lo):
                            return f_x[:, u % 2, :, lo:lo + 3, 0:8]
                        if not (isinstance(i, int) and i == 0 and u == 0):
                            pool.wait_ge(x_done, i * BU + u)
                        pool.tensor_tensor(t1[:], f(2), rr(1), ALU.mult).then_inc(x_step, 1)
                        pool.tensor_tensor(t2[:], f(1), rr(2), ALU.mult).then_inc(x_step, 1)
                        pool.tensor_tensor(t3[:], f(0), rr(0), ALU.mult).then_inc(x_step, 1)
                        pool.wait_ge(x_step, base + 3)
                        pool.tensor_tensor(f_x[:, u % 2, :, 0:3, 8:16], t1[:], t2[:], ALU.subtract).then_inc(x_step, 1)
                        pool.tensor_tensor(t3[:, :, 0, :], t3[:, :, 0, :], t3[:, :, 1, :], ALU.add).then_inc(x_step, 1)
                        pool.wait_ge(x_step, base + 5)
                        pool.tensor_tensor(f_d[:, u % 2, :, 8:16], t3[:, :, 0, :], t3[:, :, 2, :], ALU.add).then_inc(x_done, 1)

                    def unit(i, u):
                        gather(i, u)
                        if before(i, u, 2) is not None:
                            cross(*before(i, u, 2))

                    def drain(i, u):
                        if u < 2:
                            cross(*before(i, u, 2))
                    flow(pool, unit, tail=drain)

                @block.scalar
                def _(a):
                    def unit(i, u):
                        wait_slot(a, dist_in, i, u)
                        wait_units(a, r_done, i, u, 2, TJ)
                        a.activation(hid[0:64, u % 2, :], dist[:, u % 2, :], ACT.Relu, bias=cols[0:64, 2:3],
                                     scale=cols[0:64, 1:2]).then_inc(hid_done, 1)
                        wait_gathered(a, gathered, i, u)
                        wait_units(a, prods, i, u, 2, TJ)
                        wait_units(a, msg_done, i, u, 2)
                        f1 = rows[:, u % 2, :, 8:32].rearrange("p j (v o) -> p j o v", o=3)
                        a.copy(f_d[:, u % 2, :, 0:8], rows[:, u % 2, :, 0:8])
                        a.copy(f_x[:, u % 2, :, 0:3, 0:8], f1)
                        a.copy(f_x[:, u % 2, :, 3:5, 0:8], f1[:, :, 0:2, :])
                        a.copy(r[:, u % 2], r5[:, bass.ds((i * BU + u) * TJ, TJ), :]).then_inc(spread, 1)
                    flow(a, unit)

                @block.tensor
                def _(pe):
                    pe.wait_ge(ones_set, 1)

                    def window_sums(i, u):
                        wait_units(pe, hots, i, u)
                        wait_units(pe, added, i, u, 2, TJ)
                        wait_units(pe, msg_done, i, u)
                        for j in range(TJ):
                            last = pe.matmul(ps[4 + u % 2][0:D, j * P:(j + 1) * P], msg[:, u % 2, j, 0:D],
                                             oh[:, u % 2, j, :], start=True, stop=True)
                        last.then_inc(summed, 1)

                    def unit(i, u):
                        wait_units(pe, hid_done, i, u)
                        for j in range(TJ):
                            t = (i * BU + u) * TJ + j
                            if not (isinstance(i, int) and i == 0 and u == 0):
                                pe.wait_ge(r_used, t - TJ + 1)
                            pe.matmul(ps[j][:, 0:384], hid[:, u % 2, j * P:(j + 1) * P], w2m[:],
                                      start=True, stop=True).then_inc(r_done, 1)
                        if before(i, u, 2) is not None:
                            window_sums(*before(i, u, 2))

                    def drain(i, u):
                        if u < 2:
                            window_sums(*before(i, u, 2))
                    flow(pe, unit, tail=drain)

                @block.vector
                def _(v):
                    v.memset(hid[64:65, :, :], 1.0).then_inc(ones_set, 1)

                    def products(i, u, j):
                        t = (i * BU + u) * TJ + j
                        o = prod[:, j % 2]
                        R = ps[j][:, 0:384].rearrange("p (b u v) -> p b u v", b=3, v=16)
                        v.wait_ge(r_done, t + 1)
                        if j >= 2 or not (isinstance(i, int) and i == 0 and u == 0):
                            v.wait_ge(reduced, t - 1)
                        fd = f_d[:, u % 2, j, :].unsqueeze(1).broadcast_to([P, 8, 16])
                        v.tensor_tensor(o[:, 0:8, :], R[:, 0], fd, ALU.mult)
                        v.tensor_tensor(o[:, 32:40, :], R[:, 1], fd, ALU.mult)
                        fx = f_x[:, u % 2, j, 0:3, :].unsqueeze(1).broadcast_to([P, 8, 3, 16])
                        v.tensor_tensor(o[:, 8:32, :].rearrange("p (u o) v -> p u o v", o=3),
                                        R[:, 2].unsqueeze(2).broadcast_to([P, 8, 3, 16]), fx,
                                        ALU.mult).then_inc(prods, 1)

                    def reduce(i, u, j):
                        v.wait_ge(prods, (i * BU + u) * TJ + j + 1)
                        v.sem_inc(r_used, 1)
                        v.tensor_reduce(msg[:, u % 2, j, :], prod[:, j % 2], AX_X, ALU.add).then_inc(reduced, 1)

                    def direct(i, u):
                        n = i * BU + u
                        v.wait_ge(reduced, (n + 1) * TJ)
                        if not (isinstance(i, int) and i == 0 and u == 0):
                            v.wait_ge(msg_done, n)
                        for j in range(TJ):
                            v.tensor_tensor(rb[:, 8 * j:8 * j + 8, :],
                                            msg[:, u % 2, j, 32:40].unsqueeze(2).broadcast_to([P, 8, 3]),
                                            r[:, u % 2, j, 0:3].unsqueeze(1).broadcast_to([P, 8, 3]),
                                            ALU.mult).then_inc(msg_step, 1)
                        v.wait_ge(msg_step, (n + 1) * TJ)
                        for j in range(TJ):
                            m = msg[:, u % 2, j, 8:32].rearrange("p (u o) -> p u o", o=3)
                            last = v.tensor_tensor(m, m, rb[:, 8 * j:8 * j + 8, :], ALU.add)
                        last.then_inc(msg_done, 1)

                    def add(i, u):
                        wait_units(v, summed, i, u)
                        add_windows(v, ps[4 + u % 2], D, i, u, added)

                    def unit(i, u):
                        wait_units(v, summed, i, u, 2)
                        one_hots(v, oh, i, u).then_inc(hots, 1)
                        wait_units(v, x_done, i, u)
                        for j in range(TJ + 1):
                            if j < TJ:
                                products(i, u, j)
                            if j > 0:
                                reduce(i, u, j - 1)
                        direct(i, u)
                        if before(i, u, 2) is not None:
                            add(*before(i, u, 2))

                    def drain(i, u):
                        if u < 2:
                            add(*before(i, u, 2))
                    flow(v, unit, tail=drain)

        sum_to_nodes(D, ident[0:D, 0:D], D, add_to_x)
        finish(nc, sem, x_nm, out)


def finish(nc, sem, x_nm, out):
    done = sem("out_stored")
    with nc.Block() as block:
        @block.sync
        def _(sp):
            sp.dma_start(out[0:(NB - 2) * P, :].rearrange("(c p) f -> p c f", p=P),
                         x_nm[:, 0:NB - 2, :]).then_inc(done, 16)
            sp.dma_start(out[(NB - 2) * P:(NB - 1) * P, :], x_nm[:, NB - 2, :]).then_inc(done, 16)
            sp.dma_start(out[(NB - 1) * P:N, :], x_nm[0:TAIL, NB - 1, :]).then_inc(done, 16)
            sp.wait_ge(done, 48)


_WEIGHTS = ["L0_gnn_W1", "L0_gnn_b1", "L0_gnn_W2", "L0_gnn_b2", "L1_gnn_weight", "L1_gnn_bias"] + \
    [f"L2_gnn_m{m}_{k}{n}" for m in (1, 2) for n in (1, 2, 3) for k in "gbwc"] + \
    ["L3_gnn_w1", "L3_gnn_b1", "L3_gnn_w2", "L3_gnn_b2"]


def kernel(**inputs):
    import concourse.bacc as _bacc
    from concourse import mybir as _mybir
    from concourse.bass_utils import run_bass_kernel_spmd as _run

    a = {k: np.asarray(v) for k, v in inputs.items()}

    def padded(v, fill):
        return np.concatenate([v, np.full((EP - E,) + v.shape[1:], fill, v.dtype)])

    src, dst = padded(a["src"], PAD_SRC), padded(a["dst"], N)
    arrays = {
        "x": a["x"],
        "src_t": src.reshape(NT, P).T,
        "dst_t": dst.reshape(NT, P).T,
        "next_t": np.concatenate([dst[1:], dst[-1:]]).reshape(NT, P).T,
        "first": dst.reshape(NT, P)[:, 0],
        "dst_row": np.concatenate([np.full((1,), -1, dst.dtype), dst]),
        "eaT": padded(a["edge_attr_32"], 0).T,
        "rel_t": padded(a["edge_attr_3"], 1).reshape(NT, P, 3).transpose(1, 0, 2),
        "dist": padded(a["edge_weight"], 0),
    }
    for k in _WEIGHTS:
        arrays[k] = a[k]
    arrays = {k: np.ascontiguousarray(v) for k, v in arrays.items()}
    nc = _bacc.Bacc("TRN2", target_bir_lowering=False, num_devices=1)
    A = {k: nc.dram_tensor("in_" + k, list(v.shape), _mybir.dt.from_np(v.dtype), kind="ExternalInput").ap()
         for k, v in arrays.items()}
    out = nc.dram_tensor("out", [N, D], F32, kind="ExternalOutput").ap()
    build(nc, A, out)
    r = _run(nc, [{"in_" + k: v for k, v in arrays.items()}], core_ids=[0])
    return r.results[0]["out"]
```

```python
from contextlib import ExitStack

import numpy as np

import concourse.bass as bass
from concourse import mybir

F32 = mybir.dt.float32
BF16 = mybir.dt.bfloat16
I32 = mybir.dt.int32
ALU = mybir.AluOpType
ACT = mybir.ActivationFunctionType
AX_X = mybir.AxisListType.X

P = 128
N = 12500
E = 212500
D = 32
NB = -(-N // P)
NP = NB * P
TAIL = N - (NB - 1) * P
PAD_SRC = NP - 1
TJ = 4
U = TJ * P
BU = 4
BODY = BU * U
BODIES = -(-E // BODY)
EP = BODIES * BODY
NT = EP // P
UNITS = NT // TJ
LAST = E - (UNITS - 1) * U
W = 64
ACC = 12672
CH = 500
NCH = N // CH
EPS = 1e-5
GRP = 14
QC, QK, QN = 425, 5, 25
assert 4 * QC * QK * QN == E and NB % GRP == 0 and 0 < LAST < P


def flow(eng, body, last=None, tail=None, bu=BU):
    for u in range(bu):
        body(0, u)
    end = BODIES - 1 if last else BODIES
    with eng.Fori(1, end) as i:
        for u in range(bu):
            body(i, u)
    if last:
        for u in range(bu):
            last(BODIES - 1, u)
    if tail:
        for u in range(bu):
            tail(BODIES, u)


def before(i, u, lag, bu=BU):
    u -= lag
    if u < 0:
        if isinstance(i, int) and i == 0:
            return None
        i, u = i - 1, u + bu
    return i, u


def wait_units(eng, sem, i, u, back=0, per=1, bu=BU):
    w = before(i, u, back, bu)
    if w is not None:
        eng.wait_ge(sem, (w[0] * bu + w[1] + 1) * per)


def wait_pairs(eng, sem, i, k, back=0, per=1):
    wait_units(eng, sem, i, k, back, per, BU // 2)


def wait_slot(eng, sems, i, u, per=16):
    eng.wait_ge(sems[u % 2], (i * (BU // 2) + u // 2 + 1) * per)


def staged(stages, bu=BU):
    def unit(i, u):
        for f, lag in stages:
            if before(i, u, lag, bu) is not None:
                f(*before(i, u, lag, bu))

    def drain(i, u):
        for f, lag in stages:
            if lag > u:
                f(*before(i, u, lag, bu))
    return unit, drain


def build(nc, A, out):
    with ExitStack() as ctx:
        n_sem = [0]
        in_use = []

        def sb(name, shape, dt=F32):
            return ctx.enter_context(nc.sbuf_tensor(name, shape, dt))

        def local(own, name, shape, dt=F32):
            n_sem[0] += 1
            return own.enter_context(nc.sbuf_tensor(f"{name}_{n_sem[0]}", shape, dt))

        def sem(name):
            n_sem[0] += 1
            handle = nc.alloc_semaphore(name=f"{name}_{n_sem[0]}")
            in_use.append(handle)
            return handle

        def recycle():
            nc.clear_and_free_semaphores(in_use)
            in_use.clear()
            nc.all_engine_barrier()

        def sems(name, n=2):
            return [sem(f"{name}{k}") for k in range(n)]

        def dram(name, shape, dt=F32):
            return nc.dram_tensor(name, shape, dt, kind="Internal").ap()

        h_table = dram("h_table", [NP, D])
        h1_table = dram("h1_table", [NP, D + 1])
        b_table = dram("b_table", [NP + P, 64])
        keep_dram = dram("keep_dram", [EP])
        z1_dram = dram("z1_dram", [64, EP])

        ident = sb("ident", [P, P])
        iota = sb("iota", [P, P])
        iota_b = sb("iota_b", [P, P], BF16)
        x_nm = sb("x_nm", [P, NB, D])
        h_nm = sb("h_nm", [P, NB, D])
        dst_rel = [sb(f"dst_rel{k}", [P, NT]) for k in range(2)]
        dst_last = [sb(f"dst_last{k}", [P, NT]) for k in range(2)]
        node_of = [sb("node_of0", [P, NT]), sb("node_of1", [P, UNITS])]
        narrow_ok = sb("narrow_ok", [1, 1], I32)
        fold4 = sb("fold4", [P, D])
        fold_msg = sb("fold_msg", [P, D])
        first = sb("first", [1, NT], I32)
        deg_out = sb("deg_out", [P, NB])
        acc = sb("acc", [P, ACC])
        big = sb("big", [P, NP])
        src_lo, src_hi = big[:, 4 * NT:5 * NT], big[:, 5 * NT:6 * NT]
        ps = [ctx.enter_context(nc.psum_tensor(f"bank{k}", [P, 512], F32)) for k in range(8)]

        wz = sb("wz", [64, 64])
        wb = sb("wb", [D, 64])
        cols = sb("cols", [P, 32])
        w2x = sb("w2x", [65, D])
        w_l1 = sb("w_l1", [D + 1, D + 1])
        bias_l1 = sb("bias_l1", [P, D])
        m1w = [sb(f"m1w{k}", [65, 64]) for k in range(3)]
        c_rows = sb("c_rows", [1, 2, 64])
        m2w = [sb(f"m2w{k}", [96, 96]) for k in range(3)]
        w2r = sb("w2r", [65, 384])
        w2m = sb("w2m", [65, 384])

        class Chain:

            def __init__(self, eng, sem):
                self.eng, self.sem, self.n = eng, sem, 0

            def __call__(self, ins):
                self.n += 1
                ins.then_inc(self.sem, 1)
                self.eng.wait_ge(self.sem, self.n)

        with ExitStack() as own, nc.Block() as block:
            keep_dram_ready, keep_in, keep_stored = sem("keep_ready"), sem("keep_in"), sem("keep_stored")
            widest_ready, widest_turned = sem("widest_ready"), sem("widest_turned")
            widest = local(own, "widest", [P, 1])
            keep_f = acc[:, 0:NT]
            dst_i, next_i, first_i, src_i = (acc[:, k * NT:(k + 1) * NT].bitcast(I32) for k in range(1, 5))
            flat_i = acc[:, 5 * NT:7 * NT].bitcast(I32).rearrange("p (k t) -> p k t", k=2)
            nxt = big[:, 0:NT]
            fst = big[:, NT:2 * NT]
            part_i = local(own, "part_i", [P, 1], I32)
            part = local(own, "part", [P, 1])
            part_lo = big[:, 6 * NT:7 * NT].bitcast(I32)
            cleared = sem("cleared")
            loaded = sem("loaded")
            made = sem("made")
            masks = sem("masks")
            dve_step = sem("dve_step")
            n_loads = [0]

            @block.sync
            def _(sp):
                sp.wait_ge(cleared, 1)

                def load(dst, src):
                    n_loads[0] += 1
                    sp.dma_start(dst, src).then_inc(loaded, 16)
                load(dst_i, A["dst_t"])
                load(next_i, A["next_t"])
                load(first_i, A["first"].partition_broadcast(P))
                load(src_i, A["src_t"][:, 0:NT])
                load(first[:], A["first"][None, :])
                load(x_nm[:, 0:NB - 2, :], A["x"][0:(NB - 2) * P, :].rearrange("(c p) f -> p c f", p=P))
                load(x_nm[:, NB - 2, :], A["x"][(NB - 2) * P:(NB - 1) * P, :])
                load(x_nm[0:TAIL, NB - 1, :], A["x"][(NB - 1) * P:N, :])
                load(wz[0:D, :], A["L0_gnn_W1"][0:D, :])
                load(wz[D:2 * D, :], A["L0_gnn_W1"][2 * D:3 * D, :])
                load(wb[:], A["L0_gnn_W1"][D:2 * D, :])
                load(w2x[0:64, :], A["L0_gnn_W2"])
                load(w2x[64:65, :], A["L0_gnn_b2"][None, :])
                load(w_l1[0:D, 0:D], A["L1_gnn_weight"])
                load(bias_l1[:], A["L1_gnn_bias"].partition_broadcast(P))
                for k in range(3):
                    load(m1w[k][0:64, :], A[f"L2_gnn_m1_w{k + 1}"])
                load(c_rows[:, 0, :], A["L2_gnn_m1_c2"][None, :])
                load(c_rows[:, 1, :], A["L2_gnn_m1_c3"][None, :])
                load(m2w[0][0:64, :], A["L2_gnn_m2_w1"][D:96, :])
                load(m2w[0][64:96, :], A["L2_gnn_m2_w1"][0:D, :])
                load(m2w[1][:], A["L2_gnn_m2_w2"])
                load(m2w[2][:, 0:D], A["L2_gnn_m2_w3"])
                load(w2r[0:64, :], A["L3_gnn_w2"])
                load(w2r[64:65, :], A["L3_gnn_b2"][None, :])

                def column(n, rows, name, lo=0, hi=None):
                    v = A[name]
                    hi = v.shape[-1] if hi is None else hi
                    v = v[0, :] if len(v.shape) == 2 else v
                    load(cols[rows:rows + hi - lo, n:n + 1], v[lo:hi].rearrange("(a b) -> a b", b=1))
                column(0, 0, "L0_gnn_b1")
                column(1, 0, "L3_gnn_w1")
                column(2, 0, "L3_gnn_b1")
                for k in range(3):
                    column(3 + 2 * k, 0, f"L2_gnn_m1_g{k + 1}")
                    column(4 + 2 * k, 0, f"L2_gnn_m1_b{k + 1}")
                column(9, 0, "L2_gnn_m1_c1")
                column(10, 0, "L2_gnn_m2_g1", D, 96)
                column(10, 64, "L2_gnn_m2_g1", 0, D)
                column(11, 0, "L2_gnn_m2_b1", D, 96)
                column(11, 64, "L2_gnn_m2_b1", 0, D)
                for k in (1, 2):
                    column(10 + 2 * k, 0, f"L2_gnn_m2_g{k + 1}")
                    column(11 + 2 * k, 0, f"L2_gnn_m2_b{k + 1}")
                for k in range(3):
                    column(16 + k, 0, f"L2_gnn_m2_c{k + 1}")
                sp.dma_start(flat_i[:, 0, :], A["dst_row"][1:EP + 1].rearrange("(p t) -> p t", p=P)).then_inc(keep_in, 16)
                sp.dma_start(flat_i[:, 1, :], A["dst_row"][0:EP].rearrange("(p t) -> p t", p=P)).then_inc(keep_in, 16)
                sp.wait_ge(loaded, 16 * n_loads[0])
                sp.wait_ge(keep_dram_ready, 1)
                sp.dma_start(keep_dram.rearrange("(p t) -> p t", p=P), keep_f).then_inc(keep_stored, 16)
                sp.wait_ge(keep_stored, 16)

            @block.tensor
            def _(pe):
                pe.wait_ge(widest_ready, 1)
                pe.transpose(ps[0][0:1, 0:P], widest[:], ident[:]).then_inc(widest_turned, 1)

            @block.gpsimd
            def _(pool):
                pool.iota(part_i[:], [[1, 1]], base=0, channel_multiplier=1).then_inc(made, 1)
                pool.iota(iota[:], [[1, P]], base=0, channel_multiplier=0,
                          allow_small_or_imprecise_dtypes=True).then_inc(made, 1)
                pool.memset(ident[:], 0.0).then_inc(masks, 1)
                pool.wait_ge(masks, 1)
                pool.affine_select(out=ident[:], in_=ident[:], compare_op=ALU.not_equal, fill=1.0, base=0,
                                   pattern=[[-1, P]], channel_multiplier=1).then_inc(made, 1)

            @block.vector
            def _(v):
                step = Chain(v, dve_step)
                for t in (cols, x_nm, w_l1, m2w[2]):
                    step(v.memset(t[:], 0.0))
                v.memset(w_l1[D:D + 1, D:D + 1], 1.0).then_inc(cleared, 1)
                v.wait_ge(loaded, 16 * n_loads[0])
                v.wait_ge(made, 3)
                step(v.tensor_copy(iota_b[:], iota[:]))
                step(v.tensor_reduce(fold4[:], ident[:].rearrange("p (q f) -> p f q", q=4), AX_X, ALU.add))
                step(v.tensor_reduce(fold_msg[:, 8:D], ident[:, 0:120].rearrange("p (q c) -> p c q", q=5), AX_X, ALU.add))
                step(v.tensor_copy(fold_msg[:, 0:8], ident[:, 120:P]))
                step(v.tensor_copy(part[:], part_i[:]))
                step(v.tensor_scalar(part_lo, src_i, P - 1, None, ALU.bitwise_and))
                step(v.tensor_scalar(src_i, src_i, 7, None, ALU.logical_shift_right))
                step(v.tensor_copy(src_lo, part_lo))
                step(v.tensor_copy(src_hi, src_i))
                dst = keep_f
                step(v.tensor_copy(dst, dst_i))
                step(v.tensor_copy(nxt, next_i))
                step(v.tensor_copy(fst, first_i))
                step(v.tensor_tensor(nxt, nxt, dst, ALU.not_equal))
                unit_first = fst.rearrange("p (n j) -> p n j", j=TJ)[:, :, 0]
                for k, f, shape in ((0, fst, [P, NT]), (1, unit_first.unsqueeze(2).broadcast_to([P, UNITS, TJ]),
                                                        [P, UNITS, TJ])):
                    def v3(t):
                        return t if k == 0 else t.rearrange("p (n j) -> p n j", j=TJ)
                    step(v.tensor_tensor(v3(dst_rel[k][:]), v3(dst), f, ALU.subtract))
                    step(v.scalar_tensor_tensor(out=dst_last[k][:], in0=dst_rel[k][:], scalar=1.0, in1=nxt,
                                                op0=ALU.add, op1=ALU.mult))
                    step(v.tensor_scalar(dst_last[k][:], dst_last[k][:], -1.0, None, ALU.add))
                step(v.tensor_scalar(node_of[0][:], fst, part[:], None, ALU.add))
                step(v.tensor_scalar(node_of[1][:], unit_first, part[:], -float(P - W), ALU.add, ALU.add))
                v.tensor_reduce(widest[:], dst_rel[1][:], AX_X, ALU.max).then_inc(widest_ready, 1)
                v.wait_ge(widest_turned, 1)
                step(v.tensor_reduce(part[0:1, :], ps[0][0:1, 0:P], AX_X, ALU.max))
                step(v.tensor_scalar(narrow_ok[:], part[0:1, :], float(W), None, ALU.is_lt))
                v.wait_ge(keep_in, 32)
                v.tensor_tensor(keep_f, flat_i[:, 0, :], flat_i[:, 1, :], ALU.is_equal).then_inc(keep_dram_ready, 1)
                w4 = [w2r[:, 64 * k:64 * (k + 1)].rearrange("p (u v) -> p u v", v=8) for k in range(3)]
                w5 = w2r[:, 192:384].rearrange("p (u v k) -> p u v k", v=8, k=3)
                abc = w2m[:].rearrange("p (b v u) -> p b u v", b=3, u=8)
                ab, c = abc[:, 0:2], abc[:, 2]
                q = float(np.sqrt(3.0 / 32.0))
                for dst, src, s in ((ab[:, 0, :, 0:8], w4[0], 0.25), (ab[:, 0, :, 8:16], w4[1], 0.25),
                                    (ab[:, 1, :, 0:8], w4[2], q),
                                    (ab[:, 1, :, 8:16], w5[:, :, :, 2], 0.375),
                                    (c[:, :, 0:8], w5[:, :, :, 0], float(1.0 / np.sqrt(32.0))),
                                    (c[:, :, 8:16], w5[:, :, :, 1], float(np.sqrt(3.0) / 8.0))):
                    step(v.tensor_scalar(dst, src, s, None, ALU.mult))
                step(v.scalar_tensor_tensor(out=c[:, :, 0:8], in0=ab[:, 1, :, 8:16], scalar=-1.0 / 3.0,
                                            in1=c[:, :, 0:8], op0=ALU.mult, op1=ALU.add))

        def clear_sum(rows):
            with nc.Block() as block:
                @block.vector
                def _(v):
                    v.memset(acc[0:rows, :], 0.0)

        def layernorm():
            d = big[:, 0:NB * D].rearrange("p (c f) -> p c f", f=D)
            sq = big[:, NB * D:2 * NB * D].rearrange("p (c f) -> p c f", f=D)
            r1 = big[:, 2 * NB * D:2 * NB * D + NB]
            r2 = big[:, 2 * NB * D + NB:2 * NB * D + 2 * NB]

            def spread(r):
                return r.unsqueeze(2).broadcast_to([P, NB, D])
            step_done, var_ready, std_ready = sem("ln_step"), sem("var_ready"), sem("std_ready")
            with nc.Block() as block:
                @block.vector
                def _(v):
                    step = Chain(v, step_done)
                    step(v.tensor_reduce(r1, x_nm[:], AX_X, ALU.add))
                    step(v.tensor_scalar(r1, r1, 1.0 / D, None, ALU.mult))
                    step(v.tensor_tensor(d, x_nm[:], spread(r1), ALU.subtract))
                    step(v.tensor_tensor(sq, d, d, ALU.mult))
                    step(v.tensor_reduce(r2, sq, AX_X, ALU.add))
                    v.tensor_scalar(r2, r2, 1.0 / D, EPS, ALU.mult, ALU.add).then_inc(var_ready, 1)
                    v.wait_ge(std_ready, 1)
                    step(v.reciprocal(r2, r1))
                    step(v.tensor_tensor(d, d, spread(r2), ALU.mult))
                    step(v.tensor_scalar(h_nm[:], d, 0.0, None, ALU.max))

                @block.scalar
                def _(a):
                    a.wait_ge(var_ready, 1)
                    a.activation(r1, r2, ACT.Sqrt).then_inc(std_ready, 1)

        def store_table(table, src_nm):
            stored = sem("table_stored")
            with nc.Block() as block:
                @block.sync
                def _(sp):
                    sp.dma_start(table[0:NP, :].rearrange("(c p) f -> p c f", p=P), src_nm).then_inc(stored, 16)
                    sp.wait_ge(stored, 16)

        def sum_to_nodes(rows, rhs, width, post):
            turned, used, step_done = sem("turned"), sem("turned_used"), sem("post_step")
            with nc.Block() as block:
                @block.tensor
                def _(pe):
                    for g in range(NB // GRP):
                        if g >= 2:
                            pe.wait_ge(used, g - 1)
                        for j in range(GRP):
                            c = g * GRP + j
                            last = pe.matmul(ps[g % 2][:, j * width:(j + 1) * width],
                                             acc[0:rows, c * P:(c + 1) * P], rhs, start=True, stop=True)
                        last.then_inc(turned, 1)

                @block.vector
                def _(v):
                    step = Chain(v, step_done)
                    for g in range(NB // GRP):
                        v.wait_ge(turned, g + 1)
                        post(v, ps[g % 2][:, 0:GRP * width].rearrange("p (c f) -> p c f", f=width),
                             g * GRP, step)
                        v.sem_inc(used, 1)

        def split(eng, program):
            ok = eng.value_load(narrow_ok[0:1, 0:1], min_val=0, max_val=1)
            with eng.If(ok):
                program(1)
            with eng.Else():
                program(0)

        def adds(narrow):
            return 1 if narrow else TJ

        def one_hots(v, ring, i, u, narrow, columns=None):
            columns = (columns or dst_rel)[narrow]
            t = (i * BU + u) * TJ
            if narrow:
                return v.tensor_tensor(ring[:, u % 2, :, 0:W], iota[:, 0:W].unsqueeze(1).broadcast_to([P, TJ, W]),
                                       columns[:, bass.ds(t, TJ)].unsqueeze(2).broadcast_to([P, TJ, W]), ALU.is_equal)
            for j in range(TJ):
                ins = v.tensor_scalar(ring[:, u % 2, j, :], iota[:], columns[:, bass.ds(t + j, 1)], None, ALU.is_equal)
            return ins

        def window_products(pe, bank, rows, parts, hot, narrow):
            for j in range(TJ):
                pieces = parts(j)
                for k, piece in enumerate(pieces):
                    o = bank[0:rows, 0:W] if narrow else bank[0:rows, j * P:(j + 1) * P]
                    last = pe.matmul(o, piece, hot[:, j, 0:W] if narrow else hot[:, j, :],
                                     start=(k == 0 and (j == 0 or not narrow)),
                                     stop=(k == len(pieces) - 1 and (j == TJ - 1 or not narrow)))
            return last

        def add_windows(v, bank, rows, i, u, added, narrow):
            for j in range(adds(narrow)):
                t = (i * BU + u) * TJ + j
                n0 = v.value_load(first[0:1, bass.ds(t, 1)], min_val=0, max_val=N)
                if not (isinstance(t, int) and t == 0):
                    v.wait_ge(added, i * BU + u if narrow else t)
                w = acc[0:rows, bass.ds(n0, W if narrow else P)]
                v.tensor_tensor(w, w, bank[0:rows, 0:W] if narrow else bank[0:rows, j * P:(j + 1) * P],
                                ALU.add).then_inc(added, 1)

        def gather_loop(pool, table, rows_of, idx, idx_in, gathered, rows_free):
            may_gather = sem("may_gather")

            def unit(i, u):
                if u % 2 == 0:
                    pool.wait_ge(idx_in[u // 2], 16 * (i + 1))
                wait_units(pool, rows_free, i, u, BU)
                pool.sem_inc(may_gather, 1)
                for j in range(TJ):
                    pool.indirect_dma_start(
                        out=rows_of(u, j), out_offset=None, in_=table,
                        in_offset=bass.IndirectOffsetOnAxis(ap=idx[:, u // 2, (u % 2) * TJ + j:(u % 2) * TJ + j + 1],
                                                            axis=0)).then_inc(gathered[u], 16)
            flow(pool, unit)

        def load_indices(sp, idx, idx_in, gathered, i, u):
            def load(half, tile):
                sp.dma_start(idx[:, half, :], A["src_t"][:, bass.ds(tile, 2 * TJ)]).then_inc(idx_in[half], 16)
            if u == 0:
                if isinstance(i, int) and i == 0:
                    load(0, 0)
                else:
                    for k in (2, 3):
                        sp.wait_ge(gathered[k], i * 16 * TJ)
                load(1, (i * BU + 2) * TJ)
            elif u == 2:
                for k in (0, 1):
                    sp.wait_ge(gathered[k], (i + 1) * 16 * TJ)
                load(0, (i * BU + 4) * TJ)

        def wait_spare_indices(sp, idx_in):
            sp.wait_ge(idx_in[0], 16 * (BODIES + 1))

        def wait_gathered(eng, gathered, i, u):
            eng.wait_ge(gathered[u], 16 * TJ * (i + 1))

        layernorm()
        store_table(h_table, h_nm[:])
        with ExitStack() as own:
            hT = local(own, "hT", [D, 2, 4 * P], F32)
            rows = local(own, "rows", [P, NB, 64], F32)
            turned, copied, prod, rows_out, stored = (sem("b_turned"), sem("b_copied"), sem("b_prod"),
                                                      sem("b_rows"), sem("b_stored"))
            NG = -(-NB // 4)
            with nc.Block() as block:
                @block.tensor
                def _(pe):
                    for g in range(NG):
                        n = min(4, NB - 4 * g)
                        if g >= 2:
                            pe.wait_ge(copied, g - 1)
                        for j in range(n):
                            last = pe.transpose(ps[g % 2][0:D, j * P:(j + 1) * P], h_nm[:, 4 * g + j, :], ident[:])
                        last.then_inc(turned, 1)
                        pe.wait_ge(copied, g + 1)
                        if g >= 2:
                            pe.wait_ge(rows_out, g - 1)
                        for j in range(n):
                            last = pe.matmul(ps[2 + g % 2][:, j * 64:(j + 1) * 64], hT[:, g % 2, j * P:(j + 1) * P],
                                             wb[:], start=True, stop=True)
                        last.then_inc(prod, 1)

                @block.scalar
                def _(a):
                    for g in range(NG):
                        n = min(4, NB - 4 * g)
                        a.wait_ge(turned, g + 1)
                        if g >= 2:
                            a.wait_ge(prod, g - 1)
                        a.copy(hT[:, g % 2, 0:n * P], ps[g % 2][0:D, 0:n * P]).then_inc(copied, 1)

                @block.vector
                def _(v):
                    for g in range(NG):
                        n = min(4, NB - 4 * g)
                        v.wait_ge(prod, g + 1)
                        v.tensor_copy(rows[:, 4 * g:4 * g + n, :],
                                      ps[2 + g % 2][:, 0:n * 64].rearrange("p (c f) -> p c f", f=64)).then_inc(rows_out, 1)

                @block.sync
                def _(sp):
                    sp.wait_ge(rows_out, NG)
                    sp.dma_start(b_table[0:NP, :].rearrange("(c p) f -> p c f", p=P), rows[:]).then_inc(stored, 16)
                    sp.dma_start(b_table[NP:NP + P, :], rows[:, 0, :]).then_inc(stored, 16)
                    sp.wait_ge(stored, 32)
        clear_sum(D)

        with ExitStack() as own:
            def ring(name, shape, dt=F32):
                return local(own, name, shape, dt)
            idx = ring("idx", [P, 2, 2 * TJ], I32)
            rows = ring("rows", [P, BU, TJ, D])
            feat = ring("feat", [P, 2, U])
            wzb = ring("wzb", [P, 2, 64])
            bwin = big[:, 0:2 * TJ * 64].rearrange("p (s j f) -> p s j f", s=2, j=TJ)
            ohT = big[:, 2 * TJ * 64:2 * TJ * 64 + 2 * U].rearrange("p (s e) -> p s e", s=2)
            ohl = ring("ohl", [P, 2, TJ, P])
            sh = ring("sh", [P, 2, TJ, P], BF16)
            sb_ = ring("sb_", [P, 2, TJ, NB], BF16)
            hid = ring("hid", [65, 2, U])
            dst_b = ring("dst_b", [P, 2, U], I32)
            keep = ring("keep", [D, 2, U])
            run = ring("run", [D, 2, U])
            runT = ring("runT", [P, 2, TJ, D])
            idx_in, ea_in, win_in, dst_in, keep_in = (sems("idx_in"), sems("ea_in"), sems("win_in"), sems("dst_in"),
                                                      sems("keep_in"))
            gathered = sems("gathered", BU)
            (turned, rows_copied, hots, z_done, hid_done, v_done, ran, run_turned, run_copied, last_hots, summed,
             added, set_up, src_hots, counted, pe_go) = [sem(s) for s in (
                 "turned", "rows_copied", "hots", "z_done", "hid_done", "v_done", "ran", "run_turned", "run_copied",
                 "last_hots", "summed", "added", "set_up", "src_hots", "counted", "pe_go")]

            with nc.Block() as block:
                @block.sync
                def _(sp):
                    def program(narrow):
                        lo = P - W if narrow else 0

                        def unit(i, u):
                            n = i * BU + u
                            load_indices(sp, idx, idx_in, gathered, i, u)
                            wait_units(sp, z_done, i, u, 2)
                            sp.dma_start(feat[D:2 * D, u % 2, :],
                                         A["eaT"][:, bass.ds(n * U, U)]).then_inc(ea_in[u % 2], 16)
                            for j in range(adds(narrow)):
                                n0 = sp.value_load(first[0:1, bass.ds(n * TJ + j, 1)], min_val=0, max_val=N)
                                if narrow:
                                    sp.dma_start(wzb[P - W:P, u % 2, :], b_table[bass.ds(n0, W), :]).then_inc(win_in[u % 2], 16)
                                else:
                                    sp.dma_start(bwin[:, u % 2, j, :], b_table[bass.ds(n0, P), :]).then_inc(win_in[u % 2], 16)
                            wait_units(sp, hots, i, u, 2)
                            sp.dma_start(dst_b[lo:P, u % 2, :],
                                         A["dst_row"][bass.ds(n * U + 1, U)].partition_broadcast(P - lo)).then_inc(dst_in[u % 2], 16)
                            wait_units(sp, ran, i, u, 2)
                            sp.dma_start(keep[:, u % 2, :],
                                         keep_dram[bass.ds(n * U, U)].partition_broadcast(D)).then_inc(keep_in[u % 2], 16)
                        flow(sp, unit)
                    split(sp, program)
                    wait_spare_indices(sp, idx_in)

                @block.gpsimd
                def _(pool):
                    gather_loop(pool, h_table, lambda u, j: rows[:, u, j, :], idx, idx_in, gathered, turned)

                @block.tensor
                def _(pe):
                    pe.wait_ge(set_up, 2)

                    def program(narrow):
                        def turn(i, u):
                            wait_gathered(pe, gathered, i, u)
                            wait_units(pe, rows_copied, i, u, 2)
                            for j in range(TJ):
                                last = pe.transpose(ps[u % 2][0:D, j * P:(j + 1) * P], rows[:, u, j, :], ident[:])
                            last.then_inc(turned, 1)

                        def hidden(i, u):
                            wait_units(pe, rows_copied, i, u)
                            wait_units(pe, hots, i, u)
                            wait_slot(pe, ea_in, i, u)
                            wait_units(pe, hid_done, i, u, 1)
                            wait_slot(pe, win_in, i, u, 16 * adds(narrow))
                            pe.sem_inc(pe_go, 1)
                            if narrow:
                                last = pe.matmul(ps[2][0:64, :], wzb[:, u % 2, :], feat[:, u % 2, :],
                                                 start=True, stop=True)
                            else:
                                pe.matmul(ps[2][0:64, :], wz[:], feat[0:64, u % 2, :], start=True, stop=False)
                                for j in range(TJ):
                                    last = pe.matmul(ps[2][0:64, j * P:(j + 1) * P], bwin[:, u % 2, j, :],
                                                     ohT[:, u % 2, j * P:(j + 1) * P], start=False, stop=(j == TJ - 1))
                            last.then_inc(z_done, 1)

                        def outputs(i, u):
                            wait_units(pe, hid_done, i, u)
                            wait_units(pe, ran, i, u, 1)
                            pe.matmul(ps[3][0:D, :], w2x[:], hid[:, u % 2, :], start=True, stop=True).then_inc(v_done, 1)

                        def turn_run(i, u):
                            wait_units(pe, ran, i, u)
                            wait_units(pe, run_copied, i, u, 1)
                            pe.sem_inc(pe_go, 1)
                            for j in range(TJ):
                                last = pe.transpose(ps[4][:, j * D:(j + 1) * D], run[:, u % 2, j * P:(j + 1) * P],
                                                    ident[0:D, 0:D])
                            last.then_inc(run_turned, 1)

                        def window_sums(i, u):
                            wait_units(pe, run_copied, i, u)
                            wait_units(pe, last_hots, i, u)
                            wait_units(pe, added, i, u, 1, adds(narrow))
                            window_products(pe, ps[5], D, lambda j: [runT[:, u % 2, j, :]], ohl[:, u % 2],
                                            narrow).then_inc(summed, 1)

                        def count(i, u):
                            wait_units(pe, src_hots, i, u)
                            static = isinstance(i, int)
                            for j in range(TJ):
                                last = pe.matmul(ps[6][:, 0:NB], sh[:, u % 2, j, :], sb_[:, u % 2, j, :],
                                                 start=(static and i == 0 and u == 0 and j == 0),
                                                 stop=(static and i == BODIES - 1 and u == BU - 1 and j == TJ - 1))
                            last.then_inc(counted, 1)
                        unit, drain = staged(((window_sums, 4), (turn_run, 3), (outputs, 2), (hidden, 1), (count, 1),
                                              (turn, 0)))
                        flow(pe, unit, tail=drain)
                    split(pe, program)

                @block.scalar
                def _(a):
                    def copies(i, u):
                        wait_units(a, turned, i, u)
                        wait_units(a, z_done, i, u, 2)
                        a.copy(feat[0:D, u % 2, :], ps[u % 2][0:D, :]).then_inc(rows_copied, 1)

                    def relu(i, u):
                        wait_units(a, z_done, i, u)
                        wait_units(a, v_done, i, u, 2)
                        a.activation(hid[0:64, u % 2, :], ps[2][0:64, :], ACT.Relu,
                                     bias=cols[0:64, 0:1]).then_inc(hid_done, 1)

                    def copy_run(i, u):
                        wait_units(a, run_turned, i, u)
                        wait_units(a, summed, i, u, 2)
                        a.copy(runT[:, u % 2].rearrange("p j f -> p (j f)"), ps[4][:, 0:TJ * D]).then_inc(run_copied, 1)
                    unit, drain = staged(((copy_run, 3), (relu, 1), (copies, 0)))
                    flow(a, unit, tail=drain)

                @block.vector
                def _(v):
                    v.memset(hid[64:65, :, :], 1.0).then_inc(set_up, 1)
                    v.tensor_copy(wzb[0:64, :, :], wz[:].unsqueeze(1).broadcast_to([64, 2, 64])).then_inc(set_up, 1)

                    def program(narrow):
                        def nodes_by_edge(i, u):
                            wait_units(v, z_done, i, u, 2)
                            wait_slot(v, dst_in, i, u)
                            n = i * BU + u
                            if narrow:
                                v.tensor_scalar(feat[P - W:P, u % 2, :], dst_b[P - W:P, u % 2, :],
                                                node_of[1][P - W:P, bass.ds(n, 1)], None, ALU.is_equal).then_inc(hots, 1)
                                return
                            for j in range(TJ):
                                c = slice(j * P, (j + 1) * P)
                                last = v.tensor_scalar(ohT[:, u % 2, c], dst_b[:, u % 2, c],
                                                       node_of[0][:, bass.ds(n * TJ + j, 1)], None, ALU.is_equal)
                            last.then_inc(hots, 1)

                        def scan(i, u):
                            wait_units(v, v_done, i, u)
                            wait_slot(v, keep_in, i, u)
                            wait_units(v, run_turned, i, u, 2)
                            wait_units(v, ran, i, u, 1)
                            start = isinstance(i, int) and i == 0 and u == 0
                            v.tensor_tensor_scan(run[:, u % 2, :], keep[:, u % 2, :], ps[3][0:D, :],
                                                 0.0 if start else run[:, (u + 1) % 2, U - 1:U],
                                                 ALU.mult, ALU.max).then_inc(ran, 1)

                        def last_edges(i, u):
                            wait_units(v, summed, i, u, 2)
                            one_hots(v, ohl, i, u, narrow, dst_last).then_inc(last_hots, 1)

                        def sources(i, u):
                            wait_units(v, counted, i, u, 2)
                            t = bass.ds((i * BU + u) * TJ, TJ)
                            for ring_, part, width in ((sh, src_lo, P), (sb_, src_hi, NB)):
                                last = v.tensor_tensor(ring_[:, u % 2],
                                                       iota_b[:, 0:width].unsqueeze(1).broadcast_to([P, TJ, width]),
                                                       part[:, t].unsqueeze(2).broadcast_to([P, TJ, width]), ALU.is_equal)
                            last.then_inc(src_hots, 1)

                        def add(i, u):
                            wait_units(v, summed, i, u)
                            add_windows(v, ps[5], D, i, u, added, narrow)
                        unit, drain = staged(((last_edges, 3), (scan, 2), (add, 4), (nodes_by_edge, 0), (sources, 0)))
                        flow(v, unit, tail=drain)
                    split(v, program)
                    v.wait_ge(counted, UNITS)
                    v.tensor_copy(deg_out[:], ps[6][:, 0:NB])

        def l0_out(v, view, c0, step):
            xs, hs = x_nm[:, c0:c0 + GRP, :], h_nm[:, c0:c0 + GRP, :]
            step(v.tensor_tensor(hs, view, hs, ALU.max))
            step(v.tensor_tensor(xs, xs, hs, ALU.add))
        sum_to_nodes(D, ident[0:D, 0:D], D, l0_out)

        layernorm()
        with ExitStack() as own:
            rows = local(own, "scaled", [P, NB, D + 1])
            inv, root = local(own, "inv", [P, NB]), local(own, "root", [P, NB])
            step_done, clamped, rooted, ready, stored = (sem("scale_step"), sem("clamped"), sem("rooted"),
                                                         sem("scaled_ready"), sem("scaled_stored"))
            with nc.Block() as block:
                @block.vector
                def _(v):
                    step = Chain(v, step_done)
                    v.tensor_scalar(inv[:], deg_out[:], 1.0, None, ALU.max).then_inc(clamped, 1)
                    step(v.memset(rows[:], 1.0))
                    v.wait_ge(rooted, 1)
                    step(v.reciprocal(inv[:], root[:]))
                    v.tensor_tensor(rows[:, :, 0:D], h_nm[:], inv[:].unsqueeze(2).broadcast_to([P, NB, D]),
                                    ALU.mult).then_inc(ready, 1)
                    v.memset(acc[0:D + 1, :], 0.0)

                @block.scalar
                def _(a):
                    a.wait_ge(clamped, 1)
                    a.activation(root[:], inv[:], ACT.Sqrt).then_inc(rooted, 1)

                @block.sync
                def _(sp):
                    sp.wait_ge(ready, 1)
                    sp.dma_start(h1_table.rearrange("(c p) f -> p c f", p=P), rows[:]).then_inc(stored, 16)
                    sp.wait_ge(stored, 16)

        with ExitStack() as own:
            idx = local(own, "idx", [P, 2, 2 * TJ], I32)
            rows = local(own, "rows", [P, BU, TJ, D + 1])
            oh = local(own, "oh", [P, 2, TJ, P])
            idx_in, gathered = sems("idx_in"), sems("gathered", BU)
            hots, summed, added = sem("hots"), sem("summed"), sem("added")
            with nc.Block() as block:
                @block.sync
                def _(sp):
                    def unit(i, u):
                        load_indices(sp, idx, idx_in, gathered, i, u)
                    flow(sp, unit)
                    wait_spare_indices(sp, idx_in)

                @block.gpsimd
                def _(pool):
                    gather_loop(pool, h1_table, lambda u, j: rows[:, u, j, :], idx, idx_in, gathered, summed)

                @block.tensor
                def _(pe):
                    def program(narrow):
                        def unit(i, u):
                            wait_units(pe, added, i, u, 2, adds(narrow))
                            wait_units(pe, hots, i, u)
                            wait_gathered(pe, gathered, i, u)
                            window_products(pe, ps[u % 2], D + 1, lambda j: [rows[:, u, j, :]], oh[:, u % 2],
                                            narrow).then_inc(summed, 1)
                        flow(pe, unit)
                    split(pe, program)

                @block.vector
                def _(v):
                    def program(narrow):
                        def hot(i, u):
                            wait_units(v, summed, i, u, 2)
                            one_hots(v, oh, i, u, narrow).then_inc(hots, 1)

                        def add(i, u):
                            wait_units(v, summed, i, u)
                            add_windows(v, ps[u % 2], D + 1, i, u, added, narrow)
                        unit, drain = staged(((hot, 0), (add, 1)))
                        flow(v, unit, tail=drain)
                    split(v, program)

        with ExitStack() as own:
            nodes = big[:, 0:NB * (D + 1)].rearrange("p (c f) -> p c f", f=D + 1)
            inv, root = local(own, "inv", [P, NB]), local(own, "root", [P, NB])

            def l1_out(v, view, c0, step):
                step(v.tensor_copy(nodes[:, c0:c0 + GRP, :], view))
            sum_to_nodes(D + 1, w_l1[:], D + 1, l1_out)
            step_done, clamped, rooted = sem("norm_step"), sem("clamped"), sem("rooted")
            with nc.Block() as block:
                @block.vector
                def _(v):
                    step = Chain(v, step_done)
                    out_l1 = nodes[:, :, 0:D]
                    v.tensor_scalar(inv[:], nodes[:, :, D], 1.0, None, ALU.max).then_inc(clamped, 1)
                    step(v.tensor_copy(acc[64:65, :], acc[D:D + 1, :]))
                    v.wait_ge(rooted, 1)
                    step(v.reciprocal(inv[:], root[:]))
                    step(v.tensor_tensor(out_l1, out_l1, inv[:].unsqueeze(2).broadcast_to([P, NB, D]), ALU.mult))
                    step(v.tensor_tensor(out_l1, out_l1, bias_l1[:].unsqueeze(1).broadcast_to([P, NB, D]), ALU.add))
                    step(v.scalar_tensor_tensor(out=x_nm[:], in0=out_l1, scalar=0.0, in1=x_nm[:],
                                                op0=ALU.max, op1=ALU.add))

                @block.scalar
                def _(a):
                    a.wait_ge(clamped, 1)
                    a.activation(root[:], inv[:], ACT.Sqrt).then_inc(rooted, 1)

        recycle()

        layernorm()
        store_table(h_table, h_nm[:])
        def lrelu(v, dst, src):
            return v.scalar_tensor_tensor(out=dst, in0=src, scalar=0.1, in1=src, op0=ALU.mult, op1=ALU.max)

        MEAN, VAR, TMP, SCALE, SHIFT = 19, 20, 21, 22, 23

        def fold(rows, width, w, gain, bias, col, row=None):
            step_done, var_ready, rooted, shifted, const = (sem("fold_step"), sem("var_ready"), sem("rooted"),
                                                            sem("shifted"), sem("const"))

            def c(n):
                return cols[0:rows, n:n + 1]
            with nc.Block() as block:
                @block.vector
                def _(v):
                    step = Chain(v, step_done)
                    v.tensor_scalar(c(TMP), c(VAR), EPS, None, ALU.add).then_inc(var_ready, 1)
                    v.wait_ge(rooted, 1)
                    step(v.reciprocal(c(TMP), c(SCALE)))
                    step(v.tensor_tensor(c(SCALE), c(TMP), c(gain), ALU.mult))
                    step(v.tensor_tensor(c(TMP), c(MEAN), c(SCALE), ALU.mult))
                    v.tensor_tensor(c(SHIFT), c(bias), c(TMP), ALU.subtract).then_inc(shifted, 1)
                    v.wait_ge(const, 1)
                    step(v.tensor_scalar(w, w, c(SCALE), None, ALU.mult))
                    if row is None:
                        step(v.tensor_tensor(cols[0:width, col:col + 1], ps[7][0:width, 0:1],
                                             cols[0:width, col:col + 1], ALU.add))
                    else:
                        step(v.tensor_tensor(row, ps[7][0:1, 0:width], col, ALU.add))

                @block.scalar
                def _(a):
                    a.wait_ge(var_ready, 1)
                    a.activation(c(SCALE), c(TMP), ACT.Sqrt).then_inc(rooted, 1)

                @block.tensor
                def _(pe):
                    pe.wait_ge(shifted, 1)
                    if row is None:
                        pe.matmul(ps[7][0:width, 0:1], w, c(SHIFT), start=True, stop=True).then_inc(const, 1)
                    else:
                        pe.matmul(ps[7][0:1, 0:width], c(SHIFT), w, start=True, stop=True).then_inc(const, 1)

        with ExitStack() as own:
            ea = local(own, "ea", [P, 2, QK * QC])
            st = local(own, "st", [P, QN * QK, 6])
            two = local(own, "two", [P, 2])
            sq = big[:, 0:NB * D].rearrange("p (c f) -> p c f", f=D)
            ea_in = sems("ea_in")
            stats, squared, weighed, ready, joined, step_done = (sem("stats"), sem("squared"), sem("weighed"),
                                                                 sem("ea_ready"), sem("joined"), sem("bn_step"))
            with nc.Block() as block:
                @block.sync
                def _(sp):
                    def chunk(c, k, free):
                        if free is not None:
                            sp.wait_ge(stats, free)
                        for q in range(4):
                            sp.dma_start(ea[q * D:(q + 1) * D, k, :],
                                         A["eaT"][:, bass.ds(q * (E // 4) + c * (QK * QC), QK * QC)]).then_inc(ea_in[k], 16)
                    for c in (0, 1):
                        chunk(c, c, None)
                    with sp.Fori(1, QN // 2) as g:
                        for k in range(2):
                            chunk(g * 2 + k, k, g * 2 + k - 1)
                    chunk(QN - 1, 0, QN - 2)

                @block.vector
                def _(v):
                    step = Chain(v, step_done)
                    v.tensor_tensor(sq, h_nm[:], h_nm[:], ALU.mult).then_inc(squared, 1)

                    def chunk(g, k):
                        v.wait_ge(ea_in[k], (g + 1) * 64)
                        for b in range(QK):
                            last = v.bn_stats(st[:, bass.ds((g * 2 + k) * QK + b, 1), :].rearrange("p a s -> p (a s)"),
                                              ea[:, k, b * QC:(b + 1) * QC])
                        last.then_inc(stats, 1)
                    with v.Fori(0, QN // 2) as g:
                        for k in range(2):
                            chunk(g, k)
                    chunk(QN // 2, 0)
                    v.wait_ge(stats, QN)
                    step(v.bn_aggr(two[:], st[:].rearrange("p a s -> p (a s)")))
                    step(v.scalar_tensor_tensor(out=two[:, 1:2], in0=two[:, 0:1], scalar=two[:, 0:1],
                                                in1=two[:, 1:2], op0=ALU.mult, op1=ALU.add))
                    v.tensor_scalar(two[:], two[:], 0.25, None, ALU.mult).then_inc(ready, 1)
                    v.wait_ge(joined, 1)
                    v.wait_ge(weighed, 1)
                    for k in range(2):
                        step(v.tensor_scalar(cols[0:D, MEAN + k:MEAN + k + 1], ps[k][0:D, 0:1], 1.0 / E, None, ALU.mult))
                    step(v.tensor_copy(cols[D:2 * D, MEAN:MEAN + 2], ps[2][0:D, 0:2]))
                    m, s, t = (cols[0:64, n:n + 1] for n in (MEAN, VAR, TMP))
                    step(v.tensor_tensor(t, m, m, ALU.mult))
                    step(v.tensor_tensor(s, s, t, ALU.subtract))

                @block.tensor
                def _(pe):
                    pe.wait_ge(squared, 1)
                    for c in range(NB):
                        k = P if c < NB - 1 else TAIL
                        for b, src in enumerate((h_nm, sq)):
                            last = pe.matmul(ps[b][0:D, 0:1], src[0:k, c, :], deg_out[0:k, c:c + 1],
                                             start=(c == 0), stop=(c == NB - 1))
                    last.then_inc(weighed, 1)
                    pe.wait_ge(ready, 1)
                    pe.matmul(ps[2][0:D, 0:2], fold4[:], two[:], start=True, stop=True).then_inc(joined, 1)
        fold(64, 64, m1w[0][0:64, :], 3, 4, 9)

        with ExitStack() as own:
            idx = local(own, "idx", [P, 2, 2 * TJ], I32)
            rows = local(own, "rows", [P, BU, TJ, D])
            feat = local(own, "feat", [64, 2, U])
            zc = local(own, "zc", [64, 2, U])
            z1 = local(own, "z1", [64, BU, U])
            st = local(own, "st", [64, UNITS, 6])
            idx_in, ea_in, gathered, stored = sems("idx_in"), sems("ea_in"), sems("gathered", BU), sems("stored", BU)
            turned, copied, z_done, z_copied, z1_done, stats, pe_go = [sem(s) for s in (
                "turned", "copied", "z_done", "z_copied", "z1_done", "stats", "pe_go")]
            with nc.Block() as block:
                @block.sync
                def _(sp):
                    def store(i, u):
                        wait_units(sp, z1_done, i, u)
                        sp.dma_start(z1_dram[:, bass.ds((i * BU + u) * U, U)], z1[:, u, :]).then_inc(stored[u], 16)

                    def unit(i, u):
                        load_indices(sp, idx, idx_in, gathered, i, u)
                        wait_units(sp, z_done, i, u, 2)
                        sp.dma_start(feat[D:2 * D, u % 2, :],
                                     A["eaT"][:, bass.ds((i * BU + u) * U, U)]).then_inc(ea_in[u % 2], 16)
                        if before(i, u, 2) is not None:
                            store(*before(i, u, 2))

                    def drain(i, u):
                        if u < 2:
                            store(*before(i, u, 2))
                    flow(sp, unit, tail=drain)
                    wait_spare_indices(sp, idx_in)
                    for u in range(BU):
                        sp.wait_ge(stored[u], 16 * BODIES)

                @block.gpsimd
                def _(pool):
                    gather_loop(pool, h_table, lambda u, j: rows[:, u, j, :], idx, idx_in, gathered, turned)

                @block.tensor
                def _(pe):
                    def product(i, u):
                        wait_units(pe, copied, i, u)
                        wait_units(pe, z_copied, i, u, 2)
                        wait_slot(pe, ea_in, i, u)
                        pe.sem_inc(pe_go, 1)
                        pe.matmul(ps[2 + u % 2][0:64, :], m1w[0][0:64, :], feat[:, u % 2, :],
                                  start=True, stop=True).then_inc(z_done, 1)

                    def turn(i, u):
                        wait_units(pe, copied, i, u, 2)
                        wait_gathered(pe, gathered, i, u)
                        for j in range(TJ):
                            last = pe.transpose(ps[u % 2][0:D, j * P:(j + 1) * P], rows[:, u, j, :], ident[:])
                        last.then_inc(turned, 1)
                    unit, drain = staged(((product, 1), (turn, 0)))
                    flow(pe, unit, tail=drain)

                @block.scalar
                def _(a):
                    def add_const(i, u):
                        wait_units(a, z_done, i, u)
                        wait_units(a, z1_done, i, u, 2)
                        a.activation(zc[:, u % 2, :], ps[2 + u % 2][0:64, :], ACT.Identity,
                                     bias=cols[0:64, 9:10]).then_inc(z_copied, 1)

                    def copy(i, u):
                        wait_units(a, z_done, i, u, 2)
                        wait_units(a, turned, i, u)
                        a.copy(feat[0:D, u % 2, :], ps[u % 2][0:D, :]).then_inc(copied, 1)
                    unit, drain = staged(((add_const, 1), (copy, 0)))
                    flow(a, unit, tail=drain)

                @block.vector
                def _(v):
                    def unit(i, u, n=U):
                        if not (isinstance(i, int) and i == 0):
                            v.wait_ge(stored[u], i * 16)
                            v.wait_ge(stats, (i - 1) * BU + u + 1)
                        wait_units(v, z_copied, i, u)
                        lrelu(v, z1[:, u, :], zc[:, u % 2, :]).then_inc(z1_done, 1)
                        wait_units(v, z1_done, i, u)
                        v.bn_stats(st[:, bass.ds(i * BU + u, 1), :].rearrange("p a s -> p (a s)"),
                                   z1[:, u, 0:n]).then_inc(stats, 1)
                    flow(v, unit, last=lambda i, u: unit(i, u, U if u < BU - 1 else LAST))
                    v.wait_ge(stats, UNITS)
                    v.bn_aggr(cols[0:64, MEAN:MEAN + 2], st[:].rearrange("p a s -> p (a s)"))
        fold(64, 64, m1w[1][0:64, :], 5, 6, c_rows[:, 0, :], m1w[1][64:65, :])
        clear_sum(64)

        sq_sum = big[:, 0:2 * TJ * 64]
        with ExitStack() as own:
            z1 = local(own, "z1", [P, 2, U])
            w2d = local(own, "w2d", [P, P])
            ones = local(own, "ones", [65, P])
            c2 = local(own, "c2", [P, 64])
            zc = local(own, "zc", [P, 2, TJ, 2, 64])
            z2 = local(own, "z2", [P, 2, TJ, 2, 64])
            z2_sq = local(own, "z2_sq", [P, 2 * TJ * 64])
            oh = local(own, "oh", [P, 2, 2 * TJ, P])
            z1_in = sems("z1_in")
            (hots, z_done, z_copied, z2_done, squared, sq_added, summed, added, set_up, c2_spread,
             sq_cleared) = [sem(s) for s in (
                 "hots", "z_done", "z_copied", "z2_done", "squared", "sq_added", "summed", "added", "set_up",
                 "c2_spread", "sq_cleared")]
            with nc.Block() as block:
                @block.sync
                def _(sp):
                    def pair(i, k):
                        wait_pairs(sp, z_done, i, k, 2)
                        for h in range(2):
                            sp.dma_start(z1[h * 64:h * 64 + 64, k, :],
                                         z1_dram[:, bass.ds((i * BU + 2 * k + h) * U, U)]).then_inc(z1_in[k], 16)
                    flow(sp, pair, bu=BU // 2)

                @block.tensor
                def _(pe):
                    pe.wait_ge(set_up, 1)
                    pe.matmul(ps[6][:, 0:64], ones[64:65, :], m1w[1][64:65, :], start=True, stop=True).then_inc(c2_spread, 1)

                    def program(narrow):
                        def sums(i, k):
                            wait_pairs(pe, z2_done, i, k)
                            wait_pairs(pe, hots, i, k)
                            wait_pairs(pe, added, i, k, 2, 2 * adds(narrow))
                            for h in range(2):
                                window_products(pe, ps[2 + 2 * k + h], 64, lambda j: [z2[:, k, j, h, :]],
                                                oh[:, k, h * TJ:(h + 1) * TJ], narrow).then_inc(summed, 1)

                        def second(i, k):
                            wait_pairs(pe, z_copied, i, k, 2)
                            pe.wait_ge(z1_in[k], (i + 1) * 32)
                            for j in range(TJ):
                                last = pe.matmul(ps[k][:, j * P:(j + 1) * P], z1[:, k, j * P:(j + 1) * P],
                                                 w2d[:], start=True, stop=True)
                            last.then_inc(z_done, 1)
                        pair, drain = staged(((second, 0), (sums, 1)), bu=BU // 2)
                        flow(pe, pair, tail=drain, bu=BU // 2)
                    split(pe, program)

                @block.gpsimd
                def _(pool):
                    pool.memset(sq_sum, 0.0).then_inc(sq_cleared, 1)
                    pool.wait_ge(sq_cleared, 1)

                    def square(i, k, last_pair=False):
                        wait_pairs(pool, z2_done, i, k)
                        wait_pairs(pool, sq_added, i, k, 1)
                        z = z2[:, k].rearrange("p j h f -> p (j h f)")
                        pool.tensor_tensor(z2_sq[:], z, z, ALU.mult).then_inc(squared, 1)
                        wait_pairs(pool, squared, i, k)
                        if not last_pair:
                            pool.tensor_tensor(sq_sum, sq_sum, z2_sq[:], ALU.add).then_inc(sq_added, 1)
                            return
                        view = [t.rearrange("p (j h f) -> p j h f", j=TJ, h=2) for t in (sq_sum, z2_sq[:])]
                        pool.tensor_tensor(view[0][:, :, 0, :], view[0][:, :, 0, :], view[1][:, :, 0, :], ALU.add)
                        pool.tensor_tensor(view[0][0:LAST, 0, 1, :], view[0][0:LAST, 0, 1, :],
                                           view[1][0:LAST, 0, 1, :], ALU.add).then_inc(sq_added, 1)
                    flow(pool, square, last=lambda i, k: square(i, k, last_pair=(k == 1)), bu=BU // 2)

                @block.vector
                def _(v):
                    step = Chain(v, sem("set_up_step"))
                    step(v.memset(w2d[:], 0.0))
                    step(v.tensor_copy(w2d[0:64, 0:64], m1w[1][0:64, :]))
                    step(v.tensor_copy(w2d[64:P, 64:P], m1w[1][0:64, :]))
                    v.memset(ones[:], 1.0).then_inc(set_up, 1)
                    v.wait_ge(c2_spread, 1)
                    step(v.tensor_copy(c2[:], ps[6][:, 0:64]))

                    def program(narrow):
                        def add_const(i, k):
                            wait_pairs(v, z_done, i, k)
                            wait_pairs(v, z2_done, i, k, 2)
                            v.tensor_tensor(zc[:, k].rearrange("p j h f -> p (j h) f"),
                                            ps[k][:, :].rearrange("p (a f) -> p a f", f=64),
                                            c2[:].unsqueeze(1).broadcast_to([P, 2 * TJ, 64]), ALU.add).then_inc(z_copied, 1)

                        def hot(i, k):
                            wait_pairs(v, summed, i, k, 2, 2)
                            t = (i * BU + 2 * k) * TJ
                            if narrow:
                                v.tensor_tensor(oh[:, k, :, 0:W], iota[:, 0:W].unsqueeze(1).broadcast_to([P, 2 * TJ, W]),
                                                dst_rel[1][:, bass.ds(t, 2 * TJ)].unsqueeze(2).broadcast_to([P, 2 * TJ, W]),
                                                ALU.is_equal).then_inc(hots, 1)
                                return
                            for j in range(2 * TJ):
                                last = v.tensor_scalar(oh[:, k, j, :], iota[:], dst_rel[0][:, bass.ds(t + j, 1)], None,
                                                       ALU.is_equal)
                            last.then_inc(hots, 1)

                        def positive(i, k):
                            wait_pairs(v, z_copied, i, k)
                            wait_pairs(v, summed, i, k, 2, 2)
                            wait_pairs(v, squared, i, k, 2)
                            lrelu(v, z2[:, k].rearrange("p j h f -> p (j h f)"),
                                  zc[:, k].rearrange("p j h f -> p (j h f)")).then_inc(z2_done, 1)

                        def add(i, k):
                            for h in range(2):
                                v.wait_ge(summed, i * BU + 2 * k + h + 1)
                                add_windows(v, ps[2 + 2 * k + h], 64, i, 2 * k + h, added, narrow)
                        pair, drain = staged(((add_const, 0), (hot, 0), (positive, 0), (add, 1)), bu=BU // 2)
                        flow(v, pair, tail=drain, bu=BU // 2)
                    split(v, program)

        with ExitStack() as own:
            by_feature = local(own, "by_feature", [P, 64])
            column = local(own, "column", [P, 1])
            step_done, folded, joined = sem("bn_step"), sem("squares_folded"), sem("squares_joined")
            with nc.Block() as block:
                @block.tensor
                def _(pe):
                    pe.wait_ge(folded, 1)
                    pe.matmul(ps[6][0:64, 0:1], by_feature[:], column[:], start=True, stop=True).then_inc(joined, 1)

                @block.vector
                def _(v):
                    step = Chain(v, step_done)
                    m, s, t = (cols[0:64, n:n + 1] for n in (MEAN, VAR, TMP))
                    step(v.memset(column[:], 1.0))
                    v.tensor_reduce(by_feature[:], sq_sum.rearrange("p (a f) -> p f a", f=64), AX_X, ALU.add).then_inc(folded, 1)
                    step(v.tensor_reduce(m, acc[0:64, 0:N], AX_X, ALU.add))
                    step(v.tensor_scalar(m, m, 1.0 / E, None, ALU.mult))
                    v.wait_ge(joined, 1)
                    step(v.tensor_copy(s, ps[6][0:64, 0:1]))
                    step(v.tensor_tensor(t, m, m, ALU.mult))
                    step(v.scalar_tensor_tensor(out=s, in0=s, scalar=1.0 / E, in1=t, op0=ALU.mult, op1=ALU.subtract))
        fold(64, 64, m1w[2][0:64, :], 7, 8, c_rows[:, 1, :], m1w[2][64:65, :])

        recycle()

        turned, copied, prod, prod_copied = sem("n_turned"), sem("n_copied"), sem("n_prod"), sem("n_prod_copied")
        NG = -(-NB // 4)
        with nc.Block() as block:
            @block.tensor
            def _(pe):
                for g in range(NG):
                    if g >= 2:
                        pe.wait_ge(copied, g - 1)
                    for j in range(min(4, NB - 4 * g)):
                        last = pe.transpose(ps[g % 2][0:D, j * P:(j + 1) * P], h_nm[:, 4 * g + j, :], ident[:])
                    last.then_inc(turned, 1)
                for g in range(NCH):
                    if g >= 2:
                        pe.wait_ge(prod_copied, g - 1)
                    pe.matmul(ps[2 + g % 2][0:64, 0:CH], m1w[2][:], acc[0:65, g * CH:(g + 1) * CH],
                              start=True, stop=True).then_inc(prod, 1)

            @block.scalar
            def _(a):
                for g in range(NG):
                    n = min(4, NB - 4 * g) * P
                    a.wait_ge(turned, g + 1)
                    a.copy(big[64:96, g * 4 * P:g * 4 * P + n], ps[g % 2][0:D, 0:n]).then_inc(copied, 1)

            @block.vector
            def _(v):
                for g in range(NCH):
                    v.wait_ge(prod, g + 1)
                    v.tensor_copy(big[0:64, g * CH:(g + 1) * CH], ps[2 + g % 2][0:64, 0:CH]).then_inc(prod_copied, 1)

        with ExitStack() as own:
            st = local(own, "st", [96, NCH, 6])
            for k in range(3):
                width = 96 if k < 2 else D
                stats = sem("node_stats")
                with nc.Block() as block:
                    @block.vector
                    def _(v):
                        for g in range(NCH):
                            v.bn_stats(st[:, g, :], big[0:96, g * CH:(g + 1) * CH]).then_inc(stats, 1)
                        v.wait_ge(stats, NCH)
                        v.bn_aggr(cols[0:96, MEAN:MEAN + 2], st[:].rearrange("p a s -> p (a s)"))
                w = m2w[k][:, 0:width]
                fold(96, width, w, 10 + 2 * k, 11 + 2 * k, 16 + k)
                prod, used, shifted = sem("node_prod"), sem("node_used"), sem("node_shifted")
                zc = local(own, "zc", [96, 2, CH])
                with nc.Block() as block:
                    @block.tensor
                    def _(pe):
                        for g in range(NCH):
                            if g >= 4:
                                pe.wait_ge(used, g - 3)
                            pe.matmul(ps[g % 4][0:width, 0:CH], w, big[0:96, g * CH:(g + 1) * CH],
                                      start=True, stop=True).then_inc(prod, 1)

                    @block.scalar
                    def _(a):
                        for g in range(NCH):
                            a.wait_ge(prod, g + 1)
                            if k < 2 and g >= 2:
                                a.wait_ge(shifted, g - 1)
                            dst = zc[:, g % 2, :] if k < 2 else acc[0:D, g * CH:(g + 1) * CH]
                            a.activation(dst, ps[g % 4][0:width, 0:CH], ACT.Identity,
                                         bias=cols[0:width, 16 + k:17 + k]).then_inc(used, 1)

                    @block.vector
                    def _(v):
                        for g in range(NCH if k < 2 else 0):
                            v.wait_ge(used, g + 1)
                            lrelu(v, big[0:96, g * CH:(g + 1) * CH], zc[:, g % 2, :]).then_inc(shifted, 1)

        def add_to_x(v, view, c0, step):
            xs = x_nm[:, c0:c0 + GRP, :]
            step(v.tensor_tensor(xs, xs, view, ALU.add))
        sum_to_nodes(D, ident[0:D, 0:D], D, add_to_x)

        recycle()

        layernorm()
        store_table(h_table, h_nm[:])
        r5 = big[:, 0:NT * 5].rearrange("p (t k) -> p t k", k=5)
        with ExitStack() as own:
            rel = local(own, "rel", [P, NT, 3])
            n2, root = acc[:, 0:NT], acc[:, NT:2 * NT]
            sq = acc[:, 2 * NT:5 * NT].rearrange("p (t k) -> p t k", k=3)
            loaded, step_done, summed, rooted = sem("rel_loaded"), sem("rel_step"), sem("rel_summed"), sem("rel_rooted")
            with nc.Block() as block:
                @block.sync
                def _(sp):
                    sp.dma_start(rel[:], A["rel_t"]).then_inc(loaded, 16)
                    sp.wait_ge(loaded, 16)

                @block.vector
                def _(v):
                    step = Chain(v, step_done)
                    v.wait_ge(loaded, 16)
                    step(v.tensor_tensor(sq, rel[:], rel[:], ALU.mult))
                    v.tensor_reduce(n2, sq, AX_X, ALU.add).then_inc(summed, 1)
                    v.wait_ge(rooted, 1)
                    step(v.reciprocal(n2, root))
                    for k in range(5):
                        step(v.tensor_tensor(r5[:, :, k], rel[:, :, (k + 1) % 3], n2, ALU.mult))
                    step(v.memset(acc[:], 0.0))

                @block.scalar
                def _(a):
                    a.wait_ge(summed, 1)
                    a.activation(root, n2, ACT.Sqrt).then_inc(rooted, 1)

        with ExitStack() as own:
            idx = local(own, "idx", [P, 2, 2 * TJ], I32)
            rows = local(own, "rows", [P, BU, TJ, D])
            dist = local(own, "dist", [64, 2, U])
            hid = local(own, "hid", [65, 2, U])
            oh = big[:, 5 * NT:5 * NT + 2 * TJ * P].rearrange("p (s j n) -> p s j n", s=2, j=TJ)
            r = local(own, "r", [P, BU, TJ, 5])
            f_d = local(own, "f_d", [P, 2, TJ, 16])
            f_x = local(own, "f_x", [P, 2, TJ, 16, 3])
            f_5 = local(own, "f_5", [P, 2, TJ, 8, 5])
            t1 = local(own, "t1", [P, TJ, 8, 3])
            t2 = local(own, "t2", [P, TJ, 8, 3])
            t3 = local(own, "t3", [P, TJ, 8, 3])
            ab_prod = local(own, "ab_prod", [P, TJ, 2, 16, 8])
            c_prod = local(own, "c_prod", [P, TJ, 16, 24])
            c_half = local(own, "c_half", [P, TJ, 8, 24])
            msg = local(own, "msg", [P, 2, TJ, P + 8])
            idx_in, dist_in, gathered = sems("idx_in"), sems("dist_in"), sems("gathered", BU)
            (spread, hid_done, r_done, x_step, x_done, dot_step, dot_done, hots, prods, halved, ab_summed, c_summed,
             msg_done, summed, added, set_up, may_gather) = [sem(s) for s in (
                 "spread", "hid_done", "r_done", "x_step", "x_done", "dot_step", "dot_done", "hots", "prods", "halved",
                 "ab_summed", "c_summed", "msg_done", "summed", "added", "set_up", "may_gather")]
            with nc.Block() as block:
                @block.sync
                def _(sp):
                    def unit(i, u):
                        load_indices(sp, idx, idx_in, gathered, i, u)
                        wait_units(sp, hid_done, i, u, 2)
                        sp.dma_start(dist[:, u % 2, :],
                                     A["dist"][bass.ds((i * BU + u) * U, U)].partition_broadcast(64)).then_inc(dist_in[u % 2], 16)
                    flow(sp, unit)
                    wait_spare_indices(sp, idx_in)

                def by_r(lo, u):
                    return r[:, u, :, lo:lo + 3].unsqueeze(2).broadcast_to([P, TJ, 8, 3])

                @block.gpsimd
                def _(pool):
                    def gather(i, u):
                        if u % 2 == 0:
                            pool.wait_ge(idx_in[u // 2], 16 * (i + 1))
                        wait_units(pool, spread, i, u, BU)
                        pool.sem_inc(may_gather, 1)
                        for j in range(TJ):
                            pool.indirect_dma_start(
                                out=rows[:, u, j, :], out_offset=None, in_=h_table,
                                in_offset=bass.IndirectOffsetOnAxis(
                                    ap=idx[:, u // 2, (u % 2) * TJ + j:(u % 2) * TJ + j + 1], axis=0)).then_inc(gathered[u], 16)

                    def cross(i, u):
                        wait_units(pool, spread, i, u)
                        wait_units(pool, prods, i, u, 2, TJ)
                        wait_units(pool, x_done, i, u, 1)
                        pool.tensor_tensor(t1[:], f_5[:, u % 2, :, :, 2:5], by_r(1, u), ALU.mult).then_inc(x_step, 1)
                        pool.tensor_tensor(t2[:], f_5[:, u % 2, :, :, 1:4], by_r(2, u), ALU.mult).then_inc(x_step, 1)
                        wait_units(pool, x_step, i, u, 0, 2)
                        pool.tensor_tensor(f_x[:, u % 2, :, 8:16, :], t1[:], t2[:], ALU.subtract).then_inc(x_done, 1)
                    unit, drain = staged(((gather, 0), (cross, 2)))
                    flow(pool, unit, tail=drain)

                @block.scalar
                def _(a):
                    def hidden(i, u):
                        wait_slot(a, dist_in, i, u)
                        wait_units(a, r_done, i, u, 2, TJ)
                        a.activation(hid[0:64, u % 2, :], dist[:, u % 2, :], ACT.Relu, bias=cols[0:64, 2:3],
                                     scale=cols[0:64, 1:2]).then_inc(hid_done, 1)

                    def spreads(i, u):
                        wait_gathered(a, gathered, i, u)
                        wait_units(a, prods, i, u, 2, TJ)
                        wait_units(a, msg_done, i, u, BU)
                        wait_units(a, x_done, i, u, 2)
                        f1 = rows[:, u, :, 8:32].rearrange("p j (v o) -> p j v o", o=3)
                        a.copy(f_d[:, u % 2, :, 0:8], rows[:, u, :, 0:8])
                        a.copy(f_x[:, u % 2, :, 0:8, :], f1)
                        a.copy(f_5[:, u % 2, :, :, 0:3], f1)
                        a.copy(f_5[:, u % 2, :, :, 3:5], f1[:, :, :, 0:2])
                        a.copy(r[:, u], r5[:, bass.ds((i * BU + u) * TJ, TJ), :]).then_inc(spread, 1)
                    unit, drain = staged(((spreads, 1), (hidden, 0)))
                    flow(a, unit, tail=drain)

                @block.tensor
                def _(pe):
                    pe.wait_ge(set_up, 1)

                    def program(narrow):
                        def weights(i, u):
                            wait_units(pe, hid_done, i, u)
                            for j in range(TJ):
                                if not (isinstance(i, int) and i == 0 and u == 0):
                                    pe.wait_ge(prods, (i * BU + u) * TJ + j - TJ + 1)
                                pe.matmul(ps[j][:, 0:384], hid[:, u % 2, j * P:(j + 1) * P], w2m[:],
                                          start=True, stop=True).then_inc(r_done, 1)

                        def window_sums(i, u):
                            wait_units(pe, hots, i, u)
                            wait_units(pe, msg_done, i, u)
                            wait_units(pe, c_summed, i, u)
                            wait_units(pe, added, i, u, 2, adds(narrow))
                            window_products(pe, ps[4 + u % 2], P, lambda j: [msg[:, u % 2, j, 0:P]], oh[:, u % 2],
                                            narrow).then_inc(summed, 1)
                        unit, drain = staged(((weights, 0), (window_sums, 1)))
                        flow(pe, unit, tail=drain)
                    split(pe, program)

                @block.vector
                def _(v):
                    v.memset(hid[64:65, :, :], 1.0).then_inc(set_up, 1)

                    def program(narrow):
                        def dot_parts(i, u):
                            wait_units(v, spread, i, u)
                            wait_units(v, dot_done, i, u, 1)
                            v.tensor_tensor(t3[:], f_5[:, u % 2, :, :, 0:3], by_r(0, u), ALU.mult).then_inc(dot_step, 1)

                        def dot(i, u):
                            wait_units(v, dot_step, i, u)
                            v.tensor_reduce(f_d[:, u % 2, :, 8:16], t3[:], AX_X, ALU.add).then_inc(dot_done, 1)

                        def products(i, u):
                            wait_units(v, x_done, i, u)
                            wait_units(v, dot_done, i, u)
                            wait_units(v, halved, i, u, 1)
                            wait_units(v, ab_summed, i, u, 1)
                            for j in range(TJ):
                                v.wait_ge(r_done, (i * BU + u) * TJ + j + 1)
                                abc = ps[j][:, 0:384].rearrange("p (b v u) -> p b v u", b=3, u=8)
                                v.tensor_tensor(ab_prod[:, j], abc[:, 0:2],
                                                f_d[:, u % 2, j, :].unsqueeze(1).unsqueeze(3).broadcast_to([P, 2, 16, 8]),
                                                ALU.mult)
                                v.tensor_tensor(c_prod[:, j].rearrange("p v (u o) -> p v u o", o=3),
                                                abc[:, 2].unsqueeze(3).broadcast_to([P, 16, 8, 3]),
                                                f_x[:, u % 2, j].unsqueeze(2).broadcast_to([P, 16, 8, 3]),
                                                ALU.mult).then_inc(prods, 1)

                        def halve(i, u):
                            wait_units(v, prods, i, u, 0, TJ)
                            wait_units(v, c_summed, i, u, 1)
                            v.tensor_tensor(c_half[:], c_prod[:, :, 0:8, :], c_prod[:, :, 8:16, :],
                                            ALU.add).then_inc(halved, 1)

                        def sum_ab(i, u):
                            wait_units(v, summed, i, u, 2)
                            v.tensor_reduce(msg[:, u % 2, :, P - 8:P + 8].rearrange("p j (b u) -> p j b u", b=2),
                                            ab_prod[:].rearrange("p j b v u -> p j b u v"),
                                            AX_X, ALU.add).then_inc(ab_summed, 1)

                        def quarter(i, u):
                            wait_units(v, halved, i, u)
                            v.tensor_tensor(msg[:, u % 2, :, 0:96].rearrange("p j (v c) -> p j v c", v=4),
                                            c_half[:, :, 0:4, :], c_half[:, :, 4:8, :], ALU.add).then_inc(c_summed, 1)

                        def direct(i, u):
                            wait_units(v, ab_summed, i, u)
                            v.tensor_tensor(msg[:, u % 2, :, 96:120].rearrange("p j (u o) -> p j u o", o=3),
                                            msg[:, u % 2, :, P:P + 8].unsqueeze(3).broadcast_to([P, TJ, 8, 3]),
                                            by_r(0, u), ALU.mult).then_inc(msg_done, 1)

                        def hot(i, u):
                            wait_units(v, summed, i, u, 2)
                            one_hots(v, oh, i, u, narrow).then_inc(hots, 1)

                        def add(i, u):
                            wait_units(v, summed, i, u)
                            add_windows(v, ps[4 + u % 2], P, i, u, added, narrow)
                        unit, drain = staged(((halve, 1), (sum_ab, 1), (dot_parts, 0), (quarter, 1), (direct, 1), (dot, 0),
                                              (hot, 0), (products, 0), (add, 2)))
                        flow(v, unit, tail=drain)
                    split(v, program)

        sum_to_nodes(P, fold_msg[:], D, add_to_x)
        finish(nc, sem, x_nm, out)


def finish(nc, sem, x_nm, out):
    done = sem("out_stored")
    with nc.Block() as block:
        @block.sync
        def _(sp):
            sp.dma_start(out[0:(NB - 2) * P, :].rearrange("(c p) f -> p c f", p=P),
                         x_nm[:, 0:NB - 2, :]).then_inc(done, 16)
            sp.dma_start(out[(NB - 2) * P:(NB - 1) * P, :], x_nm[:, NB - 2, :]).then_inc(done, 16)
            sp.dma_start(out[(NB - 1) * P:N, :], x_nm[0:TAIL, NB - 1, :]).then_inc(done, 16)
            sp.wait_ge(done, 48)


_WEIGHTS = ["L0_gnn_W1", "L0_gnn_b1", "L0_gnn_W2", "L0_gnn_b2", "L1_gnn_weight", "L1_gnn_bias"] + \
    [f"L2_gnn_m{m}_{k}{n}" for m in (1, 2) for n in (1, 2, 3) for k in "gbwc"] + \
    ["L3_gnn_w1", "L3_gnn_b1", "L3_gnn_w2", "L3_gnn_b2"]


def kernel(**inputs):
    import concourse.bacc as _bacc
    from concourse import mybir as _mybir
    from concourse.bass_utils import run_bass_kernel_spmd as _run

    a = {k: np.asarray(v) for k, v in inputs.items()}

    def padded(v, fill):
        return np.concatenate([v, np.full((EP - E,) + v.shape[1:], fill, v.dtype)])

    src, dst = padded(a["src"], PAD_SRC), padded(a["dst"], N)
    arrays = {
        "x": a["x"],
        "src_t": np.pad(src.reshape(NT, P).T, ((0, 0), (0, 2 * TJ))),
        "dst_t": dst.reshape(NT, P).T,
        "next_t": np.concatenate([dst[1:], dst[-1:]]).reshape(NT, P).T,
        "first": dst.reshape(NT, P)[:, 0],
        "dst_row": np.concatenate([np.full((1,), -1, dst.dtype), dst]),
        "eaT": padded(a["edge_attr_32"], 0).T,
        "rel_t": padded(a["edge_attr_3"], 1).reshape(NT, P, 3).transpose(1, 0, 2),
        "dist": padded(a["edge_weight"], 0),
    }
    for k in _WEIGHTS:
        arrays[k] = a[k]
    arrays = {k: np.ascontiguousarray(v) for k, v in arrays.items()}
    nc = _bacc.Bacc("TRN2", target_bir_lowering=False, num_devices=1)
    A = {k: nc.dram_tensor("in_" + k, list(v.shape), _mybir.dt.from_np(v.dtype), kind="ExternalInput").ap()
         for k, v in arrays.items()}
    out = nc.dram_tensor("out", [N, D], F32, kind="ExternalOutput").ap()
    build(nc, A, out)
    r = _run(nc, [{"in_" + k: v for k, v in arrays.items()}], core_ids=[0])
    return r.results[0]["out"]
```

```python
from contextlib import ExitStack

import numpy as np

import concourse.bass as bass
from concourse import mybir

F32 = mybir.dt.float32
BF16 = mybir.dt.bfloat16
I32 = mybir.dt.int32
ALU = mybir.AluOpType
ACT = mybir.ActivationFunctionType
AX_X = mybir.AxisListType.X

P = 128
N = 12500
E = 212500
D = 32
NB = -(-N // P)
NP = NB * P
TAIL = N - (NB - 1) * P
PAD_SRC = NP - 1
TJ = 4
U = TJ * P
BU = 4
BODY = BU * U
BODIES = -(-E // BODY)
EP = BODIES * BODY
NT = EP // P
UNITS = NT // TJ
LAST = E - (UNITS - 1) * U
W = 64
MSG = 80
ACC = 12672
CH = 500
NCH = N // CH
EPS = 1e-5
GRP = 14
assert NB % GRP == 0 and 0 < LAST < P


def flow(eng, body, last=None, tail=None, bu=BU):
    for i in range(2):
        for u in range(bu):
            body(i, u)
    end = BODIES - 1 if last else BODIES
    with eng.Fori(2, end) as i:
        for u in range(bu):
            body(i, u)
    if last:
        for u in range(bu):
            last(BODIES - 1, u)
    if tail:
        for u in range(bu):
            tail(BODIES, u)


def before(i, u, lag, bu=BU):
    u -= lag
    if u < 0:
        if isinstance(i, int) and i == 0:
            return None
        i, u = i - 1, u + bu
    return i, u


def wait_units(eng, sem, i, u, back=0, per=1, bu=BU):
    w = before(i, u, back, bu)
    if w is not None:
        eng.wait_ge(sem, (w[0] * bu + w[1] + 1) * per)


def wait_pairs(eng, sem, i, k, back=0, per=1):
    wait_units(eng, sem, i, k, back, per, BU // 2)


def wait_slot(eng, sems, i, u, per=16):
    eng.wait_ge(sems[u % 2], (i * (BU // 2) + u // 2 + 1) * per)


def staged(stages, bu=BU):
    def unit(i, u):
        for f, lag in stages:
            if before(i, u, lag, bu) is not None:
                f(*before(i, u, lag, bu))

    def drain(i, u):
        for f, lag in stages:
            if lag > u:
                f(*before(i, u, lag, bu))
    return unit, drain


def build(nc, A, out):
    with ExitStack() as ctx:
        n_sem = [0]
        in_use = []

        def sb(name, shape, dt=F32):
            return ctx.enter_context(nc.sbuf_tensor(name, shape, dt))

        def local(own, name, shape, dt=F32):
            n_sem[0] += 1
            return own.enter_context(nc.sbuf_tensor(f"{name}_{n_sem[0]}", shape, dt))

        def sem(name):
            n_sem[0] += 1
            handle = nc.alloc_semaphore(name=f"{name}_{n_sem[0]}")
            in_use.append(handle)
            return handle

        def recycle():
            nc.clear_and_free_semaphores(in_use)
            in_use.clear()
            nc.all_engine_barrier()

        def sems(name, n=2):
            return [sem(f"{name}{k}") for k in range(n)]

        def dram(name, shape, dt=F32):
            return nc.dram_tensor(name, shape, dt, kind="Internal").ap()

        h_table = dram("h_table", [NP, D])
        h1_table = dram("h1_table", [NP, D + 1])
        b_table = dram("b_table", [NP + P, 64])
        keep_dram = dram("keep_dram", [EP])
        z1_dram = dram("z1_dram", [64, EP])

        ident = sb("ident", [P, P])
        iota = sb("iota", [P, P])
        iota_b = sb("iota_b", [P, P], BF16)
        x_nm = sb("x_nm", [P, NB, D])
        h_nm = sb("h_nm", [P, NB, D])
        dst_rel = [sb(f"dst_rel{k}", [P, NT]) for k in range(2)]
        dst_last = [sb(f"dst_last{k}", [P, NT]) for k in range(2)]
        node_of = [sb("node_of0", [P, NT]), sb("node_of1", [P, UNITS])]
        narrow_ok = sb("narrow_ok", [1, 1], I32)
        fold_msg = sb("fold_msg", [MSG, D])
        first = sb("first", [1, NT], I32)
        deg_out = sb("deg_out", [P, NB])
        ea_stats = sb("ea_stats", [D, 2])
        acc = sb("acc", [P, ACC])
        big = sb("big", [P, NP])
        src_lo, src_hi = big[:, 4 * NT:5 * NT], big[:, 5 * NT:6 * NT]
        banks = ctx.enter_context(nc.psum_tensor("banks", [P, 8, 512], F32))
        ps = [banks[:, k, :] for k in range(8)]

        wz = sb("wz", [64, 64])
        wb = sb("wb", [D, 64])
        cols = sb("cols", [P, 32])
        w2x = sb("w2x", [65, D])
        w_l1 = sb("w_l1", [D + 1, D + 1])
        bias_l1 = sb("bias_l1", [P, D])
        m1w = [sb(f"m1w{k}", [65, 64]) for k in range(3)]
        c_rows = sb("c_rows", [1, 2, 64])
        m2w = [sb(f"m2w{k}", [96, 96]) for k in range(3)]
        w2r = sb("w2r", [65, 384])
        w2m = sb("w2m", [65, 384])

        class Chain:

            def __init__(self, eng, sem):
                self.eng, self.sem, self.n = eng, sem, 0

            def __call__(self, ins):
                self.n += 1
                ins.then_inc(self.sem, 1)
                self.eng.wait_ge(self.sem, self.n)

        with ExitStack() as own, nc.Block() as block:
            keep_dram_ready, keep_in, keep_stored = sem("keep_ready"), sem("keep_in"), sem("keep_stored")
            widest_ready, widest_turned = sem("widest_ready"), sem("widest_turned")
            widest = local(own, "widest", [P, 1])
            keep_f = acc[:, 0:NT]
            dst_i, next_i, first_i, src_i = (acc[:, k * NT:(k + 1) * NT].bitcast(I32) for k in range(1, 5))
            flat_i = acc[:, 5 * NT:7 * NT].bitcast(I32).rearrange("p (k t) -> p k t", k=2)
            nxt = big[:, 0:NT]
            fst = big[:, NT:2 * NT]
            part_i = local(own, "part_i", [P, 1], I32)
            part = local(own, "part", [P, 1])
            part_lo = big[:, 6 * NT:7 * NT].bitcast(I32)
            cleared = sem("cleared")
            loaded, indices_in = sem("loaded"), sem("indices_in")
            made = sem("made")
            masks = sem("masks")
            dve_step = sem("dve_step")
            n_loads = [0]
            index_loads = ((dst_i, A["dst_t"]), (next_i, A["next_t"]), (first_i, A["first"].partition_broadcast(P)),
                           (src_i, A["src_t"][:, 0:NT]), (first[:], A["first"][None, :]))

            @block.sync
            def _(sp):
                for dst, src in index_loads:
                    sp.dma_start(dst, src).then_inc(indices_in, 16)
                sp.dma_start(flat_i[:, 0, :], A["dst_row"][1:EP + 1].rearrange("(p t) -> p t", p=P)).then_inc(keep_in, 16)
                sp.dma_start(flat_i[:, 1, :], A["dst_row"][0:EP].rearrange("(p t) -> p t", p=P)).then_inc(keep_in, 16)
                sp.wait_ge(cleared, 1)

                def load(dst, src):
                    n_loads[0] += 1
                    sp.dma_start(dst, src).then_inc(loaded, 16)
                load(x_nm[:, 0:NB - 2, :], A["x"][0:(NB - 2) * P, :].rearrange("(c p) f -> p c f", p=P))
                load(x_nm[:, NB - 2, :], A["x"][(NB - 2) * P:(NB - 1) * P, :])
                load(x_nm[0:TAIL, NB - 1, :], A["x"][(NB - 1) * P:N, :])
                load(wz[0:D, :], A["L0_gnn_W1"][0:D, :])
                load(wz[D:2 * D, :], A["L0_gnn_W1"][2 * D:3 * D, :])
                load(wb[:], A["L0_gnn_W1"][D:2 * D, :])
                load(w2x[0:64, :], A["L0_gnn_W2"])
                load(w2x[64:65, :], A["L0_gnn_b2"][None, :])
                load(w_l1[0:D, 0:D], A["L1_gnn_weight"])
                load(bias_l1[:], A["L1_gnn_bias"].partition_broadcast(P))
                for k in range(3):
                    load(m1w[k][0:64, :], A[f"L2_gnn_m1_w{k + 1}"])
                load(c_rows[:, 0, :], A["L2_gnn_m1_c2"][None, :])
                load(c_rows[:, 1, :], A["L2_gnn_m1_c3"][None, :])
                load(m2w[0][0:64, :], A["L2_gnn_m2_w1"][D:96, :])
                load(m2w[0][64:96, :], A["L2_gnn_m2_w1"][0:D, :])
                load(m2w[1][:], A["L2_gnn_m2_w2"])
                load(m2w[2][:, 0:D], A["L2_gnn_m2_w3"])
                load(w2r[0:64, :], A["L3_gnn_w2"])
                load(w2r[64:65, :], A["L3_gnn_b2"][None, :])

                def column(n, rows, name, lo=0, hi=None):
                    v = A[name]
                    hi = v.shape[-1] if hi is None else hi
                    v = v[0, :] if len(v.shape) == 2 else v
                    load(cols[rows:rows + hi - lo, n:n + 1], v[lo:hi].rearrange("(a b) -> a b", b=1))
                column(0, 0, "L0_gnn_b1")
                column(1, 0, "L3_gnn_w1")
                column(2, 0, "L3_gnn_b1")
                for k in range(3):
                    column(3 + 2 * k, 0, f"L2_gnn_m1_g{k + 1}")
                    column(4 + 2 * k, 0, f"L2_gnn_m1_b{k + 1}")
                column(9, 0, "L2_gnn_m1_c1")
                column(10, 0, "L2_gnn_m2_g1", D, 96)
                column(10, 64, "L2_gnn_m2_g1", 0, D)
                column(11, 0, "L2_gnn_m2_b1", D, 96)
                column(11, 64, "L2_gnn_m2_b1", 0, D)
                for k in (1, 2):
                    column(10 + 2 * k, 0, f"L2_gnn_m2_g{k + 1}")
                    column(11 + 2 * k, 0, f"L2_gnn_m2_b{k + 1}")
                for k in range(3):
                    column(16 + k, 0, f"L2_gnn_m2_c{k + 1}")
                sp.wait_ge(loaded, 16 * n_loads[0])
                sp.wait_ge(keep_dram_ready, 1)
                sp.dma_start(keep_dram.rearrange("(p t) -> p t", p=P), keep_f).then_inc(keep_stored, 16)
                sp.wait_ge(keep_stored, 16)

            @block.tensor
            def _(pe):
                pe.wait_ge(widest_ready, 1)
                pe.transpose(ps[0][0:1, 0:P], widest[:], ident[:]).then_inc(widest_turned, 1)

            @block.gpsimd
            def _(pool):
                pool.iota(part_i[:], [[1, 1]], base=0, channel_multiplier=1).then_inc(made, 1)
                pool.iota(iota[:], [[1, P]], base=0, channel_multiplier=0,
                          allow_small_or_imprecise_dtypes=True).then_inc(made, 1)
                pool.memset(ident[:], 0.0).then_inc(masks, 1)
                pool.wait_ge(masks, 1)
                pool.affine_select(out=ident[:], in_=ident[:], compare_op=ALU.not_equal, fill=1.0, base=0,
                                   pattern=[[-1, P]], channel_multiplier=1).then_inc(made, 1)

            @block.vector
            def _(v):
                step = Chain(v, dve_step)
                for t in (cols, x_nm, w_l1, m2w[2]):
                    step(v.memset(t[:], 0.0))
                v.memset(w_l1[D:D + 1, D:D + 1], 1.0).then_inc(cleared, 1)
                v.wait_ge(made, 3)
                step(v.tensor_copy(iota_b[:], iota[:]))
                step(v.tensor_reduce(fold_msg[:, 8:D], ident[0:MSG, 0:72].rearrange("p (q c) -> p c q", q=3), AX_X, ALU.add))
                step(v.tensor_copy(fold_msg[:, 0:8], ident[0:MSG, 72:MSG]))
                step(v.tensor_copy(part[:], part_i[:]))
                v.wait_ge(indices_in, 16 * len(index_loads))
                step(v.tensor_scalar(part_lo, src_i, P - 1, None, ALU.bitwise_and))
                step(v.tensor_scalar(src_i, src_i, 7, None, ALU.logical_shift_right))
                step(v.tensor_copy(src_lo, part_lo))
                step(v.tensor_copy(src_hi, src_i))
                dst = keep_f
                step(v.tensor_copy(dst, dst_i))
                step(v.tensor_copy(nxt, next_i))
                step(v.tensor_copy(fst, first_i))
                step(v.tensor_tensor(nxt, nxt, dst, ALU.not_equal))
                unit_first = fst.rearrange("p (n j) -> p n j", j=TJ)[:, :, 0]
                for k, f, shape in ((0, fst, [P, NT]), (1, unit_first.unsqueeze(2).broadcast_to([P, UNITS, TJ]),
                                                        [P, UNITS, TJ])):
                    def v3(t):
                        return t if k == 0 else t.rearrange("p (n j) -> p n j", j=TJ)
                    step(v.tensor_tensor(v3(dst_rel[k][:]), v3(dst), f, ALU.subtract))
                    step(v.scalar_tensor_tensor(out=dst_last[k][:], in0=dst_rel[k][:], scalar=1.0, in1=nxt,
                                                op0=ALU.add, op1=ALU.mult))
                    step(v.tensor_scalar(dst_last[k][:], dst_last[k][:], -1.0, None, ALU.add))
                step(v.tensor_scalar(node_of[0][:], fst, part[:], None, ALU.add))
                step(v.tensor_scalar(node_of[1][:], unit_first, part[:], -float(P - W), ALU.add, ALU.add))
                v.tensor_reduce(widest[:], dst_rel[1][:], AX_X, ALU.max).then_inc(widest_ready, 1)
                v.wait_ge(widest_turned, 1)
                step(v.tensor_reduce(part[0:1, :], ps[0][0:1, 0:P], AX_X, ALU.max))
                step(v.tensor_scalar(narrow_ok[:], part[0:1, :], float(W), None, ALU.is_lt))
                v.wait_ge(keep_in, 32)
                v.tensor_tensor(keep_f, flat_i[:, 0, :], flat_i[:, 1, :], ALU.is_equal).then_inc(keep_dram_ready, 1)
                v.wait_ge(loaded, 16 * n_loads[0])
                w4 = [w2r[:, 64 * k:64 * (k + 1)].rearrange("p (u v) -> p u v", v=8) for k in range(3)]
                w5 = w2r[:, 192:384].rearrange("p (u v k) -> p u v k", v=8, k=3)
                ab = w2m[:, 0:256].rearrange("p (v b u) -> p b u v", b=2, u=8)
                c = w2m[:, 256:384].rearrange("p (v u) -> p u v", u=8)
                q = float(np.sqrt(3.0 / 32.0))
                for dst, src, s in ((ab[:, 0, :, 0:8], w4[0], 0.25), (ab[:, 0, :, 8:16], w4[1], 0.25),
                                    (ab[:, 1, :, 0:8], w4[2], q),
                                    (ab[:, 1, :, 8:16], w5[:, :, :, 2], 0.375),
                                    (c[:, :, 0:8], w5[:, :, :, 0], float(1.0 / np.sqrt(32.0))),
                                    (c[:, :, 8:16], w5[:, :, :, 1], float(np.sqrt(3.0) / 8.0))):
                    step(v.tensor_scalar(dst, src, s, None, ALU.mult))
                step(v.scalar_tensor_tensor(out=c[:, :, 0:8], in0=ab[:, 1, :, 8:16], scalar=-1.0 / 3.0,
                                            in1=c[:, :, 0:8], op0=ALU.mult, op1=ALU.add))

        def clear_sum(rows):
            with nc.Block() as block:
                @block.vector
                def _(v):
                    v.memset(acc[0:rows, :], 0.0)

        def layernorm():
            d = big[:, 0:NB * D].rearrange("p (c f) -> p c f", f=D)
            sq = big[:, NB * D:2 * NB * D].rearrange("p (c f) -> p c f", f=D)
            r1 = big[:, 2 * NB * D:2 * NB * D + NB]
            r2 = big[:, 2 * NB * D + NB:2 * NB * D + 2 * NB]

            def spread(r):
                return r.unsqueeze(2).broadcast_to([P, NB, D])
            step_done, var_ready, std_ready = sem("ln_step"), sem("var_ready"), sem("std_ready")
            with nc.Block() as block:
                @block.vector
                def _(v):
                    step = Chain(v, step_done)
                    step(v.tensor_reduce(r1, x_nm[:], AX_X, ALU.add))
                    step(v.tensor_scalar(r1, r1, 1.0 / D, None, ALU.mult))
                    step(v.tensor_tensor(d, x_nm[:], spread(r1), ALU.subtract))
                    step(v.tensor_tensor(sq, d, d, ALU.mult))
                    step(v.tensor_reduce(r2, sq, AX_X, ALU.add))
                    v.tensor_scalar(r2, r2, 1.0 / D, EPS, ALU.mult, ALU.add).then_inc(var_ready, 1)
                    v.wait_ge(std_ready, 1)
                    step(v.reciprocal(r2, r1))
                    step(v.tensor_tensor(d, d, spread(r2), ALU.mult))
                    step(v.tensor_scalar(h_nm[:], d, 0.0, None, ALU.max))

                @block.scalar
                def _(a):
                    a.wait_ge(var_ready, 1)
                    a.activation(r1, r2, ACT.Sqrt).then_inc(std_ready, 1)

        def store_table(table, src_nm):
            stored = sem("table_stored")
            with nc.Block() as block:
                @block.sync
                def _(sp):
                    sp.dma_start(table[0:NP, :].rearrange("(c p) f -> p c f", p=P), src_nm).then_inc(stored, 16)
                    sp.wait_ge(stored, 16)

        def sum_to_nodes(rows, rhs, width, post):
            turned, used, step_done = sem("turned"), sem("turned_used"), sem("post_step")
            with nc.Block() as block:
                @block.tensor
                def _(pe):
                    for g in range(NB // GRP):
                        if g >= 2:
                            pe.wait_ge(used, g - 1)
                        for j in range(GRP):
                            c = g * GRP + j
                            o, block = ps[g % 2][:, j * width:(j + 1) * width], acc[0:rows, c * P:(c + 1) * P]
                            if rhs is None:
                                last = pe.transpose(o, block, ident[0:rows, 0:rows])
                            else:
                                last = pe.matmul(o, block, rhs, start=True, stop=True)
                        last.then_inc(turned, 1)

                @block.vector
                def _(v):
                    step = Chain(v, step_done)
                    for g in range(NB // GRP):
                        v.wait_ge(turned, g + 1)
                        post(v, ps[g % 2][:, 0:GRP * width].rearrange("p (c f) -> p c f", f=width),
                             g * GRP, step)
                        v.sem_inc(used, 1)

        def split(eng, program):
            ok = eng.value_load(narrow_ok[0:1, 0:1], min_val=0, max_val=1)
            with eng.If(ok):
                program(1)
            with eng.Else():
                program(0)

        def adds(narrow):
            return 1 if narrow else TJ

        def one_hots(v, ring, i, u, narrow, columns=None):
            columns = (columns or dst_rel)[narrow]
            t = (i * BU + u) * TJ
            if narrow:
                return v.tensor_tensor(ring[:, u % 2, :, 0:W], iota[:, 0:W].unsqueeze(1).broadcast_to([P, TJ, W]),
                                       columns[:, bass.ds(t, TJ)].unsqueeze(2).broadcast_to([P, TJ, W]), ALU.is_equal)
            for j in range(TJ):
                ins = v.tensor_scalar(ring[:, u % 2, j, :], iota[:], columns[:, bass.ds(t + j, 1)], None, ALU.is_equal)
            return ins

        def window_products(pe, bank, rows, parts, hot, narrow):
            for j in range(TJ):
                pieces = parts(j)
                for k, piece in enumerate(pieces):
                    o = bank[0:rows, 0:W] if narrow else bank[0:rows, j * P:(j + 1) * P]
                    last = pe.matmul(o, piece, hot[:, j, 0:W] if narrow else hot[:, j, :],
                                     start=(k == 0 and (j == 0 or not narrow)),
                                     stop=(k == len(pieces) - 1 and (j == TJ - 1 or not narrow)))
            return last

        def add_windows(v, bank, rows, i, u, added, narrow):
            for j in range(adds(narrow)):
                t = (i * BU + u) * TJ + j
                n0 = v.value_load(first[0:1, bass.ds(t, 1)], min_val=0, max_val=N)
                if not (isinstance(t, int) and t == 0):
                    v.wait_ge(added, i * BU + u if narrow else t)
                w = acc[0:rows, bass.ds(n0, W if narrow else P)]
                v.tensor_tensor(w, w, bank[0:rows, 0:W] if narrow else bank[0:rows, j * P:(j + 1) * P],
                                ALU.add).then_inc(added, 1)

        def gather_loop(pool, table, rows_of, idx, idx_in, gathered, rows_free):
            may_gather = sem("may_gather")

            def unit(i, u):
                if u % 2 == 0:
                    pool.wait_ge(idx_in[u // 2], 16 * (i + 1))
                wait_units(pool, rows_free, i, u, BU)
                pool.sem_inc(may_gather, 1)
                for j in range(TJ):
                    pool.indirect_dma_start(
                        out=rows_of(u, j), out_offset=None, in_=table,
                        in_offset=bass.IndirectOffsetOnAxis(ap=idx[:, u // 2, (u % 2) * TJ + j:(u % 2) * TJ + j + 1],
                                                            axis=0)).then_inc(gathered[u], 16)
            flow(pool, unit)

        def first_indices(eng, idx, idx_in):
            for half in range(2):
                eng.dma_start(idx[:, half, :], A["src_t"][:, half * 2 * TJ:(half + 1) * 2 * TJ]).then_inc(idx_in[half], 16)

        def load_indices(eng, idx, idx_in, gathered, i, u):
            if u % 2 == 1:
                for k in (u - 1, u):
                    eng.wait_ge(gathered[k], (i + 1) * 16 * TJ)
                eng.dma_start(idx[:, u // 2, :],
                              A["src_t"][:, bass.ds((i * BU + u + 3) * TJ, 2 * TJ)]).then_inc(idx_in[u // 2], 16)

        def last_indices(eng, idx_in):
            for half in range(2):
                eng.wait_ge(idx_in[half], 16 * (BODIES + 1))

        def wait_gathered(eng, gathered, i, u):
            eng.wait_ge(gathered[u], 16 * TJ * (i + 1))

        layernorm()
        with ExitStack() as own:
            hT = local(own, "hT", [D, 2, 4 * P], F32)
            rows = local(own, "rows", [P, NB, 64], F32)
            turned, copied, prod, rows_out, stored = (sem("b_turned"), sem("b_copied"), sem("b_prod"),
                                                      sem("b_rows"), sem("b_stored"))
            NG = -(-NB // 4)
            with nc.Block() as block:
                @block.tensor
                def _(pe):
                    for g in range(NG):
                        n = min(4, NB - 4 * g)
                        if g >= 2:
                            pe.wait_ge(copied, g - 1)
                        for j in range(n):
                            last = pe.transpose(ps[g % 2][0:D, j * P:(j + 1) * P], h_nm[:, 4 * g + j, :], ident[:])
                        last.then_inc(turned, 1)
                        pe.wait_ge(copied, g + 1)
                        if g >= 2:
                            pe.wait_ge(rows_out, g - 1)
                        for j in range(n):
                            last = pe.matmul(ps[2 + g % 2][:, j * 64:(j + 1) * 64], hT[:, g % 2, j * P:(j + 1) * P],
                                             wb[:], start=True, stop=True)
                        last.then_inc(prod, 1)

                @block.scalar
                def _(a):
                    for g in range(NG):
                        n = min(4, NB - 4 * g)
                        a.wait_ge(turned, g + 1)
                        if g >= 2:
                            a.wait_ge(prod, g - 1)
                        a.copy(hT[:, g % 2, 0:n * P], ps[g % 2][0:D, 0:n * P]).then_inc(copied, 1)

                @block.vector
                def _(v):
                    for g in range(NG):
                        n = min(4, NB - 4 * g)
                        v.wait_ge(prod, g + 1)
                        v.tensor_copy(rows[:, 4 * g:4 * g + n, :],
                                      ps[2 + g % 2][:, 0:n * 64].rearrange("p (c f) -> p c f", f=64)).then_inc(rows_out, 1)

                @block.gpsimd
                def _(pool):
                    pool.memset(acc[0:D, :], 0.0)

                @block.sync
                def _(sp):
                    sp.dma_start(h_table.rearrange("(c p) f -> p c f", p=P), h_nm[:]).then_inc(stored, 16)
                    for g in range(0, NG, 5):
                        end = min(g + 5, NG)
                        sp.wait_ge(rows_out, end)
                        lo, hi = 4 * g, min(4 * end, NB)
                        sp.dma_start(b_table[lo * P:hi * P, :].rearrange("(c p) f -> p c f", p=P),
                                     rows[:, lo:hi, :]).then_inc(stored, 16)
                    sp.dma_start(b_table[NP:NP + P, :], rows[:, 0, :]).then_inc(stored, 16)
                    sp.wait_ge(stored, (2 + -(-NG // 5)) * 16)

        with ExitStack() as own:
            def ring(name, shape, dt=F32):
                return local(own, name, shape, dt)
            idx = ring("idx", [P, 2, 2 * TJ], I32)
            rows = ring("rows", [P, BU, TJ, D])
            feat = ring("feat", [P, 2, U])
            wzb = ring("wzb", [P, 2, 64])
            bwin = big[:, 0:2 * TJ * 64].rearrange("p (s j f) -> p s j f", s=2, j=TJ)
            ohT = big[:, 2 * TJ * 64:2 * TJ * 64 + 2 * U].rearrange("p (s e) -> p s e", s=2)
            ohl = ring("ohl", [P, 2, TJ, P])
            sh = ring("sh", [P, 2, TJ, P], BF16)
            sb_ = ring("sb_", [P, 2, TJ, NB], BF16)
            hid = ring("hid", [65, 2, U])
            dst_b = ring("dst_b", [P, 2, U], I32)
            keep = ring("keep", [D, 2, U])
            run = ring("run", [D, 2, U])
            runT = ring("runT", [P, 2, TJ, D])
            idx_in, ea_in, win_in, dst_in, keep_in = (sems("idx_in"), sems("ea_in"), sems("win_in"), sems("dst_in"),
                                                      sems("keep_in"))
            gathered = sems("gathered", BU)
            (turned, rows_copied, hots, z_done, hid_done, v_done, ran, run_turned, run_copied, last_hots, summed,
             added, set_up, src_hots, counted, pe_go) = [sem(s) for s in (
                 "turned", "rows_copied", "hots", "z_done", "hid_done", "v_done", "ran", "run_turned", "run_copied",
                 "last_hots", "summed", "added", "set_up", "src_hots", "counted", "pe_go")]

            with nc.Block() as block:
                @block.sync
                def _(sp):
                    def program(narrow):
                        lo = P - W if narrow else 0

                        def unit(i, u):
                            n = i * BU + u
                            wait_units(sp, z_done, i, u, 2)
                            sp.dma_start(feat[D:2 * D, u % 2, :],
                                         A["eaT"][:, bass.ds(n * U, U)]).then_inc(ea_in[u % 2], 16)
                            for j in range(adds(narrow)):
                                n0 = sp.value_load(first[0:1, bass.ds(n * TJ + j, 1)], min_val=0, max_val=N)
                                if narrow:
                                    sp.dma_start(wzb[P - W:P, u % 2, :], b_table[bass.ds(n0, W), :]).then_inc(win_in[u % 2], 16)
                                else:
                                    sp.dma_start(bwin[:, u % 2, j, :], b_table[bass.ds(n0, P), :]).then_inc(win_in[u % 2], 16)
                            wait_units(sp, hots, i, u, 2)
                            sp.dma_start(dst_b[lo:P, u % 2, :],
                                         A["dst_row"][bass.ds(n * U + 1, U)].partition_broadcast(P - lo)).then_inc(dst_in[u % 2], 16)
                            wait_units(sp, ran, i, u, 2)
                            sp.dma_start(keep[:, u % 2, :],
                                         keep_dram[bass.ds(n * U, U)].partition_broadcast(D)).then_inc(keep_in[u % 2], 16)
                        flow(sp, unit)
                    split(sp, program)

                @block.gpsimd
                def _(pool):
                    gather_loop(pool, h_table, lambda u, j: rows[:, u, j, :], idx, idx_in, gathered, turned)

                @block.tensor
                def _(pe):
                    pe.wait_ge(set_up, 2)

                    def program(narrow):
                        def turn(i, u):
                            wait_gathered(pe, gathered, i, u)
                            wait_units(pe, rows_copied, i, u, 2)
                            for j in range(TJ):
                                last = pe.transpose(ps[u % 2][0:D, j * P:(j + 1) * P], rows[:, u, j, :], ident[:])
                            last.then_inc(turned, 1)

                        def hidden(i, u):
                            wait_units(pe, rows_copied, i, u)
                            wait_units(pe, hots, i, u)
                            wait_slot(pe, ea_in, i, u)
                            wait_units(pe, hid_done, i, u, 1)
                            wait_slot(pe, win_in, i, u, 16 * adds(narrow))
                            pe.sem_inc(pe_go, 1)
                            if narrow:
                                last = pe.matmul(ps[2][0:64, :], wzb[:, u % 2, :], feat[:, u % 2, :],
                                                 start=True, stop=True)
                            else:
                                pe.matmul(ps[2][0:64, :], wz[:], feat[0:64, u % 2, :], start=True, stop=False)
                                for j in range(TJ):
                                    last = pe.matmul(ps[2][0:64, j * P:(j + 1) * P], bwin[:, u % 2, j, :],
                                                     ohT[:, u % 2, j * P:(j + 1) * P], start=False, stop=(j == TJ - 1))
                            last.then_inc(z_done, 1)

                        def outputs(i, u):
                            wait_units(pe, hid_done, i, u)
                            wait_units(pe, ran, i, u, 1)
                            pe.matmul(ps[3][0:D, :], w2x[:], hid[:, u % 2, :], start=True, stop=True).then_inc(v_done, 1)

                        def turn_run(i, u):
                            wait_units(pe, ran, i, u)
                            wait_units(pe, run_copied, i, u, 1)
                            pe.sem_inc(pe_go, 1)
                            for j in range(TJ):
                                last = pe.transpose(ps[4][:, j * D:(j + 1) * D], run[:, u % 2, j * P:(j + 1) * P],
                                                    ident[0:D, 0:D])
                            last.then_inc(run_turned, 1)

                        def window_sums(i, u):
                            wait_units(pe, run_copied, i, u)
                            wait_units(pe, last_hots, i, u)
                            wait_units(pe, added, i, u, 1, adds(narrow))
                            window_products(pe, ps[5], D, lambda j: [runT[:, u % 2, j, :]], ohl[:, u % 2],
                                            narrow).then_inc(summed, 1)

                        def count(i, u):
                            wait_units(pe, src_hots, i, u)
                            static = isinstance(i, int)
                            for j in range(TJ):
                                last = pe.matmul(ps[6][:, 0:NB], sh[:, u % 2, j, :], sb_[:, u % 2, j, :],
                                                 start=(static and i == 0 and u == 0 and j == 0),
                                                 stop=(static and i == BODIES - 1 and u == BU - 1 and j == TJ - 1))
                            last.then_inc(counted, 1)
                        unit, drain = staged(((window_sums, 4), (turn_run, 3), (outputs, 2), (hidden, 1), (count, 1),
                                              (turn, 0)))
                        flow(pe, unit, tail=drain)
                    split(pe, program)

                @block.scalar
                def _(a):
                    def copies(i, u):
                        wait_units(a, turned, i, u)
                        wait_units(a, z_done, i, u, 2)
                        a.copy(feat[0:D, u % 2, :], ps[u % 2][0:D, :]).then_inc(rows_copied, 1)

                    def relu(i, u):
                        wait_units(a, z_done, i, u)
                        wait_units(a, v_done, i, u, 2)
                        a.activation(hid[0:64, u % 2, :], ps[2][0:64, :], ACT.Relu,
                                     bias=cols[0:64, 0:1]).then_inc(hid_done, 1)

                    def copy_run(i, u):
                        wait_units(a, run_turned, i, u)
                        wait_units(a, summed, i, u, 2)
                        a.copy(runT[:, u % 2].rearrange("p j f -> p (j f)"), ps[4][:, 0:TJ * D]).then_inc(run_copied, 1)

                    def indices(i, u):
                        load_indices(a, idx, idx_in, gathered, i, u)
                    unit, drain = staged(((copy_run, 3), (relu, 1), (copies, 0), (indices, 0)))
                    first_indices(a, idx, idx_in)
                    flow(a, unit, tail=drain)
                    last_indices(a, idx_in)

                @block.vector
                def _(v):
                    v.memset(hid[64:65, :, :], 1.0).then_inc(set_up, 1)
                    v.tensor_copy(wzb[0:64, :, :], wz[:].unsqueeze(1).broadcast_to([64, 2, 64])).then_inc(set_up, 1)

                    def program(narrow):
                        def nodes_by_edge(i, u):
                            wait_units(v, z_done, i, u, 2)
                            wait_slot(v, dst_in, i, u)
                            n = i * BU + u
                            if narrow:
                                v.tensor_scalar(feat[P - W:P, u % 2, :], dst_b[P - W:P, u % 2, :],
                                                node_of[1][P - W:P, bass.ds(n, 1)], None, ALU.is_equal).then_inc(hots, 1)
                                return
                            for j in range(TJ):
                                c = slice(j * P, (j + 1) * P)
                                last = v.tensor_scalar(ohT[:, u % 2, c], dst_b[:, u % 2, c],
                                                       node_of[0][:, bass.ds(n * TJ + j, 1)], None, ALU.is_equal)
                            last.then_inc(hots, 1)

                        def scan(i, u):
                            wait_units(v, v_done, i, u)
                            wait_slot(v, keep_in, i, u)
                            wait_units(v, run_turned, i, u, 2)
                            wait_units(v, ran, i, u, 1)
                            start = isinstance(i, int) and i == 0 and u == 0
                            v.tensor_tensor_scan(run[:, u % 2, :], keep[:, u % 2, :], ps[3][0:D, :],
                                                 0.0 if start else run[:, (u + 1) % 2, U - 1:U],
                                                 ALU.mult, ALU.max).then_inc(ran, 1)

                        def last_edges(i, u):
                            wait_units(v, summed, i, u, 2)
                            one_hots(v, ohl, i, u, narrow, dst_last).then_inc(last_hots, 1)

                        def sources(i, u):
                            wait_units(v, counted, i, u, 2)
                            t = bass.ds((i * BU + u) * TJ, TJ)
                            for ring_, part, width in ((sh, src_lo, P), (sb_, src_hi, NB)):
                                last = v.tensor_tensor(ring_[:, u % 2],
                                                       iota_b[:, 0:width].unsqueeze(1).broadcast_to([P, TJ, width]),
                                                       part[:, t].unsqueeze(2).broadcast_to([P, TJ, width]), ALU.is_equal)
                            last.then_inc(src_hots, 1)

                        def add(i, u):
                            wait_units(v, summed, i, u)
                            add_windows(v, ps[5], D, i, u, added, narrow)
                        unit, drain = staged(((last_edges, 3), (scan, 2), (add, 4), (nodes_by_edge, 0), (sources, 0)))
                        flow(v, unit, tail=drain)
                    split(v, program)
                    v.wait_ge(counted, UNITS)
                    v.tensor_copy(deg_out[:], ps[6][:, 0:NB])

        def l0_out(v, view, c0, step):
            xs, hs = x_nm[:, c0:c0 + GRP, :], h_nm[:, c0:c0 + GRP, :]
            step(v.tensor_tensor(hs, view, hs, ALU.max))
            step(v.tensor_tensor(xs, xs, hs, ALU.add))
        sum_to_nodes(D, None, D, l0_out)

        layernorm()
        with ExitStack() as own:
            rows = local(own, "scaled", [P, NB, D + 1])
            inv, root = local(own, "inv", [P, NB]), local(own, "root", [P, NB])
            step_done, clamped, rooted, ready, stored = (sem("scale_step"), sem("clamped"), sem("rooted"),
                                                         sem("scaled_ready"), sem("scaled_stored"))
            with nc.Block() as block:
                @block.vector
                def _(v):
                    step = Chain(v, step_done)
                    v.tensor_scalar(inv[:], deg_out[:], 1.0, None, ALU.max).then_inc(clamped, 1)
                    step(v.memset(rows[:], 1.0))
                    v.wait_ge(rooted, 1)
                    step(v.reciprocal(inv[:], root[:]))
                    v.tensor_tensor(rows[:, :, 0:D], h_nm[:], inv[:].unsqueeze(2).broadcast_to([P, NB, D]),
                                    ALU.mult).then_inc(ready, 1)
                    v.memset(acc[0:D + 1, :], 0.0)

                @block.scalar
                def _(a):
                    a.wait_ge(clamped, 1)
                    a.activation(root[:], inv[:], ACT.Sqrt).then_inc(rooted, 1)

                @block.sync
                def _(sp):
                    sp.wait_ge(ready, 1)
                    sp.dma_start(h1_table.rearrange("(c p) f -> p c f", p=P), rows[:]).then_inc(stored, 16)
                    sp.wait_ge(stored, 16)

        with ExitStack() as own:
            idx = local(own, "idx", [P, 2, 2 * TJ], I32)
            rows = local(own, "rows", [P, BU, TJ, D + 1])
            oh = local(own, "oh", [P, 2, TJ, P])
            ea = local(own, "ea", [D, 2, U])
            st = local(own, "st", [D, UNITS, 6])
            idx_in, ea_in, gathered = sems("idx_in"), sems("ea_in"), sems("gathered", BU)
            hots, summed, added, stats = sem("hots"), sem("summed"), sem("added"), sem("stats")
            with nc.Block() as block:
                @block.sync
                def _(sp):
                    def unit(i, u):
                        wait_units(sp, stats, i, u, 2)
                        sp.dma_start(ea[:, u % 2, :], A["eaT"][:, bass.ds((i * BU + u) * U, U)]).then_inc(ea_in[u % 2], 16)
                        load_indices(sp, idx, idx_in, gathered, i, u)
                    first_indices(sp, idx, idx_in)
                    flow(sp, unit)
                    last_indices(sp, idx_in)

                @block.gpsimd
                def _(pool):
                    gather_loop(pool, h1_table, lambda u, j: rows[:, u, j, :], idx, idx_in, gathered, summed)

                @block.tensor
                def _(pe):
                    def program(narrow):
                        def unit(i, u):
                            wait_units(pe, added, i, u, 2, adds(narrow))
                            wait_units(pe, hots, i, u)
                            wait_gathered(pe, gathered, i, u)
                            window_products(pe, ps[u % 2], D + 1, lambda j: [rows[:, u, j, :]], oh[:, u % 2],
                                            narrow).then_inc(summed, 1)
                        flow(pe, unit)
                    split(pe, program)

                @block.vector
                def _(v):
                    def program(narrow):
                        def hot(i, u):
                            wait_units(v, summed, i, u, 2)
                            one_hots(v, oh, i, u, narrow).then_inc(hots, 1)

                        def edge_stats(i, u, n=U):
                            wait_slot(v, ea_in, i, u)
                            v.bn_stats(st[:, bass.ds(i * BU + u, 1), :].rearrange("p a s -> p (a s)"),
                                       ea[:, u % 2, 0:n]).then_inc(stats, 1)

                        def add(i, u):
                            wait_units(v, summed, i, u)
                            add_windows(v, ps[u % 2], D + 1, i, u, added, narrow)
                        unit, drain = staged(((hot, 0), (edge_stats, 0), (add, 1)))

                        def last_body(i, u):
                            hot(i, u)
                            edge_stats(i, u, U if u < BU - 1 else LAST)
                            add(*before(i, u, 1))
                        flow(v, unit, last=last_body, tail=drain)
                    split(v, program)
                    v.wait_ge(stats, UNITS)
                    v.bn_aggr(ea_stats[:], st[:].rearrange("p a s -> p (a s)"))

        with ExitStack() as own:
            nodes = big[:, 0:NB * (D + 1)].rearrange("p (c f) -> p c f", f=D + 1)
            inv, root = local(own, "inv", [P, NB]), local(own, "root", [P, NB])

            def l1_out(v, view, c0, step):
                step(v.tensor_copy(nodes[:, c0:c0 + GRP, :], view))
            sum_to_nodes(D + 1, w_l1[:], D + 1, l1_out)
            step_done, clamped, rooted = sem("norm_step"), sem("clamped"), sem("rooted")
            with nc.Block() as block:
                @block.vector
                def _(v):
                    step = Chain(v, step_done)
                    out_l1 = nodes[:, :, 0:D]
                    v.tensor_scalar(inv[:], nodes[:, :, D], 1.0, None, ALU.max).then_inc(clamped, 1)
                    step(v.tensor_copy(acc[64:65, :], acc[D:D + 1, :]))
                    v.wait_ge(rooted, 1)
                    step(v.reciprocal(inv[:], root[:]))
                    step(v.tensor_tensor(out_l1, out_l1, inv[:].unsqueeze(2).broadcast_to([P, NB, D]), ALU.mult))
                    step(v.tensor_tensor(out_l1, out_l1, bias_l1[:].unsqueeze(1).broadcast_to([P, NB, D]), ALU.add))
                    step(v.scalar_tensor_tensor(out=x_nm[:], in0=out_l1, scalar=0.0, in1=x_nm[:],
                                                op0=ALU.max, op1=ALU.add))

                @block.scalar
                def _(a):
                    a.wait_ge(clamped, 1)
                    a.activation(root[:], inv[:], ACT.Sqrt).then_inc(rooted, 1)

        recycle()

        layernorm()
        store_table(h_table, h_nm[:])
        def lrelu(v, dst, src):
            return v.scalar_tensor_tensor(out=dst, in0=src, scalar=0.1, in1=src, op0=ALU.mult, op1=ALU.max)

        MEAN, VAR, TMP, SCALE, SHIFT = 19, 20, 21, 22, 23

        def fold(rows, width, w, gain, bias, col, row=None):
            step_done, var_ready, rooted, shifted, const = (sem("fold_step"), sem("var_ready"), sem("rooted"),
                                                            sem("shifted"), sem("const"))

            def c(n):
                return cols[0:rows, n:n + 1]
            with nc.Block() as block:
                @block.vector
                def _(v):
                    step = Chain(v, step_done)
                    v.tensor_scalar(c(TMP), c(VAR), EPS, None, ALU.add).then_inc(var_ready, 1)
                    v.wait_ge(rooted, 1)
                    step(v.reciprocal(c(TMP), c(SCALE)))
                    step(v.tensor_tensor(c(SCALE), c(TMP), c(gain), ALU.mult))
                    step(v.tensor_tensor(c(TMP), c(MEAN), c(SCALE), ALU.mult))
                    v.tensor_tensor(c(SHIFT), c(bias), c(TMP), ALU.subtract).then_inc(shifted, 1)
                    v.wait_ge(const, 1)
                    step(v.tensor_scalar(w, w, c(SCALE), None, ALU.mult))
                    if row is None:
                        step(v.tensor_tensor(cols[0:width, col:col + 1], ps[7][0:width, 0:1],
                                             cols[0:width, col:col + 1], ALU.add))
                    else:
                        step(v.tensor_tensor(row, ps[7][0:1, 0:width], col, ALU.add))

                @block.scalar
                def _(a):
                    a.wait_ge(var_ready, 1)
                    a.activation(c(SCALE), c(TMP), ACT.Sqrt).then_inc(rooted, 1)

                @block.tensor
                def _(pe):
                    pe.wait_ge(shifted, 1)
                    if row is None:
                        pe.matmul(ps[7][0:width, 0:1], w, c(SHIFT), start=True, stop=True).then_inc(const, 1)
                    else:
                        pe.matmul(ps[7][0:1, 0:width], c(SHIFT), w, start=True, stop=True).then_inc(const, 1)

        with ExitStack() as own:
            sq = big[:, 0:NB * D].rearrange("p (c f) -> p c f", f=D)
            squared, weighed, step_done = sem("squared"), sem("weighed"), sem("bn_step")
            with nc.Block() as block:
                @block.vector
                def _(v):
                    step = Chain(v, step_done)
                    v.tensor_tensor(sq, h_nm[:], h_nm[:], ALU.mult).then_inc(squared, 1)
                    step(v.tensor_copy(cols[D:2 * D, MEAN:MEAN + 2], ea_stats[:]))
                    v.wait_ge(weighed, 1)
                    for k in range(2):
                        step(v.tensor_scalar(cols[0:D, MEAN + k:MEAN + k + 1], ps[k][0:D, 0:1], 1.0 / E, None, ALU.mult))
                    m, s, t = (cols[0:D, n:n + 1] for n in (MEAN, VAR, TMP))
                    step(v.tensor_tensor(t, m, m, ALU.mult))
                    step(v.tensor_tensor(s, s, t, ALU.subtract))

                @block.tensor
                def _(pe):
                    pe.wait_ge(squared, 1)
                    for c in range(NB):
                        k = P if c < NB - 1 else TAIL
                        for b, src in enumerate((h_nm, sq)):
                            last = pe.matmul(ps[b][0:D, 0:1], src[0:k, c, :], deg_out[0:k, c:c + 1],
                                             start=(c == 0), stop=(c == NB - 1))
                    last.then_inc(weighed, 1)
        fold(64, 64, m1w[0][0:64, :], 3, 4, 9)

        with ExitStack() as own:
            idx = local(own, "idx", [P, 2, 2 * TJ], I32)
            rows = local(own, "rows", [P, BU, TJ, D])
            feat = local(own, "feat", [64, 2, U])
            zc = local(own, "zc", [64, 2, U])
            z1 = local(own, "z1", [64, BU, U])
            st = local(own, "st", [64, UNITS, 6])
            idx_in, ea_in, gathered, stored = sems("idx_in"), sems("ea_in"), sems("gathered", BU), sems("stored", BU)
            turned, copied, z_done, z_copied, z1_done, stats, pe_go = [sem(s) for s in (
                "turned", "copied", "z_done", "z_copied", "z1_done", "stats", "pe_go")]
            with nc.Block() as block:
                @block.sync
                def _(sp):
                    def store(i, u):
                        wait_units(sp, z1_done, i, u)
                        sp.dma_start(z1_dram[:, bass.ds((i * BU + u) * U, U)], z1[:, u, :]).then_inc(stored[u], 16)

                    def unit(i, u):
                        wait_units(sp, z_done, i, u, 2)
                        sp.dma_start(feat[D:2 * D, u % 2, :],
                                     A["eaT"][:, bass.ds((i * BU + u) * U, U)]).then_inc(ea_in[u % 2], 16)
                        if before(i, u, 2) is not None:
                            store(*before(i, u, 2))
                        load_indices(sp, idx, idx_in, gathered, i, u)

                    def drain(i, u):
                        if u < 2:
                            store(*before(i, u, 2))
                    first_indices(sp, idx, idx_in)
                    flow(sp, unit, tail=drain)
                    last_indices(sp, idx_in)
                    for u in range(BU):
                        sp.wait_ge(stored[u], 16 * BODIES)

                @block.gpsimd
                def _(pool):
                    gather_loop(pool, h_table, lambda u, j: rows[:, u, j, :], idx, idx_in, gathered, turned)

                @block.tensor
                def _(pe):
                    def product(i, u):
                        wait_units(pe, copied, i, u)
                        wait_units(pe, z_copied, i, u, 2)
                        wait_slot(pe, ea_in, i, u)
                        pe.sem_inc(pe_go, 1)
                        pe.matmul(ps[2 + u % 2][0:64, :], m1w[0][0:64, :], feat[:, u % 2, :],
                                  start=True, stop=True).then_inc(z_done, 1)

                    def turn(i, u):
                        wait_units(pe, copied, i, u, 2)
                        wait_gathered(pe, gathered, i, u)
                        for j in range(TJ):
                            last = pe.transpose(ps[u % 2][0:D, j * P:(j + 1) * P], rows[:, u, j, :], ident[:])
                        last.then_inc(turned, 1)
                    unit, drain = staged(((product, 1), (turn, 0)))
                    flow(pe, unit, tail=drain)

                @block.scalar
                def _(a):
                    def add_const(i, u):
                        wait_units(a, z_done, i, u)
                        wait_units(a, z1_done, i, u, 2)
                        a.activation(zc[:, u % 2, :], ps[2 + u % 2][0:64, :], ACT.Identity,
                                     bias=cols[0:64, 9:10]).then_inc(z_copied, 1)

                    def copy(i, u):
                        wait_units(a, z_done, i, u, 2)
                        wait_units(a, turned, i, u)
                        a.copy(feat[0:D, u % 2, :], ps[u % 2][0:D, :]).then_inc(copied, 1)
                    unit, drain = staged(((add_const, 1), (copy, 0)))
                    flow(a, unit, tail=drain)

                @block.vector
                def _(v):
                    def unit(i, u, n=U):
                        if not (isinstance(i, int) and i == 0):
                            v.wait_ge(stored[u], i * 16)
                            v.wait_ge(stats, (i - 1) * BU + u + 1)
                        wait_units(v, z_copied, i, u)
                        lrelu(v, z1[:, u, :], zc[:, u % 2, :]).then_inc(z1_done, 1)
                        wait_units(v, z1_done, i, u)
                        v.bn_stats(st[:, bass.ds(i * BU + u, 1), :].rearrange("p a s -> p (a s)"),
                                   z1[:, u, 0:n]).then_inc(stats, 1)
                    flow(v, unit, last=lambda i, u: unit(i, u, U if u < BU - 1 else LAST))
                    v.wait_ge(stats, UNITS)
                    v.bn_aggr(cols[0:64, MEAN:MEAN + 2], st[:].rearrange("p a s -> p (a s)"))
        fold(64, 64, m1w[1][0:64, :], 5, 6, c_rows[:, 0, :], m1w[1][64:65, :])
        clear_sum(64)

        sq_sum = big[:, 0:2 * TJ * 64]
        with ExitStack() as own:
            z1 = local(own, "z1", [P, 2, U])
            w2d = local(own, "w2d", [P, P])
            ones = local(own, "ones", [65, P])
            c2 = local(own, "c2", [P, 64])
            zc = local(own, "zc", [P, 2, TJ, 2, 64])
            z2 = local(own, "z2", [P, 2, TJ, 2, 64])
            z2_sq = local(own, "z2_sq", [P, 2 * TJ * 64])
            oh = local(own, "oh", [P, 2, 2 * TJ, P])
            z1_in = sems("z1_in")
            (hots, z_done, z_copied, z2_done, squared, sq_added, summed, added, set_up, c2_spread,
             sq_cleared) = [sem(s) for s in (
                 "hots", "z_done", "z_copied", "z2_done", "squared", "sq_added", "summed", "added", "set_up",
                 "c2_spread", "sq_cleared")]
            with nc.Block() as block:
                @block.sync
                def _(sp):
                    def pair(i, k):
                        wait_pairs(sp, z_done, i, k, 2)
                        for h in range(2):
                            sp.dma_start(z1[h * 64:h * 64 + 64, k, :],
                                         z1_dram[:, bass.ds((i * BU + 2 * k + h) * U, U)]).then_inc(z1_in[k], 16)
                    flow(sp, pair, bu=BU // 2)

                @block.tensor
                def _(pe):
                    pe.wait_ge(set_up, 1)
                    pe.matmul(ps[6][:, 0:64], ones[64:65, :], m1w[1][64:65, :], start=True, stop=True).then_inc(c2_spread, 1)

                    def program(narrow):
                        def sums(i, k):
                            wait_pairs(pe, z2_done, i, k)
                            wait_pairs(pe, hots, i, k)
                            wait_pairs(pe, added, i, k, 2, 2 * adds(narrow))
                            for h in range(2):
                                window_products(pe, ps[2 + 2 * k + h], 64, lambda j: [z2[:, k, j, h, :]],
                                                oh[:, k, h * TJ:(h + 1) * TJ], narrow).then_inc(summed, 1)

                        def second(i, k):
                            wait_pairs(pe, z_copied, i, k, 2)
                            pe.wait_ge(z1_in[k], (i + 1) * 32)
                            for j in range(TJ):
                                last = pe.matmul(ps[k][:, j * P:(j + 1) * P], z1[:, k, j * P:(j + 1) * P],
                                                 w2d[:], start=True, stop=True)
                            last.then_inc(z_done, 1)
                        pair, drain = staged(((second, 0), (sums, 1)), bu=BU // 2)
                        flow(pe, pair, tail=drain, bu=BU // 2)
                    split(pe, program)

                @block.gpsimd
                def _(pool):
                    pool.memset(sq_sum, 0.0).then_inc(sq_cleared, 1)
                    pool.wait_ge(sq_cleared, 1)

                    def square(i, k, last_pair=False):
                        wait_pairs(pool, z2_done, i, k)
                        wait_pairs(pool, sq_added, i, k, 1)
                        z = z2[:, k].rearrange("p j h f -> p (j h f)")
                        pool.tensor_tensor(z2_sq[:], z, z, ALU.mult).then_inc(squared, 1)
                        wait_pairs(pool, squared, i, k)
                        if not last_pair:
                            pool.tensor_tensor(sq_sum, sq_sum, z2_sq[:], ALU.add).then_inc(sq_added, 1)
                            return
                        view = [t.rearrange("p (j h f) -> p j h f", j=TJ, h=2) for t in (sq_sum, z2_sq[:])]
                        pool.tensor_tensor(view[0][:, :, 0, :], view[0][:, :, 0, :], view[1][:, :, 0, :], ALU.add)
                        pool.tensor_tensor(view[0][0:LAST, 0, 1, :], view[0][0:LAST, 0, 1, :],
                                           view[1][0:LAST, 0, 1, :], ALU.add).then_inc(sq_added, 1)
                    flow(pool, square, last=lambda i, k: square(i, k, last_pair=(k == 1)), bu=BU // 2)

                @block.vector
                def _(v):
                    step = Chain(v, sem("set_up_step"))
                    step(v.memset(w2d[:], 0.0))
                    step(v.tensor_copy(w2d[0:64, 0:64], m1w[1][0:64, :]))
                    step(v.tensor_copy(w2d[64:P, 64:P], m1w[1][0:64, :]))
                    v.memset(ones[:], 1.0).then_inc(set_up, 1)
                    v.wait_ge(c2_spread, 1)
                    step(v.tensor_copy(c2[:], ps[6][:, 0:64]))

                    def program(narrow):
                        def add_const(i, k):
                            wait_pairs(v, z_done, i, k)
                            wait_pairs(v, z2_done, i, k, 2)
                            v.tensor_tensor(zc[:, k].rearrange("p j h f -> p (j h) f"),
                                            ps[k][:, :].rearrange("p (a f) -> p a f", f=64),
                                            c2[:].unsqueeze(1).broadcast_to([P, 2 * TJ, 64]), ALU.add).then_inc(z_copied, 1)

                        def hot(i, k):
                            wait_pairs(v, summed, i, k, 2, 2)
                            t = (i * BU + 2 * k) * TJ
                            if narrow:
                                v.tensor_tensor(oh[:, k, :, 0:W], iota[:, 0:W].unsqueeze(1).broadcast_to([P, 2 * TJ, W]),
                                                dst_rel[1][:, bass.ds(t, 2 * TJ)].unsqueeze(2).broadcast_to([P, 2 * TJ, W]),
                                                ALU.is_equal).then_inc(hots, 1)
                                return
                            for j in range(2 * TJ):
                                last = v.tensor_scalar(oh[:, k, j, :], iota[:], dst_rel[0][:, bass.ds(t + j, 1)], None,
                                                       ALU.is_equal)
                            last.then_inc(hots, 1)

                        def positive(i, k):
                            wait_pairs(v, z_copied, i, k)
                            wait_pairs(v, summed, i, k, 2, 2)
                            wait_pairs(v, squared, i, k, 2)
                            lrelu(v, z2[:, k].rearrange("p j h f -> p (j h f)"),
                                  zc[:, k].rearrange("p j h f -> p (j h f)")).then_inc(z2_done, 1)

                        def add(i, k):
                            for h in range(2):
                                v.wait_ge(summed, i * BU + 2 * k + h + 1)
                                add_windows(v, ps[2 + 2 * k + h], 64, i, 2 * k + h, added, narrow)
                        pair, drain = staged(((add_const, 0), (hot, 0), (positive, 0), (add, 1)), bu=BU // 2)
                        flow(v, pair, tail=drain, bu=BU // 2)
                    split(v, program)

        with ExitStack() as own:
            by_feature = local(own, "by_feature", [P, 64])
            column = local(own, "column", [P, 1])
            step_done, folded, joined = sem("bn_step"), sem("squares_folded"), sem("squares_joined")
            with nc.Block() as block:
                @block.tensor
                def _(pe):
                    pe.wait_ge(folded, 1)
                    pe.matmul(ps[6][0:64, 0:1], by_feature[:], column[:], start=True, stop=True).then_inc(joined, 1)

                @block.vector
                def _(v):
                    step = Chain(v, step_done)
                    m, s, t = (cols[0:64, n:n + 1] for n in (MEAN, VAR, TMP))
                    step(v.memset(column[:], 1.0))
                    v.tensor_reduce(by_feature[:], sq_sum.rearrange("p (a f) -> p f a", f=64), AX_X, ALU.add).then_inc(folded, 1)
                    step(v.tensor_reduce(m, acc[0:64, 0:N], AX_X, ALU.add))
                    step(v.tensor_scalar(m, m, 1.0 / E, None, ALU.mult))
                    v.wait_ge(joined, 1)
                    step(v.tensor_copy(s, ps[6][0:64, 0:1]))
                    step(v.tensor_tensor(t, m, m, ALU.mult))
                    step(v.scalar_tensor_tensor(out=s, in0=s, scalar=1.0 / E, in1=t, op0=ALU.mult, op1=ALU.subtract))
        fold(64, 64, m1w[2][0:64, :], 7, 8, c_rows[:, 1, :], m1w[2][64:65, :])

        recycle()

        NG = -(-NB // 4)
        with ExitStack() as own:
            st = local(own, "st", [96, NCH, 6])
            zc = local(own, "zc", [96, 2, CH])
            turned, copied, prod, prod_copied, stats = [sem(s) for s in (
                "n_turned", "n_copied", "n_prod", "n_prod_copied", "node_stats")]

            def chunk_stats(v, g):
                return v.bn_stats(st[:, g, :], big[0:96, g * CH:(g + 1) * CH])
            with nc.Block() as block:
                @block.tensor
                def _(pe):
                    for g in range(NG):
                        if g >= 2:
                            pe.wait_ge(copied, g - 1)
                        for j in range(min(4, NB - 4 * g)):
                            last = pe.transpose(ps[g % 2][0:D, j * P:(j + 1) * P], h_nm[:, 4 * g + j, :], ident[:])
                        last.then_inc(turned, 1)
                        if g < NCH:
                            if g >= 2:
                                pe.wait_ge(prod_copied, g - 1)
                            pe.matmul(ps[2 + g % 2][0:64, 0:CH], m1w[2][:], acc[0:65, g * CH:(g + 1) * CH],
                                      start=True, stop=True).then_inc(prod, 1)

                @block.scalar
                def _(a):
                    for g in range(NG):
                        n = min(4, NB - 4 * g) * P
                        a.wait_ge(turned, g + 1)
                        a.copy(big[64:96, g * 4 * P:g * 4 * P + n], ps[g % 2][0:D, 0:n]).then_inc(copied, 1)

                @block.vector
                def _(v):
                    for g in range(NCH + 1):
                        if g < NCH:
                            v.wait_ge(prod, g + 1)
                            v.tensor_copy(big[0:64, g * CH:(g + 1) * CH],
                                          ps[2 + g % 2][0:64, 0:CH]).then_inc(prod_copied, 1)
                        if g >= 1:
                            v.wait_ge(prod_copied, g)
                            v.wait_ge(copied, (g * CH - 1) // (4 * P) + 1)
                            chunk_stats(v, g - 1).then_inc(stats, 1)
                    v.wait_ge(stats, NCH)
                    v.bn_aggr(cols[0:96, MEAN:MEAN + 2], st[:].rearrange("p a s -> p (a s)"))

            for k in range(3):
                width = 96 if k < 2 else D
                w = m2w[k][:, 0:width]
                fold(96, width, w, 10 + 2 * k, 11 + 2 * k, 16 + k)
                prod, used, shifted, stats = sem("node_prod"), sem("node_used"), sem("node_shifted"), sem("node_stats")
                with nc.Block() as block:
                    @block.tensor
                    def _(pe):
                        for g in range(NCH):
                            if g >= 4:
                                pe.wait_ge(used, g - 3)
                            pe.matmul(ps[g % 4][0:width, 0:CH], w, big[0:96, g * CH:(g + 1) * CH],
                                      start=True, stop=True).then_inc(prod, 1)

                    @block.scalar
                    def _(a):
                        for g in range(NCH):
                            a.wait_ge(prod, g + 1)
                            if k < 2 and g >= 2:
                                a.wait_ge(shifted, g - 1)
                            dst = zc[:, g % 2, :] if k < 2 else acc[0:D, g * CH:(g + 1) * CH]
                            a.activation(dst, ps[g % 4][0:width, 0:CH], ACT.Identity,
                                         bias=cols[0:width, 16 + k:17 + k]).then_inc(used, 1)

                    @block.vector
                    def _(v):
                        if k == 2:
                            return
                        for g in range(NCH + 1):
                            if g < NCH:
                                v.wait_ge(used, g + 1)
                                lrelu(v, big[0:96, g * CH:(g + 1) * CH], zc[:, g % 2, :]).then_inc(shifted, 1)
                            if g >= 1:
                                v.wait_ge(shifted, g)
                                chunk_stats(v, g - 1).then_inc(stats, 1)
                        v.wait_ge(stats, NCH)
                        v.bn_aggr(cols[0:96, MEAN:MEAN + 2], st[:].rearrange("p a s -> p (a s)"))

        def add_to_x(v, view, c0, step):
            xs = x_nm[:, c0:c0 + GRP, :]
            step(v.tensor_tensor(xs, xs, view, ALU.add))
        sum_to_nodes(D, None, D, add_to_x)

        recycle()

        layernorm()
        store_table(h_table, h_nm[:])
        r5 = big[:, 0:NT * 5].rearrange("p (t k) -> p t k", k=5)
        with ExitStack() as own:
            rel = local(own, "rel", [P, NT, 3])
            n2, root = acc[:, 0:NT], acc[:, NT:2 * NT]
            sq = acc[:, 2 * NT:5 * NT].rearrange("p (t k) -> p t k", k=3)
            loaded, step_done, summed, rooted = sem("rel_loaded"), sem("rel_step"), sem("rel_summed"), sem("rel_rooted")
            with nc.Block() as block:
                @block.sync
                def _(sp):
                    sp.dma_start(rel[:], A["rel_t"]).then_inc(loaded, 16)
                    sp.wait_ge(loaded, 16)

                @block.vector
                def _(v):
                    step = Chain(v, step_done)
                    v.wait_ge(loaded, 16)
                    step(v.tensor_tensor(sq, rel[:], rel[:], ALU.mult))
                    v.tensor_reduce(n2, sq, AX_X, ALU.add).then_inc(summed, 1)
                    v.wait_ge(rooted, 1)
                    step(v.reciprocal(n2, root))
                    for k in range(5):
                        step(v.tensor_tensor(r5[:, :, k], rel[:, :, (k + 1) % 3], n2, ALU.mult))
                    step(v.memset(acc[:], 0.0))

                @block.scalar
                def _(a):
                    a.wait_ge(summed, 1)
                    a.activation(root, n2, ACT.Sqrt).then_inc(rooted, 1)

        with ExitStack() as own:
            idx = local(own, "idx", [P, 2, 2 * TJ], I32)
            rows = local(own, "rows", [P, BU, TJ, D])
            dist = local(own, "dist", [64, 2, U])
            hid = local(own, "hid", [65, 2, U])
            oh = big[:, 5 * NT:5 * NT + 2 * TJ * P].rearrange("p (s j n) -> p s j n", s=2, j=TJ)
            r = local(own, "r", [P, BU, TJ, 5])
            f_d = local(own, "f_d", [P, 2, TJ, 16])
            f_x = local(own, "f_x", [P, 2, TJ, 16, 3])
            f_5 = local(own, "f_5", [P, 2, TJ, 8, 5])
            away = local(own, "away", [P, TJ, P])
            one = local(own, "one", [P, 1])
            t1 = local(own, "t1", [P, TJ, 8, 3])
            t2 = local(own, "t2", [P, TJ, 8, 3])
            t3 = local(own, "t3", [P, 2, TJ, 8, 3])
            ab_prod = local(own, "ab_prod", [P, TJ, 16, 16])
            c_prod = local(own, "c_prod", [P, TJ, 16, 24])
            c_half = local(own, "c_half", [P, TJ, 8, 24])
            c_quarter = local(own, "c_quarter", [P, TJ, 4, 24])
            msg = local(own, "msg", [P, 2, TJ, MSG + 8])
            idx_in, dist_in, gathered = sems("idx_in"), sems("dist_in"), sems("gathered", BU)
            (spread, hid_done, r_done, x_step, x_done, dot_step, dot_done, hots, prods, halved, quartered, ab_summed,
             c_summed, away_done, msg_done, summed, added, set_up, may_gather) = [sem(s) for s in (
                 "spread", "hid_done", "r_done", "x_step", "x_done", "dot_step", "dot_done", "hots", "prods", "halved",
                 "quartered", "ab_summed", "c_summed", "away_done", "msg_done", "summed", "added", "set_up", "may_gather")]
            with nc.Block() as block:
                @block.sync
                def _(sp):
                    def unit(i, u):
                        wait_units(sp, hid_done, i, u, 2)
                        sp.dma_start(dist[:, u % 2, :],
                                     A["dist"][bass.ds((i * BU + u) * U, U)].partition_broadcast(64)).then_inc(dist_in[u % 2], 16)
                        load_indices(sp, idx, idx_in, gathered, i, u)
                    first_indices(sp, idx, idx_in)
                    flow(sp, unit)
                    last_indices(sp, idx_in)

                def by_r(lo, u):
                    return r[:, u, :, lo:lo + 3].unsqueeze(2).broadcast_to([P, TJ, 8, 3])

                @block.gpsimd
                def _(pool):
                    def gather(i, u):
                        if u % 2 == 0:
                            pool.wait_ge(idx_in[u // 2], 16 * (i + 1))
                        wait_units(pool, spread, i, u, BU)
                        pool.sem_inc(may_gather, 1)
                        for j in range(TJ):
                            pool.indirect_dma_start(
                                out=rows[:, u, j, :], out_offset=None, in_=h_table,
                                in_offset=bass.IndirectOffsetOnAxis(
                                    ap=idx[:, u // 2, (u % 2) * TJ + j:(u % 2) * TJ + j + 1], axis=0)).then_inc(gathered[u], 16)

                    def cross(i, u):
                        wait_units(pool, spread, i, u)
                        wait_units(pool, prods, i, u, 2, TJ)
                        wait_units(pool, x_done, i, u, 1)
                        pool.tensor_tensor(t1[:], f_5[:, u % 2, :, :, 2:5], by_r(1, u), ALU.mult).then_inc(x_step, 1)
                        pool.tensor_tensor(t2[:], f_5[:, u % 2, :, :, 1:4], by_r(2, u), ALU.mult).then_inc(x_step, 1)
                        wait_units(pool, x_step, i, u, 0, 2)
                        pool.tensor_tensor(f_x[:, u % 2, :, 8:16, :], t1[:], t2[:], ALU.subtract).then_inc(x_done, 1)

                    def dot_parts(i, u):
                        wait_units(pool, spread, i, u)
                        wait_units(pool, dot_done, i, u, 2)
                        pool.tensor_tensor(t3[:, u % 2], f_5[:, u % 2, :, :, 0:3], by_r(0, u), ALU.mult).then_inc(dot_step, 1)

                    def eighth(i, u):
                        wait_units(pool, quartered, i, u)
                        wait_units(pool, summed, i, u, 2)
                        pool.tensor_tensor(msg[:, u % 2, :, 0:48].rearrange("p j (v c) -> p j v c", v=2),
                                           c_quarter[:, :, 0:2, :], c_quarter[:, :, 2:4, :], ALU.add).then_inc(c_summed, 1)
                    unit, drain = staged(((gather, 0), (dot_parts, 2), (cross, 2), (eighth, 4)))
                    flow(pool, unit, tail=drain)

                @block.scalar
                def _(a):
                    def hidden(i, u):
                        wait_slot(a, dist_in, i, u)
                        wait_units(a, r_done, i, u, 2, TJ)
                        a.activation(hid[0:64, u % 2, :], dist[:, u % 2, :], ACT.Relu, bias=cols[0:64, 2:3],
                                     scale=cols[0:64, 1:2]).then_inc(hid_done, 1)

                    def spreads(i, u):
                        wait_gathered(a, gathered, i, u)
                        wait_units(a, prods, i, u, 2, TJ)
                        wait_units(a, msg_done, i, u, BU)
                        wait_units(a, x_done, i, u, 2)
                        f1 = rows[:, u, :, 8:32].rearrange("p j (v o) -> p j v o", o=3)
                        a.copy(f_d[:, u % 2, :, 0:8], rows[:, u, :, 0:8])
                        a.copy(f_x[:, u % 2, :, 0:8, :], f1)
                        a.copy(f_5[:, u % 2, :, :, 0:3], f1)
                        a.copy(f_5[:, u % 2, :, :, 3:5], f1[:, :, :, 0:2])
                        a.copy(r[:, u], r5[:, bass.ds((i * BU + u) * TJ, TJ), :]).then_inc(spread, 1)

                    def program(narrow):
                        width = W if narrow else P

                        def hot(i, u):
                            wait_units(a, hots, i, u, 1)
                            for j in range(TJ):
                                last = a.activation(away[:, j, 0:width], iota[:, 0:width], ACT.Abs,
                                                    bias=dst_rel[narrow][:, bass.ds((i * BU + u) * TJ + j, 1)], scale=-1.0)
                            last.then_inc(away_done, 1)
                            wait_units(a, away_done, i, u)
                            wait_units(a, summed, i, u, 2)
                            a.activation(oh[:, u % 2, :, 0:width], away[:, :, 0:width], ACT.Relu, bias=one[:],
                                         scale=-1.0).then_inc(hots, 1)
                        unit, drain = staged(((spreads, 1), (hidden, 0), (hot, 2)))
                        flow(a, unit, tail=drain)
                    a.wait_ge(set_up, 1)
                    split(a, program)

                @block.tensor
                def _(pe):
                    pe.wait_ge(set_up, 2)

                    def program(narrow):
                        def weights(i, u):
                            wait_units(pe, hid_done, i, u)
                            for j in range(TJ):
                                if not (isinstance(i, int) and i == 0 and u == 0):
                                    pe.wait_ge(prods, (i * BU + u) * TJ + j - TJ + 1)
                                pe.matmul(ps[j][:, 0:384], hid[:, u % 2, j * P:(j + 1) * P], w2m[:],
                                          start=True, stop=True).then_inc(r_done, 1)

                        def window_sums(i, u):
                            wait_units(pe, hots, i, u)
                            wait_units(pe, msg_done, i, u)
                            wait_units(pe, c_summed, i, u)
                            wait_units(pe, added, i, u, 2, adds(narrow))
                            window_products(pe, ps[4 + u % 2], MSG, lambda j: [msg[:, u % 2, j, 0:MSG]], oh[:, u % 2],
                                            narrow).then_inc(summed, 1)
                        unit, drain = staged(((weights, 0), (window_sums, 1)))
                        flow(pe, unit, tail=drain)
                    split(pe, program)

                @block.vector
                def _(v):
                    v.memset(one[:], 1.0).then_inc(set_up, 1)
                    v.wait_ge(set_up, 1)
                    v.memset(hid[64:65, :, :], 1.0).then_inc(set_up, 1)

                    def program(narrow):
                        def dot(i, u):
                            wait_units(v, dot_step, i, u)
                            v.tensor_reduce(f_d[:, u % 2, :, 8:16], t3[:, u % 2], AX_X, ALU.add).then_inc(dot_done, 1)

                        def products(i, u):
                            wait_units(v, x_done, i, u)
                            wait_units(v, dot_done, i, u)
                            wait_units(v, halved, i, u, 1)
                            wait_units(v, ab_summed, i, u, 1)
                            for j in range(TJ):
                                if j % 2 == 0:
                                    v.wait_ge(r_done, (i * BU + u) * TJ + j + 2)
                                    v.tensor_tensor(ab_prod[:, j:j + 2],
                                                    banks[:, j:j + 2, 0:256].rearrange("p j (v a) -> p j v a", v=16),
                                                    f_d[:, u % 2, j:j + 2, :].unsqueeze(3).broadcast_to([P, 2, 16, 16]),
                                                    ALU.mult)
                                v.tensor_tensor(c_prod[:, j].rearrange("p v (u o) -> p v u o", o=3),
                                                ps[j][:, 256:384].rearrange("p (v u) -> p v u", u=8).unsqueeze(3).broadcast_to([P, 16, 8, 3]),
                                                f_x[:, u % 2, j].unsqueeze(2).broadcast_to([P, 16, 8, 3]),
                                                ALU.mult).then_inc(prods, 1)

                        def halve(i, u):
                            wait_units(v, prods, i, u, 0, TJ)
                            wait_units(v, quartered, i, u, 1)
                            v.tensor_tensor(c_half[:], c_prod[:, :, 0:8, :], c_prod[:, :, 8:16, :],
                                            ALU.add).then_inc(halved, 1)

                        def sum_ab(i, u):
                            wait_units(v, summed, i, u, 2)
                            v.tensor_reduce(msg[:, u % 2, :, MSG - 8:MSG + 8], ab_prod[:].rearrange("p j v a -> p j a v"),
                                            AX_X, ALU.add).then_inc(ab_summed, 1)

                        def quarter(i, u):
                            wait_units(v, halved, i, u)
                            wait_units(v, c_summed, i, u, 1)
                            v.tensor_tensor(c_quarter[:], c_half[:, :, 0:4, :], c_half[:, :, 4:8, :],
                                            ALU.add).then_inc(quartered, 1)

                        def direct(i, u):
                            wait_units(v, ab_summed, i, u)
                            v.tensor_tensor(msg[:, u % 2, :, 48:72].rearrange("p j (u o) -> p j u o", o=3),
                                            msg[:, u % 2, :, MSG:MSG + 8].unsqueeze(3).broadcast_to([P, TJ, 8, 3]),
                                            by_r(0, u), ALU.mult).then_inc(msg_done, 1)

                        def add(i, u):
                            wait_units(v, summed, i, u)
                            add_windows(v, ps[4 + u % 2], MSG, i, u, added, narrow)
                        unit, drain = staged(((halve, 1), (sum_ab, 1), (quarter, 1), (dot, 0), (direct, 1),
                                              (products, 0), (add, 2)))
                        flow(v, unit, tail=drain)
                    split(v, program)

        sum_to_nodes(MSG, fold_msg[:], D, add_to_x)
        finish(nc, sem, x_nm, out)


def finish(nc, sem, x_nm, out):
    done = sem("out_stored")
    with nc.Block() as block:
        @block.sync
        def _(sp):
            sp.dma_start(out[0:(NB - 2) * P, :].rearrange("(c p) f -> p c f", p=P),
                         x_nm[:, 0:NB - 2, :]).then_inc(done, 16)
            sp.dma_start(out[(NB - 2) * P:(NB - 1) * P, :], x_nm[:, NB - 2, :]).then_inc(done, 16)
            sp.dma_start(out[(NB - 1) * P:N, :], x_nm[0:TAIL, NB - 1, :]).then_inc(done, 16)
            sp.wait_ge(done, 48)


_WEIGHTS = ["L0_gnn_W1", "L0_gnn_b1", "L0_gnn_W2", "L0_gnn_b2", "L1_gnn_weight", "L1_gnn_bias"] + \
    [f"L2_gnn_m{m}_{k}{n}" for m in (1, 2) for n in (1, 2, 3) for k in "gbwc"] + \
    ["L3_gnn_w1", "L3_gnn_b1", "L3_gnn_w2", "L3_gnn_b2"]


def kernel(**inputs):
    import concourse.bacc as _bacc
    from concourse import mybir as _mybir
    from concourse.bass_utils import run_bass_kernel_spmd as _run

    a = {k: np.asarray(v) for k, v in inputs.items()}

    def padded(v, fill):
        return np.concatenate([v, np.full((EP - E,) + v.shape[1:], fill, v.dtype)])

    src, dst = padded(a["src"], PAD_SRC), padded(a["dst"], N)
    arrays = {
        "x": a["x"],
        "src_t": np.pad(src.reshape(NT, P).T, ((0, 0), (0, BU * TJ))),
        "dst_t": dst.reshape(NT, P).T,
        "next_t": np.concatenate([dst[1:], dst[-1:]]).reshape(NT, P).T,
        "first": dst.reshape(NT, P)[:, 0],
        "dst_row": np.concatenate([np.full((1,), -1, dst.dtype), dst]),
        "eaT": padded(a["edge_attr_32"], 0).T,
        "rel_t": padded(a["edge_attr_3"], 1).reshape(NT, P, 3).transpose(1, 0, 2),
        "dist": padded(a["edge_weight"], 0),
    }
    for k in _WEIGHTS:
        arrays[k] = a[k]
    arrays = {k: np.ascontiguousarray(v) for k, v in arrays.items()}
    nc = _bacc.Bacc("TRN2", target_bir_lowering=False, num_devices=1)
    A = {k: nc.dram_tensor("in_" + k, list(v.shape), _mybir.dt.from_np(v.dtype), kind="ExternalInput").ap()
         for k, v in arrays.items()}
    out = nc.dram_tensor("out", [N, D], F32, kind="ExternalOutput").ap()
    build(nc, A, out)
    r = _run(nc, [{"in_" + k: v for k, v in arrays.items()}], core_ids=[0])
    return r.results[0]["out"]
```
